# Optimizing a Trainium2 kernel written in Bass

```python
import numpy as np
import jax
import jax.numpy as jnp

def _softmax(x, axis=-1):
    return jax.nn.softmax(x, axis=axis)

def _gelu(x):
    return jax.nn.gelu(x, approximate=True)

def _silu(x):
    return jax.nn.silu(x)

def _sigmoid(x):
    return jax.nn.sigmoid(x)

def _layernorm(x, axis=-1, eps=1e-05):
    m = jnp.mean(x, axis=axis, keepdims=True)
    v = jnp.var(x, axis=axis, keepdims=True)
    return (x - m) / jnp.sqrt(v + eps)

def _scatter_add(tgt, idx, src, axis=0):
    return tgt.at[idx].add(src)

def _segment_sum(src, seg, n):
    return jax.ops.segment_sum(src, seg, n)
kernel_name = 'mk_recurrent_d2_jaxref_r8_946b6a'

def setup_inputs(seed: int=0):
    np.random.seed(seed)
    _w = jnp.asarray

    def _L0_attn_setup():
        import jax, jax.numpy as jnp
        import numpy as np
        K = 128
        H = 16
        key = jax.random.key(seed)
        ks = jax.random.split(key, 6)
        s = 1.0 / np.sqrt(K)
        return {'x': jax.random.normal(ks[0], (2, 256, K), dtype=jnp.float32), 'Wq': jax.random.uniform(ks[1], (K, K), jnp.float32, -s, s), 'Wk': jax.random.uniform(ks[2], (K, K), jnp.float32, -s, s), 'Wv': jax.random.uniform(ks[3], (K, K), jnp.float32, -s, s), 'Wu': jax.random.uniform(ks[4], (K, K), jnp.float32, -s, s), 'bu': jax.random.uniform(ks[5], (K,), jnp.float32, -s, s)}
    _L0_attn_in = _L0_attn_setup()

    def _L0_ffn_setup():
        import jax, jax.numpy as jnp
        import numpy as np

        def _moe_layer(x, rw, rb, ew, eb):
            logits = jnp.einsum('bsh,eh->bse', x, rw) + rb
            probs = jax.nn.softmax(logits, axis=-1)
            _, topk_idx = jax.lax.top_k(probs, 2)
            out = jnp.zeros_like(x)
            num_experts = rw.shape[0]
            for e in range(num_experts):
                mask = (topk_idx == e).any(axis=-1)
                expert_out = jnp.einsum('bsh,dh->bsd', x, ew[e]) + eb[e]
                out = out + jnp.where(mask[..., None], expert_out, 0.0)
            return out
        key = jax.random.key(seed)
        ks = jax.random.split(key, 4)
        L, E, H = (2, 8, 128)
        B, S = (4, 512)
        return {'hidden_states': jax.random.normal(ks[0], (B, S, H), dtype=jnp.float32), 'router_w': jax.random.normal(ks[1], (L, E, H), dtype=jnp.float32) * (1.0 / np.sqrt(H)), 'router_b': jnp.zeros((L, E), dtype=jnp.float32), 'expert_w': jax.random.normal(ks[2], (L, E, H, H), dtype=jnp.float32) * (1.0 / np.sqrt(H)), 'expert_b': jnp.zeros((L, E, H), dtype=jnp.float32)}
    _L0_ffn_in = _L0_ffn_setup()

    def _L1_attn_setup():
        import jax, jax.numpy as jnp
        import numpy as np
        B, S, D, H = (8, 256, 128, 16)
        HD = D // H
        HID = 4 * HD
        MAX_LR = 0.01
        NUM_LAYERS = 2

        def _split_heads(x):
            b, s, _ = x.shape
            return x.reshape(b, s, H, HD).transpose(0, 2, 1, 3).reshape(b * H, s, HD)

        def _merge_heads(x, b):
            return x.reshape(b, H, -1, HD).transpose(0, 2, 1, 3).reshape(b, -1, D)

        def _rmsnorm_w(x, w, eps=1e-06):
            return x * w * jax.lax.rsqrt(jnp.mean(x * x, axis=-1, keepdims=True) + eps)

        def _pf_rmsnorm(h):
            rms = jnp.sqrt(jnp.mean(h * h, axis=-1, keepdims=True) + 1e-08)
            return (h / rms, rms)

        def _pf_rmsnorm_bwd(d_out, h_norm, rms):
            d = d_out.shape[-1]
            dy = jnp.sum(d_out * h_norm, axis=-1, keepdims=True)
            return (d_out - h_norm * dy / d) / rms

        def _gelu_grad(x):
            cdf = 0.5 * (1.0 + jax.lax.erf(x * 0.7071067811865476))
            pdf = jnp.exp(-0.5 * x * x) * 0.3989422804014327
            return cdf + x * pdf

        def _memory_forward(x, Ws):
            h = x
            n = len(Ws)
            for i, W in enumerate(Ws):
                h = jnp.matmul(h, W)
                if i < n - 1:
                    h = jax.nn.gelu(h, approximate=False)
            h = jnp.nan_to_num(h, nan=0.0, posinf=0.0, neginf=0.0)
            h_norm, _ = _pf_rmsnorm(h)
            return h_norm + x

        def _memory_grad(keys, values, theta, Ws):
            Ws = [jax.lax.stop_gradient(W) for W in Ws]
            acts = [keys]
            pres = []
            h = keys
            n = len(Ws)
            for i, W in enumerate(Ws):
                pre = jnp.matmul(h, W)
                pres.append(pre)
                h = jax.nn.gelu(pre, approximate=False) if i < n - 1 else pre
                acts.append(h)
            h_norm, rms = _pf_rmsnorm(acts[-1])
            pred = h_norm + keys
            d_pred = 2.0 * theta[..., None] * (pred - values)
            d_h = _pf_rmsnorm_bwd(d_pred, h_norm, rms)
            grads = [None] * n
            for i in range(n - 1, -1, -1):
                grads[i] = jnp.einsum('bsi,bso->bio', acts[i], d_h)
                if i > 0:
                    d_h = jnp.matmul(d_h, Ws[i].transpose(0, 2, 1)) * _gelu_grad(pres[i - 1])
            return grads

        def _clip_grads(grads, max_norm=10.0):
            sq = sum((jnp.sum(g.reshape(g.shape[0], -1) ** 2, axis=1) for g in grads))
            coef = jnp.minimum(max_norm / (jnp.sqrt(sq) + 1e-06), 1.0)
            coef = jax.lax.stop_gradient(coef)[:, None, None]
            return [g * coef for g in grads]
        key = jax.random.key(seed)
        ks = jax.random.split(key, 12)
        xav0 = float(np.sqrt(2.0 / (HD + HID)))
        xav1 = float(np.sqrt(2.0 / (HID + HD)))
        return {'x': jax.random.normal(ks[0], (B, S, D), jnp.float32), 'W_K': jax.random.normal(ks[1], (D, D), jnp.float32) / np.float32(np.sqrt(D)), 'W_V': jax.random.normal(ks[2], (D, D), jnp.float32) / np.float32(np.sqrt(D)), 'W_Q': jax.random.normal(ks[3], (D, D), jnp.float32) / np.float32(np.sqrt(D)), 'mem_W0': jax.random.normal(ks[4], (HD, HID), jnp.float32) * xav0, 'mem_W1': jax.random.normal(ks[5], (HID, HD), jnp.float32) * xav1, 'k_norm_w': jnp.ones((HD,), jnp.float32), 'q_norm_w': jnp.ones((HD,), jnp.float32), 'store_norm_w': jnp.ones((D,), jnp.float32), 'retrieve_norm_w': jnp.ones((D,), jnp.float32), 'alpha_w': jax.random.normal(ks[6], (D, H), jnp.float32) * 0.01, 'alpha_b': jnp.full((H,), -5.0, jnp.float32), 'theta_w': jax.random.normal(ks[7], (D, H), jnp.float32) * 0.01, 'theta_b': jnp.full((H,), -3.0, jnp.float32), 'eta_w': jax.random.normal(ks[8], (D, H), jnp.float32) * 0.01, 'eta_b': jnp.zeros((H,), jnp.float32)}
    _L1_attn_in = _L1_attn_setup()

    def _L1_ffn_setup():
        import jax, jax.numpy as jnp
        import numpy as np
        H_DIM, E_DIM = (128, 64)
        N_SHARED, N_ROUTED, TOP_K = (2, 16, 4)
        B, S = (4, 256)
        key = jax.random.key(seed)
        ks = jax.random.split(key, 6)
        sc = 1.0 / np.sqrt(H_DIM)
        ec = 1.0 / np.sqrt(E_DIM)
        return {'x': jax.random.normal(ks[0], (B, S, H_DIM), dtype=jnp.float32), 'shared_up': jax.random.uniform(ks[1], (N_SHARED, E_DIM, H_DIM), jnp.float32, -sc, sc), 'shared_down': jax.random.uniform(ks[2], (N_SHARED, H_DIM, E_DIM), jnp.float32, -ec, ec), 'routed_up': jax.random.uniform(ks[3], (N_ROUTED, E_DIM, H_DIM), jnp.float32, -sc, sc), 'routed_down': jax.random.uniform(ks[4], (N_ROUTED, H_DIM, E_DIM), jnp.float32, -ec, ec), 'router_w': jax.random.uniform(ks[5], (N_ROUTED, H_DIM), jnp.float32, -sc, sc)}
    _L1_ffn_in = _L1_ffn_setup()
    _d = {'L0_attn_x': _L0_attn_in['x'], 'L0_attn_Wq': _L0_attn_in['Wq'], 'L0_attn_Wk': _L0_attn_in['Wk'], 'L0_attn_Wv': _L0_attn_in['Wv'], 'L0_attn_Wu': _L0_attn_in['Wu'], 'L0_attn_bu': _L0_attn_in['bu'], 'L0_ffn_router_w': _L0_ffn_in['router_w'], 'L0_ffn_router_b': _L0_ffn_in['router_b'], 'L0_ffn_expert_w': _L0_ffn_in['expert_w'], 'L0_ffn_expert_b': _L0_ffn_in['expert_b'], 'L1_attn_W_K': _L1_attn_in['W_K'], 'L1_attn_W_V': _L1_attn_in['W_V'], 'L1_attn_W_Q': _L1_attn_in['W_Q'], 'L1_attn_mem_W0': _L1_attn_in['mem_W0'], 'L1_attn_mem_W1': _L1_attn_in['mem_W1'], 'L1_attn_k_norm_w': _L1_attn_in['k_norm_w'], 'L1_attn_q_norm_w': _L1_attn_in['q_norm_w'], 'L1_attn_store_norm_w': _L1_attn_in['store_norm_w'], 'L1_attn_retrieve_norm_w': _L1_attn_in['retrieve_norm_w'], 'L1_attn_alpha_w': _L1_attn_in['alpha_w'], 'L1_attn_alpha_b': _L1_attn_in['alpha_b'], 'L1_attn_theta_w': _L1_attn_in['theta_w'], 'L1_attn_theta_b': _L1_attn_in['theta_b'], 'L1_attn_eta_w': _L1_attn_in['eta_w'], 'L1_attn_eta_b': _L1_attn_in['eta_b'], 'L1_ffn_shared_up': _L1_ffn_in['shared_up'], 'L1_ffn_shared_down': _L1_ffn_in['shared_down'], 'L1_ffn_routed_up': _L1_ffn_in['routed_up'], 'L1_ffn_routed_down': _L1_ffn_in['routed_down'], 'L1_ffn_router_w': _L1_ffn_in['router_w']}
    _x0 = _d['L0_attn_x']
    _d['L0_attn_x'] = jax.random.normal(jax.random.fold_in(jax.random.key(seed), 1), (16, 256, 128), dtype=_x0.dtype)
    del _x0
    return _d

def reference(L0_attn_x, L0_attn_Wq, L0_attn_Wk, L0_attn_Wv, L0_attn_Wu, L0_attn_bu, L0_ffn_router_w, L0_ffn_router_b, L0_ffn_expert_w, L0_ffn_expert_b, L1_attn_W_K, L1_attn_W_V, L1_attn_W_Q, L1_attn_mem_W0, L1_attn_mem_W1, L1_attn_k_norm_w, L1_attn_q_norm_w, L1_attn_store_norm_w, L1_attn_retrieve_norm_w, L1_attn_alpha_w, L1_attn_alpha_b, L1_attn_theta_w, L1_attn_theta_b, L1_attn_eta_w, L1_attn_eta_b, L1_ffn_shared_up, L1_ffn_shared_down, L1_ffn_routed_up, L1_ffn_routed_down, L1_ffn_router_w):

    def _L0_attn_ref(x, Wq, Wk, Wv, Wu, bu):
        import jax, jax.numpy as jnp
        import numpy as np
        K = 128
        H = 16
        b, t, k = x.shape
        hd = k // H
        scale = jnp.asarray(k, x.dtype) ** 0.25
        q = (jnp.einsum('btk,ok->bto', x, Wq) / scale).reshape(b, t, H, hd)
        kk = (jnp.einsum('btk,ok->bto', x, Wk) / scale).reshape(b, t, H, hd)
        v = jnp.einsum('btk,ok->bto', x, Wv).reshape(b, t, H, hd)
        dot = jnp.einsum('bthd,bshd->bhts', q, kk)
        att = jax.nn.softmax(dot, axis=-1)
        out = jnp.einsum('bhts,bshd->bthd', att, v).reshape(b, t, k)
        return jnp.einsum('btk,ok->bto', out, Wu) + bu

    def _L0_ffn_ref(hidden_states, router_w, router_b, expert_w, expert_b):
        import jax, jax.numpy as jnp
        import numpy as np

        def _moe_layer(x, rw, rb, ew, eb):
            logits = jnp.einsum('bsh,eh->bse', x, rw) + rb
            probs = jax.nn.softmax(logits, axis=-1)
            _, topk_idx = jax.lax.top_k(probs, 2)
            out = jnp.zeros_like(x)
            num_experts = rw.shape[0]
            for e in range(num_experts):
                mask = (topk_idx == e).any(axis=-1)
                expert_out = jnp.einsum('bsh,dh->bsd', x, ew[e]) + eb[e]
                out = out + jnp.where(mask[..., None], expert_out, 0.0)
            return out
        x = hidden_states
        num_layers = router_w.shape[0]
        for l in range(num_layers):
            x = _moe_layer(x, router_w[l], router_b[l], expert_w[l], expert_b[l])
        return x

    def _L1_attn_ref(x, W_K, W_V, W_Q, mem_W0, mem_W1, k_norm_w, q_norm_w, store_norm_w, retrieve_norm_w, alpha_w, alpha_b, theta_w, theta_b, eta_w, eta_b):
        import jax, jax.numpy as jnp
        import numpy as np
        B, S, D, H = (8, 256, 128, 16)
        HD = D // H
        HID = 4 * HD
        MAX_LR = 0.01
        NUM_LAYERS = 2

        def _split_heads(x):
            b, s, _ = x.shape
            return x.reshape(b, s, H, HD).transpose(0, 2, 1, 3).reshape(b * H, s, HD)

        def _merge_heads(x, b):
            return x.reshape(b, H, -1, HD).transpose(0, 2, 1, 3).reshape(b, -1, D)

        def _rmsnorm_w(x, w, eps=1e-06):
            return x * w * jax.lax.rsqrt(jnp.mean(x * x, axis=-1, keepdims=True) + eps)

        def _pf_rmsnorm(h):
            rms = jnp.sqrt(jnp.mean(h * h, axis=-1, keepdims=True) + 1e-08)
            return (h / rms, rms)

        def _pf_rmsnorm_bwd(d_out, h_norm, rms):
            d = d_out.shape[-1]
            dy = jnp.sum(d_out * h_norm, axis=-1, keepdims=True)
            return (d_out - h_norm * dy / d) / rms

        def _gelu_grad(x):
            cdf = 0.5 * (1.0 + jax.lax.erf(x * 0.7071067811865476))
            pdf = jnp.exp(-0.5 * x * x) * 0.3989422804014327
            return cdf + x * pdf

        def _memory_forward(x, Ws):
            h = x
            n = len(Ws)
            for i, W in enumerate(Ws):
                h = jnp.matmul(h, W)
                if i < n - 1:
                    h = jax.nn.gelu(h, approximate=False)
            h = jnp.nan_to_num(h, nan=0.0, posinf=0.0, neginf=0.0)
            h_norm, _ = _pf_rmsnorm(h)
            return h_norm + x

        def _memory_grad(keys, values, theta, Ws):
            Ws = [jax.lax.stop_gradient(W) for W in Ws]
            acts = [keys]
            pres = []
            h = keys
            n = len(Ws)
            for i, W in enumerate(Ws):
                pre = jnp.matmul(h, W)
                pres.append(pre)
                h = jax.nn.gelu(pre, approximate=False) if i < n - 1 else pre
                acts.append(h)
            h_norm, rms = _pf_rmsnorm(acts[-1])
            pred = h_norm + keys
            d_pred = 2.0 * theta[..., None] * (pred - values)
            d_h = _pf_rmsnorm_bwd(d_pred, h_norm, rms)
            grads = [None] * n
            for i in range(n - 1, -1, -1):
                grads[i] = jnp.einsum('bsi,bso->bio', acts[i], d_h)
                if i > 0:
                    d_h = jnp.matmul(d_h, Ws[i].transpose(0, 2, 1)) * _gelu_grad(pres[i - 1])
            return grads

        def _clip_grads(grads, max_norm=10.0):
            sq = sum((jnp.sum(g.reshape(g.shape[0], -1) ** 2, axis=1) for g in grads))
            coef = jnp.minimum(max_norm / (jnp.sqrt(sq) + 1e-06), 1.0)
            coef = jax.lax.stop_gradient(coef)[:, None, None]
            return [g * coef for g in grads]
        b = x.shape[0]
        bh = b * H
        Ws = [jnp.broadcast_to(mem_W0, (bh,) + mem_W0.shape), jnp.broadcast_to(mem_W1, (bh,) + mem_W1.shape)]
        mom = [jnp.zeros_like(W) for W in Ws]
        x_n = _rmsnorm_w(x, store_norm_w)
        keys = _rmsnorm_w(_split_heads(x_n @ W_K), k_norm_w)
        values = _split_heads(x_n @ W_V)
        alpha = jax.nn.sigmoid(x_n @ alpha_w + alpha_b)
        theta = jax.nn.sigmoid(x_n @ theta_w + theta_b) * MAX_LR
        eta = jax.nn.sigmoid(x_n @ eta_w + eta_b)
        to_bh = lambda t: t.transpose(0, 2, 1).reshape(bh, -1)
        alpha, theta, eta = (to_bh(alpha), to_bh(theta), to_bh(eta))
        grads = _clip_grads(_memory_grad(keys, values, theta, Ws))
        a_mean = jnp.mean(alpha, axis=1)[:, None, None]
        e_mean = jnp.mean(eta, axis=1)[:, None, None]
        new_Ws = []
        for W, m, g in zip(Ws, mom, grads):
            new_m = e_mean * m - g
            new_w = (1.0 - a_mean) * W + new_m
            new_w = jnp.where(jnp.isfinite(new_w), new_w, jax.lax.stop_gradient(W))
            new_Ws.append(new_w)
        q = _rmsnorm_w(_split_heads(_rmsnorm_w(x, retrieve_norm_w) @ W_Q), q_norm_w)
        out = _memory_forward(q, new_Ws)
        return _merge_heads(out, b)

    def _L1_ffn_ref(x, shared_up, shared_down, routed_up, routed_down, router_w):
        import jax, jax.numpy as jnp
        import numpy as np
        H_DIM, E_DIM = (128, 64)
        N_SHARED, N_ROUTED, TOP_K = (2, 16, 4)
        B, S = (4, 256)
        b, s, h = x.shape
        xt = x.reshape(-1, h)
        up_s = jnp.einsum('th,seh->tse', xt, shared_up)
        shared = jnp.einsum('tse,she->th', jax.nn.gelu(up_s, approximate=False), shared_down)
        probs = jax.nn.softmax(xt @ router_w.T, axis=-1)
        topk_p, topk_i = jax.lax.top_k(probs, TOP_K)
        gate = jnp.zeros_like(probs).at[jnp.arange(xt.shape[0])[:, None], topk_i].add(topk_p)
        up_r = jnp.einsum('th,reh->tre', xt, routed_up)
        act = jax.nn.gelu(up_r, approximate=False) * gate[:, :, None]
        routed = jnp.einsum('tre,rhe->th', act, routed_down)
        return (shared + routed).reshape(b, s, h)
    x = L0_attn_x
    xn = _layernorm(x, axis=-1)
    s = _L0_attn_ref(xn, L0_attn_Wq, L0_attn_Wk, L0_attn_Wv, L0_attn_Wu, L0_attn_bu)
    g = _silu(_L0_ffn_ref(xn, L0_ffn_router_w, L0_ffn_router_b, L0_ffn_expert_w, L0_ffn_expert_b))
    x = x + s * g
    xn = _layernorm(x, axis=-1)
    s = _L1_attn_ref(xn, L1_attn_W_K, L1_attn_W_V, L1_attn_W_Q, L1_attn_mem_W0, L1_attn_mem_W1, L1_attn_k_norm_w, L1_attn_q_norm_w, L1_attn_store_norm_w, L1_attn_retrieve_norm_w, L1_attn_alpha_w, L1_attn_alpha_b, L1_attn_theta_w, L1_attn_theta_b, L1_attn_eta_w, L1_attn_eta_b)
    g = _silu(_L1_ffn_ref(xn, L1_ffn_shared_up, L1_ffn_shared_down, L1_ffn_routed_up, L1_ffn_routed_down, L1_ffn_router_w))
    x = x + s * g
    return x

_drawn_inputs = setup_inputs


def setup_inputs(seed=0):
    import zlib

    import numpy as np

    out = dict(_drawn_inputs(seed))
    spreads = {'L0_ffn_router_b': (0.0, 0.1),
     'L0_ffn_expert_b': (0.0, 0.294),
     'L1_attn_k_norm_w': (1.0, 0.2),
     'L1_attn_q_norm_w': (1.0, 0.2),
     'L1_attn_store_norm_w': (1.0, 0.6),
     'L1_attn_retrieve_norm_w': (1.0, 0.2),
     'L1_attn_alpha_b': (-5.0, 0.6),
     'L1_attn_theta_b': (-3.0, 0.2),
     'L1_attn_eta_b': (0.0, 0.1)}
    factors = {'L0_attn_Wq': 8.0,
     'L0_attn_Wk': 8.0,
     'L1_attn_alpha_w': 8.0,
     'L1_attn_theta_w': 8.0,
     'L1_ffn_routed_up': 2.746,
     'L1_ffn_router_w': 2.9}
    for name, (base, spread) in spreads.items():
        noise = np.random.default_rng([zlib.crc32(name.encode()), seed]).standard_normal(out[name].shape)
        drawn = base * np.exp(spread * noise) if base else spread * noise
        out[name] = jnp.asarray(drawn.astype(out[name].dtype))
    for name, factor in factors.items():
        out[name] = (out[name] * factor).astype(out[name].dtype)
    return out
```

```python
from contextlib import ExitStack

import concourse.bass as bass
from concourse import mybir

ALU = mybir.AluOpType
ACT = mybir.ActivationFunctionType
AX_X = mybir.AxisListType.X
F32 = mybir.dt.float32
F32R = mybir.dt.float32r
I32 = mybir.dt.int32

P = 128
B, S, D = 16, 256, 128
TT = S // P
NT = B * TT
H, HD = 16, 8
NJ, NG = 4, 4
HID = 4 * HD
E0, TOP0 = 8, 2
E1, TOP1 = 16, 4
FE = 64
NC1 = 1 + E1 * FE // P
LN_EPS, RMS_EPS, PF_EPS = 1e-5, 1e-6, 1e-8
ATT_SCALE = float(D) ** 0.25
CLIP = 10.0
MAX_LR = 0.01
RSQRT_MAGIC = float(0x5F3759DF)
BIG = 3.0e38

T_Q, T_K, T_V, T_U, T_EXP, T_UP, T_DOWN, T_ROUTE, N_T = 0, 1, 2, 3, 4, 20, 29, 38, 39

N_R = 2 * E0 + E1

C_ID = 0
C_SELQ = C_ID + P
C_SELK = C_SELQ + 1
C_ONEK = C_SELK + 1
C_HEAD = C_ONEK + 1
C_BD0 = C_HEAD + P
C_BD1T = C_BD0 + H * HID
C_BD1 = C_BD1T + P
C_CODE = C_BD1 + NG * HD
C_REP8 = C_CODE + E1
C_REP32 = C_REP8 + P
C_SEL0 = C_REP32 + P
C_SEL1 = C_SEL0 + E0 * P
C_ONE = C_SEL1 + 8 * P
N_C = C_ONE + 1


class Signal:

    def __init__(self, sem, per):
        self.sem, self.per = sem, per

    def now(self, i, k=None):
        return i * self.per + self.per + (self.per if k is None else k)

    def before(self, i, k=None):
        return i * self.per + (self.per if k is None else k)


class Steps:

    def __init__(self, sem, per=0, turn=0):
        self.sem, self.per, self.turn, self.n = sem, per, turn, 0

    def one(self):
        self.n += 1
        return 1

    def value(self):
        return self.turn * self.per + self.n

    def end(self):
        assert self.n == self.per, (self.n, self.per)


DVE_TURN0, DVE_TURN1 = 29, 123


def build(nc, consts, L0_attn_x, L0_attn_Wq, L0_attn_Wk, L0_attn_Wv, L0_attn_Wu, L0_attn_bu,
          L0_ffn_router_w, L0_ffn_router_b, L0_ffn_expert_w, L0_ffn_expert_b,
          L1_attn_W_K, L1_attn_W_V, L1_attn_W_Q, L1_attn_mem_W0, L1_attn_mem_W1,
          L1_attn_k_norm_w, L1_attn_q_norm_w, L1_attn_store_norm_w, L1_attn_retrieve_norm_w,
          L1_attn_alpha_w, L1_attn_alpha_b, L1_attn_theta_w, L1_attn_theta_b, L1_attn_eta_w,
          L1_attn_eta_b, L1_ffn_shared_up, L1_ffn_shared_down, L1_ffn_routed_up,
          L1_ffn_routed_down, L1_ffn_router_w, out):
    ctx = ExitStack()
    with ctx:
        def sb(name, shape, dt=F32):
            return ctx.enter_context(nc.sbuf_tensor(name, shape, dt))

        def sem(name):
            return ctx.enter_context(nc.semaphore(name))

        cst = sb("cst", [P, N_C])
        ident = cst[:, C_ID:C_ID + P]
        wraw = sb("wraw", [P, N_T, P])
        wT = sb("wT", [P, N_T, P])
        wq_rep = sb("wq_rep", [P, NJ, P])
        wk_rep = sb("wk_rep", [P, NJ, P])
        wv_route = sb("wv_route", [P, D + E0])
        sel0 = sb("sel0", [E0, E0, P], F32R)
        sel1 = sb("sel1", [2 * E1, NC1 - 1, P], F32R)
        exp_b = sb("exp_b", [E0, 2, D])
        bu_bc = sb("bu_bc", [P, D])
        rb_bc = sb("rb_bc", [P, 2, E0])
        gate_b = sb("gate_b", [P, 3 * H])
        norm_col = sb("norm_col", [P, 2])
        knq = sb("knq", [P, 2, HD])
        knq_bc = sb("knq_bc", [P, 2, H, HD])
        wraw1 = sb("wraw1", [P, 3, P])
        graw1 = sb("graw1", [P, 3 * H])
        NPRO = 3 * D + 3 * H + E1
        w_pro = sb("w_pro", [P, NPRO])
        mem0 = sb("mem0", [HD, HID])
        mem1 = sb("mem1", [HID, HD])
        mem1r = sb("mem1r", [HID, H, HD])
        rep = sb("rep", [P, 2 * HID + HD])
        NW = H * HID + P
        w_bd = sb("w_bd", [P, NW])
        w1_bd = sb("w1_bd", [P, NG * HD])
        w1t_bd = sb("w1t_bd", [P, H * HID])
        x_all = sb("x_all", [P, B, TT, D])
        stats = sb("stats", [P, NT, 6])
        mean = sb("mean", [P, NT])
        nrm = sb("nrm", [P, 2, NT])
        nrm_in = sb("nrm_in", [P, 2, NT])
        nt0 = sb("nt0", [P, NT])
        nt1 = sb("nt1", [P, NT])
        newt = sb("newt", [P, 2 * NT])

        xn = sb("xn", [P, TT, D])
        xnT = sb("xnT", [P, S])
        v1 = sb("v1", [P, TT, H, 32])
        logit = sb("logit", [P, TT, E1])
        work = sb("work", [P, TT, E1])
        hit = sb("hit", [P, TT, E1])
        code = sb("code", [P, TT, E1])
        top = sb("top", [P, TT])
        chosen = sb("chosen", [P, TT, E1])
        mask = sb("mask", [P, TT, 2 * E1])
        maskT = sb("maskT", [2 * E1, S], F32R)
        big = ctx.enter_context(ExitStack())

        def sb0(name, shape, dt=F32):
            return big.enter_context(nc.sbuf_tensor(name, shape, dt))

        psum = ctx.enter_context(nc.psum_tensor("psum", [P, 8, 512], F32))

        consts_in, raw_in, small_in, x_in = sem("consts_in"), sem("raw_in"), sem("small_in"), sem("x_in")
        x_out = sem("x_out")
        raw_turned, raw_copied, mem_rep, setup_done = (
            sem("raw_turned"), sem("raw_copied"), sem("mem_rep"), sem("setup_done"))
        zeroed = sem("zeroed")
        rep_src = sem("rep_src")
        dve_setup = sem("dve_setup")
        stats_ready = sem("stats_ready")
        dve_mid = sem("dve_mid")
        layer0_done = sem("layer0_done")

        loads = [
            (wraw[:, T_Q, :], L0_attn_Wq), (wraw[:, T_K, :], L0_attn_Wk),
            (wraw[:, T_V, :], L0_attn_Wv), (wraw[:, T_U, :], L0_attn_Wu),
            (wraw[:, T_EXP:T_UP, :], L0_ffn_expert_w.rearrange("l e d h -> d (l e) h")),
            (wraw[:, T_UP, :], L1_ffn_shared_up.rearrange("s e h -> (s e) h")),
            (wraw[:, T_UP + 1:T_DOWN, :], L1_ffn_routed_up.rearrange("(c s) e h -> (s e) c h", s=2)),
            (wraw[:, T_DOWN, :].rearrange("p (s e) -> p s e", s=2), L1_ffn_shared_down.rearrange("s h e -> h s e")),
            (wraw[:, T_DOWN + 1:T_ROUTE, :].rearrange("p c (s e) -> p (c s) e", s=2),
             L1_ffn_routed_down.rearrange("r h e -> h r e")),
            (wraw[0:2 * E0, T_ROUTE, :], L0_ffn_router_w.rearrange("l e h -> (l e) h")),
            (wraw[2 * E0:2 * E0 + E1, T_ROUTE, :], L1_ffn_router_w),
        ]
        small = [
            (wraw1[:, 0, :], L1_attn_W_K), (wraw1[:, 1, :], L1_attn_W_Q), (wraw1[:, 2, :], L1_attn_W_V),
            (graw1[:, 0:H], L1_attn_alpha_w), (graw1[:, H:2 * H], L1_attn_eta_w), (graw1[:, 2 * H:3 * H], L1_attn_theta_w),
            (gate_b[:, 0:H], L1_attn_alpha_b.partition_broadcast(P)),
            (gate_b[:, H:2 * H], L1_attn_eta_b.partition_broadcast(P)),
            (gate_b[:, 2 * H:3 * H], L1_attn_theta_b.partition_broadcast(P)),
            (bu_bc[:, :], L0_attn_bu.partition_broadcast(P)),
            (rb_bc[:, :, :], L0_ffn_router_b.partition_broadcast(P)),
            (norm_col[:, 0:1], L1_attn_store_norm_w.rearrange("(p a) -> p a", a=1)),
            (norm_col[:, 1:2], L1_attn_retrieve_norm_w.rearrange("(p a) -> p a", a=1)),
            (knq[:, 0, :], L1_attn_k_norm_w.partition_broadcast(P)),
            (knq[:, 1, :], L1_attn_q_norm_w.partition_broadcast(P)),
            (exp_b[:, :, :], L0_ffn_expert_b.rearrange("l e d -> e l d")),
            (mem0[:, :], L1_attn_mem_W0), (mem1[:, :], L1_attn_mem_W1),
        ]
        n_groups = (N_T + 3) // 4

        def newton(dve, chain, y, x, t, n):
            yi, xi = y.bitcast(I32), x.bitcast(I32)
            dve.tensor_scalar(yi, xi, 1, None, ALU.logical_shift_right).then_inc(chain.sem, chain.one())
            dve.wait_ge(chain.sem, chain.value())
            dve.tensor_scalar(yi, yi, -1.0, RSQRT_MAGIC, ALU.mult, ALU.add).then_inc(chain.sem, chain.one())
            dve.wait_ge(chain.sem, chain.value())
            for _ in range(3):
                dve.tensor_tensor(t, y, y, ALU.mult).then_inc(chain.sem, chain.one())
                dve.wait_ge(chain.sem, chain.value())
                dve.scalar_tensor_tensor(out=t, in0=t, scalar=-0.5, in1=x, op0=ALU.mult, op1=ALU.mult).then_inc(chain.sem, chain.one())
                dve.wait_ge(chain.sem, chain.value())
                dve.scalar_tensor_tensor(out=y, in0=t, scalar=1.5, in1=y, op0=ALU.add, op1=ALU.mult).then_inc(chain.sem, chain.one())
                dve.wait_ge(chain.sem, chain.value())

        def layer_stats(dve, chain, second):
            me, mo = stats[:, :, 1], stats[:, :, 4]
            dve.tensor_tensor(nt0[:, :], me, mo, ALU.add).then_inc(chain.sem, chain.one())
            dve.wait_ge(chain.sem, chain.value())
            dve.tensor_scalar(mean[:, :], nt0[:, :], 0.5, None, ALU.mult).then_inc(chain.sem, chain.one())
            dve.tensor_tensor(nt1[:, :], me, mo, ALU.subtract).then_inc(chain.sem, chain.one())
            dve.wait_ge(chain.sem, chain.value())
            dve.scalar_tensor_tensor(out=nt1[:, :], in0=nt1[:, :], scalar=0.25, in1=nt1[:, :],
                                     op0=ALU.mult, op1=ALU.mult).then_inc(chain.sem, chain.one())
            dve.wait_ge(chain.sem, chain.value())
            dve.tensor_tensor(nt0[:, :], stats[:, :, 2], stats[:, :, 5], ALU.add).then_inc(chain.sem, chain.one())
            dve.wait_ge(chain.sem, chain.value())
            dve.scalar_tensor_tensor(out=nt0[:, :], in0=nt0[:, :], scalar=1.0 / D, in1=nt1[:, :],
                                     op0=ALU.mult, op1=ALU.add).then_inc(chain.sem, chain.one())
            dve.wait_ge(chain.sem, chain.value())
            dve.tensor_scalar(nrm_in[:, 0, :], nt0[:, :], LN_EPS, None, ALU.add).then_inc(chain.sem, chain.one())
            dve.wait_ge(chain.sem, chain.value())
            if not second:
                newton(dve, chain, nrm[:, 0, :], nrm_in[:, 0, :], newt[:, 0:NT], NT)
                return
            dve.reciprocal(nt1[:, :], nrm_in[:, 0, :]).then_inc(chain.sem, chain.one())
            dve.wait_ge(chain.sem, chain.value())
            dve.tensor_tensor(nt1[:, :], nt0[:, :], nt1[:, :], ALU.mult).then_inc(chain.sem, chain.one())
            dve.wait_ge(chain.sem, chain.value())
            dve.tensor_scalar(nrm_in[:, 1, :], nt1[:, :], RMS_EPS, None, ALU.add).then_inc(chain.sem, chain.one())
            dve.wait_ge(chain.sem, chain.value())
            newton(dve, chain, nrm[:, :, :].rearrange("p a n -> p (a n)"), nrm_in[:, :, :].rearrange("p a n -> p (a n)"),
                   newt[:, :], 2 * NT)

        with nc.Block() as block:
            @block.sync
            def _(sp):
                sp.dma_start(cst[:, :], consts).then_inc(consts_in, 16)
                for dst, src in loads:
                    sp.dma_start(dst, src).then_inc(raw_in, 16)
                sp.dma_start(x_all[:, :, :, :], L0_attn_x.rearrange("b (t p) d -> p b t d", p=P)).then_inc(x_in, 16)

            @block.gpsimd
            def _(pool):
                pool.memset(v1[:, :, :, :], 0.0).then_inc(zeroed, 1)
                pool.memset(wq_rep[:, :, :], 0.0).then_inc(zeroed, 1)
                pool.memset(wk_rep[:, :, :], 0.0).then_inc(zeroed, 1)
                pool.memset(mask[:, :, :], 0.0).then_inc(zeroed, 1)
                pool.wait_ge(zeroed, 4)
                pool.memset(v1[:, :, :, HD:HD + 1], 1.0).then_inc(zeroed, 1)

            @block.scalar
            def _(act):
                for dst, src in small:
                    act.dma_start(dst, src).then_inc(small_in, 16)
                for n in range(n_groups):
                    m = min(4, N_T - 4 * n)
                    act.wait_ge(raw_turned, n + 1)
                    w = m * P if n < n_groups - 1 else (m - 1) * P + N_R
                    nc.scalar.activation(wT[:, 4 * n:4 * n + m, :].rearrange("p m n -> p (m n)")[:, 0:w],
                                         psum[:, n % 4, 0:w], ACT.Copy).then_inc(raw_copied, 1)

            @block.tensor
            def _(pe):
                pe.wait_ge(consts_in, 16)
                pe.wait_ge(raw_in, 16 * len(loads))
                for n in range(n_groups):
                    m = min(4, N_T - 4 * n)
                    if n >= 4:
                        pe.wait_ge(raw_copied, n - 3)
                    for t in range(m):
                        r = N_R if 4 * n + t == T_ROUTE else P
                        last = nc.tensor.transpose(psum[:, n % 4, t * P:t * P + r], wraw[0:r, 4 * n + t, :], ident[0:r, 0:r])
                    last.then_inc(raw_turned, 1)
                pe.wait_ge(small_in, 16 * len(small))
                pe.wait_ge(rep_src, 1)
                nc.tensor.matmul(psum[:, 4, 0:HID], cst[0:HD, C_REP8:C_REP8 + P], mem0[:, :], start=True, stop=True)
                nc.tensor.matmul(psum[:, 4, HID:HID + HD], cst[0:HID, C_REP32:C_REP32 + P], mem1[:, :], start=True, stop=True)
                nc.tensor.matmul(psum[:, 4, HID + HD:2 * HID + HD], mem1r[:, :, :].rearrange("j h d -> j (h d)"),
                                 cst[0:HID, C_ID:C_ID + HID], start=True, stop=True).then_inc(mem_rep, 1)

            @block.vector
            def _(dve):
                ch = Steps(dve_setup)
                dve.wait_ge(small_in, 16 * len(small))
                dve.wait_ge(consts_in, 16)
                dve.tensor_copy(mem1r[:, :, :], mem1[:, :].unsqueeze(1).to_broadcast([HID, H, HD])).then_inc(rep_src, 1)
                dve.tensor_copy(sel0[:, :, :], cst[0:E0, C_SEL0:C_SEL0 + E0 * P].rearrange("e (a p) -> e a p", p=P)).then_inc(ch.sem, ch.one())
                dve.tensor_copy(sel1[:, :, :], cst[0:2 * E1, C_SEL1:C_SEL1 + 8 * P].rearrange("e (a p) -> e a p", p=P)).then_inc(ch.sem, ch.one())
                dve.tensor_copy(knq_bc[:, :, :, :].rearrange("p a h d -> p a h d"),
                                knq[:, :, :].unsqueeze(2).to_broadcast([P, 2, H, HD])).then_inc(ch.sem, ch.one())
                for m, (col, c) in enumerate(((0, 0), (1, 1), (0, 2))):
                    dve.tensor_scalar(w_pro[:, m * D:m * D + D], wraw1[:, c, :], norm_col[:, col:col + 1], None, ALU.mult).then_inc(ch.sem, ch.one())
                dve.tensor_scalar(w_pro[:, 3 * D:3 * D + 3 * H], graw1[:, :], norm_col[:, 0:1], None, ALU.mult).then_inc(ch.sem, ch.one())
                dve.wait_ge(mem_rep, 1)
                dve.tensor_tensor(w_bd[:, 0:H * HID].rearrange("p (h j) -> p h j", h=H),
                                  cst[:, C_BD0:C_BD0 + H * HID].rearrange("p (h j) -> p h j", h=H),
                                  psum[:, 4, 0:HID].unsqueeze(1).to_broadcast([P, H, HID]), ALU.mult).then_inc(ch.sem, ch.one())
                dve.tensor_tensor(w1_bd[:, :].rearrange("p (g d) -> p g d", g=NG),
                                  cst[:, C_BD1:C_BD1 + NG * HD].rearrange("p (g d) -> p g d", g=NG),
                                  psum[:, 4, HID:HID + HD].unsqueeze(1).to_broadcast([P, NG, HD]), ALU.mult).then_inc(ch.sem, ch.one())
                turned = psum[:, 4, HID + HD:2 * HID + HD]
                dve.tensor_tensor(w1t_bd[:, :].rearrange("p (h j) -> p h j", h=H),
                                  cst[:, C_BD0:C_BD0 + H * HID].rearrange("p (h j) -> p h j", h=H),
                                  turned.unsqueeze(1).to_broadcast([P, H, HID]), ALU.mult).then_inc(ch.sem, ch.one())
                dve.tensor_tensor(w_bd[:, H * HID:NW].rearrange("p (g j) -> p g j", g=NG),
                                  cst[:, C_BD1T:C_BD1T + P].rearrange("p (g j) -> p g j", g=NG),
                                  turned.unsqueeze(1).to_broadcast([P, NG, HID]), ALU.mult).then_inc(ch.sem, ch.one())
                dve.wait_ge(raw_copied, n_groups)
                dve.wait_ge(zeroed, 5)
                for rep_w, t, signs in ((wq_rep, T_Q, (1, -1, 1)), (wk_rep, T_K, (1, 1, -1))):
                    for r, sign in enumerate(signs):
                        dve.tensor_scalar(
                     rep_w[:, :, :].rearrange("p j (g c) -> p (j g) c", g=NG)[:, :, HD * r:HD * r + HD],
                     wT[:, t, :].rearrange("p (h d) -> p h d", h=H), sign / ATT_SCALE, None, ALU.mult).then_inc(ch.sem, ch.one())
                dve.tensor_copy(wv_route[:, 0:D], wT[:, T_V, :]).then_inc(ch.sem, ch.one())
                dve.tensor_copy(wv_route[:, D:D + E0], wT[:, T_ROUTE, 0:E0]).then_inc(ch.sem, ch.one())
                dve.tensor_copy(w_pro[:, 3 * D + 3 * H:NPRO], wT[:, T_ROUTE, 2 * E0:2 * E0 + E1]).then_inc(ch.sem, ch.one())
                dve.wait_ge(x_in, 16)
                with dve.Fori(0, NT) as t:
                    dve.bn_stats(stats[:, bass.ds(t, 1), :].rearrange("p a s -> p (a s)"),
                                 x_all[:, :, :, :].rearrange("p b t d -> p (b t) d")[:, bass.ds(t, 1), :].rearrange("p a d -> p (a d)")
                                 ).then_inc(stats_ready, 1)
                dve.wait_ge(stats_ready, NT)
                layer_stats(dve, ch, False)

        qhi, khi = sb0("qhi", [P, NJ, S], F32R), sb0("khi", [P, NJ, S], F32R)
        qst, kst = sb0("qst", [P, NJ, S], F32R), sb0("kst", [P, NJ, S], F32R)
        mneg = sb0("mneg", [P, TT, NJ, P])
        NPT = 3
        pT = sb0("pT", [P, NPT, 2, 2, S])
        oTs = sb0("oTs", [P, NJ, S])
        rsum = sb0("rsum", [P, TT * H])
        att = sb0("att", [P, TT, D])
        attT = sb0("attT", [P, S])
        xm = sb0("xm", [P, 2, 2, S])
        yT = sb0("yT", [P, S])
        th0 = sb0("th0", [P, S])
        gT0 = sb0("gT0", [P, S])
        sat = sb0("sat", [P, TT, D])
        zat = sb0("zat", [P, TT, D])

        scr = psum[:, 0:4, :].rearrange("p (s g) n -> p s g n", s=2)
        oT = psum[:, 4:6, :].rearrange("p a (j n) -> p (a j) n", j=2)
        pa, pb = psum[:, 6, :], psum[:, 7, :]
        NU = NJ * 2
        MASK_AT = 3

        xn_ready = Signal(sem("xn_ready"), 1)
        xn_turned = Signal(sem("xn_turned"), 1)
        xnT_ready = Signal(sem("xnT_ready"), 1)
        v_made = Signal(sem("v_made"), 1)
        v_ready = Signal(sem("v_ready"), 1)
        qk_made = Signal(sem("qk_made"), 2)
        qk_high = Signal(sem("qk_high"), 2)
        qk_ready = Signal(sem("qk_ready"), 2)
        scores_made = Signal(sem("scores_made"), NU)
        max_taken = Signal(sem("max_taken"), NU)
        max_turned = Signal(sem("max_turned"), 1)
        max_placed = Signal(sem("max_placed"), 1)
        st_made = Signal(sem("st_made"), NU)
        probs_ready = Signal(sem("probs_ready"), NU)
        pv_made = Signal(sem("pv_made"), NU)
        o_copied = Signal(sem("o_copied"), 1)
        o_turned = Signal(sem("o_turned"), 1)
        att_ready = Signal(sem("att_ready"), 1)
        att_turned = Signal(sem("att_turned"), 1)
        attT_ready = Signal(sem("attT_ready"), 1)
        s_made = Signal(sem("s_made"), 1)
        logits_made = Signal(sem("logits_made"), 1)
        router_read = Signal(sem("router_read"), 1)
        logits_read = Signal(sem("logits_read"), 1)
        mask_ready = Signal(sem("mask_ready"), 2)
        mask_turned = Signal(sem("mask_turned"), 2)
        maskT_ready = Signal(sem("maskT_ready"), 2)
        NCH = E0 // 2
        spread = Signal(sem("spread"), 2 * NCH)
        chosen_x = Signal(sem("chosen_x"), 2 * NCH)
        chunk_used = Signal(sem("chunk_used"), 2 * (NCH - 1))
        moe_made = Signal(sem("moe_made"), 2)
        yT_ready = Signal(sem("yT_ready"), 1)
        tanh_ready = Signal(sem("tanh_ready"), 1)
        gT_ready = Signal(sem("gT_ready"), 1)
        g_turned = Signal(sem("g_turned"), 1)
        x_updated = Signal(sem("x_updated"), 1)
        dve_turn0 = sem("dve_turn0")
        dve_front = sem("dve_front")
        x_waits_met = sem("x_waits_met")

        def choose(dve, chain, n, rounds, keep):
            w, hi, co, ch = (a[:, :, 0:n] for a in (work, hit, code, chosen))
            codes = cst[:, C_CODE + E1 - n:C_CODE + E1].unsqueeze(1).to_broadcast([P, TT, n])
            topb = top[:, :].unsqueeze(2).to_broadcast([P, TT, n])
            for r in range(rounds):
                dve.tensor_reduce(top[:, :], w, AX_X, ALU.max).then_inc(chain.sem, chain.one())
                dve.wait_ge(chain.sem, chain.value())
                dve.tensor_tensor(hi, w, topb, ALU.is_equal).then_inc(chain.sem, chain.one())
                dve.wait_ge(chain.sem, chain.value())
                dve.tensor_tensor(co, hi, codes, ALU.mult).then_inc(chain.sem, chain.one())
                dve.wait_ge(chain.sem, chain.value())
                dve.tensor_reduce(top[:, :], co, AX_X, ALU.max).then_inc(chain.sem, chain.one())
                dve.wait_ge(chain.sem, chain.value())
                dve.tensor_tensor(hi, co, topb, ALU.is_equal).then_inc(chain.sem, chain.one())
                dve.wait_ge(chain.sem, chain.value())
                if r < rounds - 1:
                    dve.scalar_tensor_tensor(out=w, in0=hi, scalar=-keep, in1=w, op0=ALU.mult, op1=ALU.add).then_inc(chain.sem, chain.one())
                    dve.wait_ge(chain.sem, chain.value())
                if r == 0:
                    dve.tensor_copy(ch, hi).then_inc(chain.sem, chain.one())
                    dve.wait_ge(chain.sem, chain.value())
                elif r < rounds - 1:
                    dve.tensor_tensor(ch, ch, hi, ALU.add).then_inc(chain.sem, chain.one())
                    dve.wait_ge(chain.sem, chain.value())
            return ch, hi

        with nc.Block() as block:
            @block.tensor
            def _(pe):
                for sg in (xn_turned, v_made, qk_made, scores_made, max_turned, st_made, pv_made, o_turned, att_turned,
                           s_made, logits_made, mask_turned, spread, chunk_used, moe_made, g_turned):
                    pe.sem_inc(sg.sem, sg.per)

                def turn_tokens(n):
                    pe.wait_ge(xn_ready.sem, xn_ready.now(n))
                    pe.wait_ge(chosen_x.sem, chosen_x.before(n))
                    for t in range(TT):
                        last = nc.tensor.transpose(pa[:, t * P:t * P + P], xn[:, t, :], ident)
                    last.then_inc(xn_turned.sem, 1)

                def project(n):
                    pe.wait_ge(xnT_ready.sem, xnT_ready.now(n))
                    pe.wait_ge(gT_ready.sem, gT_ready.before(n))
                    for t in range(TT):
                        last = nc.tensor.matmul(pb[:, t * 136:t * 136 + 136], xnT[:, t * P:t * P + P], wv_route[:, :],
                                                start=True, stop=True)
                    last.then_inc(v_made.sem, 1)
                    pe.wait_ge(probs_ready.sem, probs_ready.before(n))
                    for m, w in enumerate((wq_rep, wk_rep)):
                        o = scr[:, m, :, :].rearrange("p g (j n) -> p (g j) n", j=2)
                        for j in range(NJ):
                            last = nc.tensor.matmul(o[:, j, :], w[:, j, :], xnT[:, :], start=True, stop=True)
                        last.then_inc(qk_made.sem, 1)

                def turn(i, follows):
                    def scores(u):
                        j, gp = u // 2, u % 2
                        if u == 0:
                            pe.wait_ge(qk_ready.sem, qk_ready.now(i))
                        if u >= 2:
                            pe.wait_ge(max_taken.sem, max_taken.now(i, u - 1))
                        for t in range(TT):
                            for g2 in range(2):
                                r = 32 * (2 * gp + g2)
                                last = nc.tensor.matmul(scr[:, u % 2, g2, t * S:t * S + S], qst[r:r + 32, j, t * P:t * P + P],
                                                        kst[r:r + 32, j, :], start=True, stop=True)
                        last.then_inc(scores_made.sem, 1)

                    def mask_turn(l):
                        pe.wait_ge(mask_ready.sem, mask_ready.now(i, l + 1))
                        if l == 1:
                            pe.wait_ge(logits_read.sem, logits_read.now(i))
                        for t in range(TT):
                            last = nc.tensor.transpose(pa[0:E0, t * P:t * P + P], mask[:, t, 0:E0], ident)
                        last.then_inc(mask_turned.sem, 1)

                    def spread_chunk(l, c):
                        if c == 0:
                            pe.wait_ge(maskT_ready.sem, maskT_ready.now(i, l + 1))
                        else:
                            pe.wait_ge(chosen_x.sem, chosen_x.now(i, NCH * l + c))
                        for e2 in range(2):
                            last = nc.tensor.matmul(pa[:, e2 * S:e2 * S + S], sel0[:, 2 * c + e2, :], maskT[0:E0, :],
                                                    start=True, stop=True)
                        last.then_inc(spread.sem, 1)

                    def experts(l, c):
                        if c == 0:
                            if l == 0:
                                pe.wait_ge(v_ready.sem, v_ready.now(i))
                                pe.wait_ge(router_read.sem, router_read.now(i))
                            else:
                                pe.wait_ge(yT_ready.sem, yT_ready.now(i))
                            nc.tensor.matmul(pb[:, 0:S], exp_b[:, l, :], maskT[0:E0, :].bitcast(F32), start=True, stop=False)
                        pe.wait_ge(chosen_x.sem, chosen_x.now(i, NCH * l + c + 1))
                        for e2 in range(2):
                            last = nc.tensor.matmul(pb[:, 0:S], wT[:, T_EXP + E0 * l + 2 * c + e2, :], xm[:, c % 2, e2, :],
                                                    start=False, stop=(c == NCH - 1 and e2 == 1))
                        last.then_inc((chunk_used if c < NCH - 1 else moe_made).sem, 1)

                    def route_again():
                        pe.wait_ge(yT_ready.sem, yT_ready.now(i))
                        for t in range(TT):
                            last = nc.tensor.matmul(pa[:, t * E0:t * E0 + E0], yT[:, t * P:t * P + P], wT[:, T_ROUTE, E0:2 * E0],
                                                    start=True, stop=True)
                        last.then_inc(logits_made.sem, 1)

                    def scores_t(u):
                        j, gp = u // 2, u % 2
                        if u == 0:
                            pe.wait_ge(max_placed.sem, max_placed.now(i))
                        if u >= 2:
                            pe.wait_ge(probs_ready.sem, probs_ready.now(i, u - 1))
                        for c in range(2):
                            for g2 in range(2):
                                r = 32 * (2 * gp + g2)
                                last = nc.tensor.matmul(scr[:, u % 2, g2, c * S:c * S + S], kst[r:r + 32, j, c * P:c * P + P],
                                                        qst[r:r + 32, j, :], start=True, stop=True)
                        last.then_inc(st_made.sem, 1)

                    def weigh(u):
                        j, gp = u // 2, u % 2
                        pe.wait_ge(probs_ready.sem, probs_ready.now(i, u + 1))
                        for c in range(2):
                            for g2 in range(2):
                                g = 2 * gp + g2
                                last = nc.tensor.matmul(oT[32 * g:32 * g + 32, j, :], v1[:, c, NG * j + g, :],
                                                        pT[:, u % NPT, g2, c, :], start=(c == 0), stop=(c == 1),
                                                        skip_group_check=True)
                        last.then_inc(pv_made.sem, 1)

                    scores(0)
                    scores(1)
                    mask_turn(0)
                    scores(2)
                    spread_chunk(0, 0)
                    scores(3)
                    for c in range(NCH):
                        if c + 1 < NCH:
                            spread_chunk(0, c + 1)
                        experts(0, c)
                        scores(NCH + c)
                    pe.wait_ge(max_taken.sem, max_taken.now(i))
                    pe.wait_ge(x_updated.sem, x_updated.before(i))
                    for j in range(NJ):
                        for t in range(TT):
                            last = nc.tensor.transpose(oT[:, j, t * P:t * P + P], mneg[:, t, j, :], ident)
                    last.then_inc(max_turned.sem, 1)
                    route_again()
                    for u in range(NU + 1):
                        if u < NU:
                            scores_t(u)
                        if u >= 1:
                            weigh(u - 1)
                        if u == MASK_AT:
                            mask_turn(1)
                        if u == MASK_AT + 1:
                            spread_chunk(1, 0)
                        if u > MASK_AT + 1 and u - MASK_AT - 2 < NCH - 1:
                            spread_chunk(1, u - MASK_AT - 1)
                            experts(1, u - MASK_AT - 2)
                    for c in range(NU - MASK_AT - 1, NCH):
                        if c < NCH - 1:
                            spread_chunk(1, c + 1)
                            experts(1, c)
                    oX = psum[:, 4:6, :].rearrange("p t (j c) -> p t j c", j=NJ)
                    if follows:
                        turn_tokens(i + 1)
                    experts(1, NCH - 1)
                    pe.wait_ge(o_copied.sem, o_copied.now(i))
                    for t in range(TT):
                        for j in range(NJ):
                            last = nc.tensor.transpose(oX[:, t, j, :], oTs[:, j, t * P:t * P + P], ident)
                    last.then_inc(o_turned.sem, 1)
                    if follows:
                        project(i + 1)
                    pe.wait_ge(att_ready.sem, att_ready.now(i))
                    for t in range(TT):
                        last = nc.tensor.transpose(psum[:, 4, t * P:t * P + P], att[:, t, :], ident)
                    last.then_inc(att_turned.sem, 1)
                    pe.wait_ge(gT_ready.sem, gT_ready.now(i))
                    for t in range(TT):
                        last = nc.tensor.transpose(psum[:, 5, t * P:t * P + P], gT0[:, t * P:t * P + P], ident)
                    last.then_inc(g_turned.sem, 1)
                    pe.wait_ge(attT_ready.sem, attT_ready.now(i))
                    for t in range(TT):
                        last = nc.tensor.matmul(psum[:, 5, S + t * P:S + t * P + P], attT[:, t * P:t * P + P], wT[:, T_U, :],
                                                start=True, stop=True)
                    last.then_inc(s_made.sem, 1)

                turn_tokens(0)
                project(0)
                with pe.Fori(0, B - 1) as i:
                    turn(i, True)
                turn(B - 1, False)

            @block.scalar
            def _(act):
                for sg in (xnT_ready, v_ready, qk_high, probs_ready, o_copied, maskT_ready, yT_ready, tanh_ready, attT_ready):
                    act.sem_inc(sg.sem, sg.per)

                def tokens_copy(n):
                    act.wait_ge(xn_turned.sem, xn_turned.now(n))
                    act.wait_ge(qk_made.sem, qk_made.before(n))
                    act.wait_ge(chosen_x.sem, chosen_x.before(n, NCH))
                    nc.scalar.activation(xnT[:, :], pa[:, 0:S], ACT.Copy).then_inc(xnT_ready.sem, 1)

                def values_copy(n):
                    act.wait_ge(v_made.sem, v_made.now(n))
                    act.wait_ge(router_read.sem, router_read.now(n))
                    act.wait_ge(pv_made.sem, pv_made.before(n))
                    nc.scalar.activation(v1[:, :, :, 0:HD],
                                         pb[:, 0:TT * 136].rearrange("p (t c) -> p t c", t=TT)[:, :, 0:D]
                                         .rearrange("p t (h d) -> p t h d", h=H), ACT.Copy).then_inc(v_ready.sem, 1)

                def high_parts(n):
                    for m, hi in enumerate((qhi, khi)):
                        act.wait_ge(qk_made.sem, qk_made.now(n, m + 1))
                        act.wait_ge(qk_ready.sem, qk_ready.before(n))
                        src = scr[:, m, :, :].rearrange("p g (j n) -> p (g j) n", j=2)
                        if m == 0:
                            nc.scalar.activation(hi[:, :, :], src, ACT.Copy).then_inc(qk_high.sem, 1)
                        else:
                            nc.scalar.activation(hi[:, :, :], src, ACT.Identity, bias=cst[:, C_ONEK:C_ONEK + 1]
                                                 ).then_inc(qk_high.sem, 1)

                def turn(i, follows):
                    def probs(u):
                        act.wait_ge(st_made.sem, st_made.now(i, u + 1))
                        if u >= NPT:
                            act.wait_ge(pv_made.sem, pv_made.now(i, u + 1 - NPT))
                        else:
                            act.wait_ge(pv_made.sem, pv_made.before(i))
                        nc.scalar.activation(pT[:, u % NPT, :, :, :].rearrange("p g c n -> p g (c n)"), scr[:, u % 2, :, :],
                                             ACT.Exp).then_inc(probs_ready.sem, 1)

                    def mask_copy(l):
                        act.wait_ge(mask_turned.sem, mask_turned.now(i, l + 1))
                        if l == 0:
                            act.wait_ge(moe_made.sem, moe_made.before(i))
                        else:
                            act.wait_ge(moe_made.sem, moe_made.now(i, 1))
                        nc.scalar.activation(maskT[0:E0, :], pa[0:E0, 0:S], ACT.Copy).then_inc(maskT_ready.sem, 1)

                    mask_copy(0)
                    act.wait_ge(moe_made.sem, moe_made.now(i, 1))
                    nc.scalar.activation(yT[:, :], pb[:, 0:S], ACT.Copy).then_inc(yT_ready.sem, 1)
                    for u in range(NU):
                        probs(u)
                        if u == MASK_AT:
                            mask_copy(1)
                    act.wait_ge(pv_made.sem, pv_made.now(i))
                    act.wait_ge(o_turned.sem, o_turned.before(i))
                    nc.scalar.activation(oTs[:, :, :], oT, ACT.Copy).then_inc(o_copied.sem, 1)
                    if follows:
                        tokens_copy(i + 1)
                    act.wait_ge(moe_made.sem, moe_made.now(i))
                    act.wait_ge(gT_ready.sem, gT_ready.before(i))
                    nc.scalar.activation(th0[:, :], pb[:, 0:S], ACT.Tanh, scale=0.5).then_inc(tanh_ready.sem, 1)
                    if follows:
                        high_parts(i + 1)
                        values_copy(i + 1)
                    act.wait_ge(att_turned.sem, att_turned.now(i))
                    act.wait_ge(s_made.sem, s_made.before(i))
                    nc.scalar.activation(attT[:, :], psum[:, 4, 0:S], ACT.Copy).then_inc(attT_ready.sem, 1)

                tokens_copy(0)
                high_parts(0)
                values_copy(0)
                with act.Fori(0, B - 1) as i:
                    turn(i, True)
                turn(B - 1, False)

            @block.vector
            def _(dve):
                for sg in (xn_ready, qk_ready, max_taken, max_placed, att_ready, router_read, logits_read, mask_ready,
                           chosen_x, gT_ready, x_updated):
                    dve.sem_inc(sg.sem, sg.per)
                dve.memset(mneg[:, :, :, :], 0.0).then_inc(stats_ready, 1)
                dve.wait_ge(stats_ready, NT + 1)

                def normalise(n, ch):
                    dve.wait_ge(xn_turned.sem, xn_turned.before(n))
                    for t in range(TT):
                        ins = dve.tensor_scalar(xn[:, t, :], x_all[:, bass.ds(n, 1), t, :].rearrange("p a d -> p (a d)"),
                                                mean[:, bass.ds(n * TT + t, 1)], nrm[:, 0, bass.ds(n * TT + t, 1)],
                                                ALU.subtract, ALU.mult)
                        if t == TT - 1:
                            ins.then_inc(xn_ready.sem, 1)
                        else:
                            ins.then_inc(ch.sem, ch.one())

                def pick(n, l, src, read, ch):
                    dve.tensor_tensor(work[:, :, 0:E0], src, rb_bc[:, l, :].unsqueeze(1).to_broadcast([P, TT, E0]),
                                      ALU.add).then_inc(read.sem, 1)
                    dve.wait_ge(read.sem, read.now(n))
                    first, second = choose(dve, ch, E0, TOP0, BIG)
                    if l == 0:
                        dve.wait_ge(mask_turned.sem, mask_turned.before(n))
                    else:
                        dve.wait_ge(mask_turned.sem, mask_turned.now(n, 1))
                    dve.tensor_tensor(mask[:, :, 0:E0], first, second, ALU.add).then_inc(mask_ready.sem, 1)

                def route(n, ch):
                    dve.wait_ge(v_made.sem, v_made.now(n))
                    pick(n, 0, pb[:, 0:TT * 136].rearrange("p (t c) -> p t c", t=TT)[:, :, D:D + E0], router_read, ch)

                def strips(n):
                    for m, (st, hi, sel) in enumerate(((qst, qhi, C_SELQ), (kst, khi, C_SELK))):
                        dve.wait_ge(qk_high.sem, qk_high.now(n, m + 1))
                        dve.wait_ge(st_made.sem, st_made.before(n))
                        src = scr[:, m, :, :].rearrange("p g (j n) -> p (g j) n", j=2)
                        dve.scalar_tensor_tensor(out=st[:, :, :], in0=src, scalar=cst[:, sel:sel + 1], in1=hi[:, :, :].bitcast(F32),
                                                 op0=ALU.mult, op1=ALU.add).then_inc(qk_ready.sem, 1)

                def turn(i, follows):
                    ch = Steps(dve_turn0, DVE_TURN0, i)

                    def maximum(u):
                        j, gp = u // 2, u % 2
                        dve.wait_ge(scores_made.sem, scores_made.now(i, u + 1))
                        o = mneg[:, :, j, 64 * gp:64 * gp + 64].rearrange("p t (g c) -> p g t c", g=2)[:, :, :, 24]
                        dve.tensor_reduce(o, scr[:, u % 2, :, :].rearrange("p g (t n) -> p g t n", t=TT), AX_X, ALU.max,
                                          negate=True).then_inc(max_taken.sem, 1)

                    def mult_chunk(l, c, src):
                        k = NCH * l + c
                        dve.wait_ge(spread.sem, spread.now(i, k + 1))
                        if c >= 2:
                            dve.wait_ge(chunk_used.sem, chunk_used.now(i, (NCH - 1) * l + c - 1))
                        elif l == 1:
                            dve.wait_ge(moe_made.sem, moe_made.now(i, 1))
                        else:
                            dve.wait_ge(moe_made.sem, moe_made.before(i))
                        dve.tensor_tensor(xm[:, c % 2, :, :], pa[:, 0:2 * S].rearrange("p (e n) -> p e n", e=2),
                                          src[:, :].unsqueeze(1).to_broadcast([P, 2, S]), ALU.mult).then_inc(chosen_x.sem, 1)

                    dve.wait_ge(max_turned.sem, max_turned.before(i))
                    maximum(0)
                    maximum(1)
                    for c in range(NCH):
                        mult_chunk(0, c, xnT)
                        maximum(c + 2)
                    maximum(NCH + 2)
                    maximum(NCH + 3)
                    dve.wait_ge(max_turned.sem, max_turned.now(i))
                    dve.wait_ge(qk_ready.sem, qk_ready.now(i))
                    for a in range(2):
                        ins = dve.tensor_tensor(qst[:, 2 * a:2 * a + 2, :], oT[:, 2 * a:2 * a + 2, :],
                                                qst[:, 2 * a:2 * a + 2, :].bitcast(F32), ALU.add)
                        if a == 0:
                            ins.then_inc(ch.sem, ch.one())
                        else:
                            ins.then_inc(max_placed.sem, 1)

                    dve.wait_ge(logits_made.sem, logits_made.now(i))
                    pick(i, 1, pa[:, 0:TT * E0].rearrange("p (t c) -> p t c", t=TT), logits_read, ch)
                    if follows:
                        normalise(i + 1, ch)
                    for c in range(NCH):
                        mult_chunk(1, c, yT)
                    dve.wait_ge(tanh_ready.sem, tanh_ready.now(i))
                    dve.wait_ge(g_turned.sem, g_turned.before(i))
                    dve.scalar_tensor_tensor(out=gT0[:, :], in0=th0[:, :], scalar=1.0, in1=pb[:, 0:S],
                                             op0=ALU.add, op1=ALU.mult).then_inc(gT_ready.sem, 1)
                    dve.wait_ge(o_turned.sem, o_turned.now(i))
                    oh = psum[:, 4:6, :].rearrange("p t (h c) -> p (t h) c", c=32)
                    dve.reciprocal(rsum[:, :], oh[:, :, HD]).then_inc(ch.sem, ch.one())
                    dve.wait_ge(ch.sem, ch.value())
                    dve.wait_ge(att_turned.sem, att_turned.before(i))
                    dve.tensor_tensor(att[:, :, :].rearrange("p t (h d) -> p (t h) d", d=HD), oh[:, :, 0:HD],
                                      rsum[:, :].unsqueeze(2).to_broadcast([P, TT * H, HD]), ALU.mult).then_inc(att_ready.sem, 1)
                    if follows:
                        route(i + 1, ch)
                        strips(i + 1)
                    dve.wait_ge(s_made.sem, s_made.now(i))
                    dve.wait_ge(g_turned.sem, g_turned.now(i))
                    dve.tensor_tensor(sat[:, :, :], psum[:, 5, S:2 * S].rearrange("p (t d) -> p t d", t=TT),
                                      bu_bc[:, :].unsqueeze(1).to_broadcast([P, TT, D]), ALU.add).then_inc(ch.sem, ch.one())
                    dve.wait_ge(ch.sem, ch.value())
                    dve.scalar_tensor_tensor(out=zat[:, :, :], in0=sat[:, :, :], scalar=0.5,
                                             in1=psum[:, 5, 0:S].rearrange("p (t d) -> p t d", t=TT), op0=ALU.mult, op1=ALU.mult).then_inc(ch.sem, ch.one())
                    dve.wait_ge(ch.sem, ch.value())
                    xs = x_all[:, bass.ds(i, 1), :, :].rearrange("p a t d -> p (a t) d")
                    dve.tensor_tensor(xs, xs, zat[:, :, :], ALU.add).then_inc(x_updated.sem, 1)
                    dve.wait_ge(x_updated.sem, x_updated.now(i))
                    dve.sem_inc(x_waits_met, 1)
                    for t in range(TT):
                        dve.bn_stats(stats[:, bass.ds(i * TT + t, 1), :].rearrange("p a s -> p (a s)"),
                                     x_all[:, bass.ds(i, 1), t, :].rearrange("p a d -> p (a d)")).then_inc(stats_ready, 1)
                    if follows:
                        ch.end()

                first = Steps(dve_front)
                normalise(0, first)
                route(0, first)
                strips(0)
                with dve.Fori(0, B - 1) as i:
                    turn(i, True)
                turn(B - 1, False)
        big.close()

        with nc.Block() as block:
            @block.vector
            def _(dve):
                ch = Steps(dve_mid)
                dve.wait_ge(stats_ready, 2 * NT + 1)
                layer_stats(dve, ch, True)

        pro = sb("pro", [P, TT, 3 * D])
        gl = sb("gl", [P, TT, 3 * H])
        th1 = sb("th1", [P, TT, 3 * H])
        thx = sb("thx", [P, TT, 2 * H, HD])
        th2 = sb("th2", [P, TT, H])
        sq = sb("sq", [P, TT, 2 * D])
        ms = sb("ms", [P, 2 * TT * H])
        rinv = sb("rinv", [P, 2 * TT * H])
        scratch = sb("scratch", [P, 2 * TT * H])
        kq = sb("kq", [P, TT, 2 * D])
        kmv = sb("kmv", [P, TT, D])
        kqT = sb("kqT", [P, 2, S])
        aT = sb("aT", [P, NJ, S])
        a1 = sb("a1", [P, TT, H * HID])
        pre = sb("pre", [P, TT, H * HID])
        pdf = sb("pdf", [P, TT, H * HID])
        inv = sb("inv", [P, TT, H * HID])
        gg = sb("gg", [P, TT, H * HID])
        dh1 = sb("dh1", [P, TT, H * HID])
        hT = sb("hT", [P, S])
        h1 = sb("h1", [P, TT, D])
        h1sq = sb("h1sq", [P, TT, D])
        hn = sb("hn", [P, TT, D])
        dp = sb("dp", [P, TT, D])
        tmp = sb("tmp", [P, TT, D])
        dy = sb("dy", [P, TT * H])
        dh = sb("dh", [P, TT, D])
        dhT = sb("dhT", [P, S])
        gm = sb("gm", [P, NW])
        gsq = sb("gsq", [P, NW])
        gsum = sb("gsum", [P, 1])
        sums = sb("sums", [P, 2])
        cf = sb("cf", [P, 8])
        nw = sb("nw", [P, NW])
        nwok = sb("nwok", [P, NW], I32)
        nwf = sb("nwf", [P, NW])
        nw1 = sb("nw1", [P, P])
        h2 = sb("h2", [P, TT, D])
        h2ok = sb("h2ok", [P, TT, D], I32)
        hz = sb("hz", [P, TT, D])
        y2 = sb("y2", [P, TT, D])
        actT = sb("actT", [P, NC1, S])
        rld = sb("rld", [P, TT, E1])
        rex = sb("rex", [P, TT, E1])
        rsm = sb("rsm", [P, TT])
        prob = sb("prob", [P, TT, E1])
        thf = sb("thf", [P, S])
        gT1 = sb("gT1", [P, S])

        px = psum[:, 0:2, :]
        pt, pf = psum[:, 4, :], psum[:, 5, :]
        pg = psum[:, 6:8, :].rearrange("p b n -> p (b n)")
        G0, G1, GS, GQ, GH = 0, 512, 640, 642, 768
        NUP = (NC1 + 1) // 2
        RING = NUP + 4
        BD = P // NJ

        def sig(name, per=1):
            return Signal(sem(name), per)

        xn1_ready, xn1_turned, xn1T_ready = sig("xn1_ready"), sig("xn1_turned"), sig("xn1T_ready")
        pro_made, pro_read, pro_ready = sig("pro_made"), sig("pro_read"), sig("pro_ready", TT)
        gl_ready = sig("gl_ready", TT)
        th1_ready, sq_ready = sig("th1_ready"), sig("sq_ready")
        ring_made, ring_read = sig("ring_made", RING), sig("ring_read", RING)
        kq_ready, kq_turned, kqT_ready = sig("kq_ready"), sig("kq_turned"), sig("kqT_ready")
        thx_ready, kmv_ready = sig("thx_ready"), sig("kmv_ready")
        pre_made, pre_read, a1_ready = sig("pre_made", TT), sig("pre_read", TT), sig("a1_ready", TT)
        pre_copied = sig("pre_copied", TT)
        rex_ready, pdf_ready, pm_ready = sig("rex_ready"), sig("pdf_ready", TT), sig("pm_ready", TT)
        gates_ready, gates_turned, gatesT_ready = sig("gates_ready"), sig("gates_turned"), sig("gatesT_ready")
        NGC = (NC1 - 1) // 2
        gates_spread, gated = sig("gates_spread", NGC), sig("gated", NGC)
        h1T_made, h1T_copied, h1_turned = sig("h1T_made"), sig("h1T_copied"), sig("h1_turned")
        h1_copied, h1_ready = sig("h1_copied"), sig("h1_ready")
        dh_ready, dh_turned, dhT_ready = sig("dh_ready"), sig("dh_turned"), sig("dhT_ready")
        back_made, dh1_ready = sig("back_made", TT), sig("dh1_ready", TT)
        g1_made, g0_made, gm_ready = sig("g1_made"), sig("g0_made"), sig("gm_ready")
        gsum_ready, gtotal_made = sig("gsum_ready"), sig("gtotal_made")
        nwf_set, nw_ready, nw_turned, nw1_ready = sig("nwf_set"), sig("nw_ready"), sig("nw_turned"), sig("nw1_ready")
        h2T_made, h2T_copied, h2_turned, h2_ready = sig("h2T_made"), sig("h2T_copied"), sig("h2_turned"), sig("h2_ready")
        hz_set = sig("hz_set")
        ffn_made, thf_ready, gT1_ready, gf_turned = sig("ffn_made"), sig("thf_ready"), sig("gT1_ready"), sig("gf_turned")
        y_ready = sig("y_ready")
        y_stored = sem("y_stored")
        dve_turn1 = sem("dve_turn1")
        dve_waits_met, pool_waits_met = sem("dve_waits_met"), sem("pool_waits_met")

        with nc.Block() as block:
            @block.sync
            def _(sp):
                with sp.Fori(0, B) as i:
                    sp.wait_ge(y_ready.sem, y_ready.now(i))
                    sp.dma_start(out.rearrange("b (t p) d -> b p t d", p=P)[bass.ds(i, 1)].rearrange("a p t d -> (a p) t d"),
                                 x_all[:, bass.ds(i, 1), :, :].rearrange("p a t d -> p (a t) d")).then_inc(y_stored, 16)
                sp.wait_ge(y_stored, 16 * B)

            @block.gpsimd
            def _(pool):
                for sg in (thx_ready, kmv_ready, pm_ready, nwf_set, hz_set):
                    pool.sem_inc(sg.sem, sg.per)
                with pool.Fori(0, B) as i:
                    pool.wait_ge(h2T_made.sem, h2T_made.before(i))
                    pool.sem_inc(pool_waits_met, 1)
                    pool.tensor_copy(nwf[:, :], w_bd[:, :]).then_inc(nwf_set.sem, 1)
                    pool.wait_ge(y_ready.sem, y_ready.before(i))
                    pool.sem_inc(pool_waits_met, 1)
                    pool.memset(hz[:, :, :], 0.0).then_inc(hz_set.sem, 1)
                    pool.wait_ge(th1_ready.sem, th1_ready.now(i))
                    pool.wait_ge(g1_made.sem, g1_made.before(i))
                    pool.sem_inc(pool_waits_met, 1)
                    pool.tensor_copy(thx[:, :, :, :], th1[:, :, 0:2 * H].unsqueeze(3).to_broadcast([P, TT, 2 * H, HD])
                                     ).then_inc(thx_ready.sem, 1)
                    pool.wait_ge(kq_ready.sem, kq_ready.now(i))
                    pool.wait_ge(dh_ready.sem, dh_ready.before(i))
                    pool.tensor_tensor(kmv[:, :, :], kq[:, :, 0:D], pro[:, :, 2 * D:3 * D], ALU.subtract).then_inc(kmv_ready.sem, 1)
                    for t in range(TT):
                        pool.wait_ge(pdf_ready.sem, pdf_ready.now(i, t + 1))
                        pool.tensor_tensor(pdf[:, t, :], pdf[:, t, :], pre[:, t, :], ALU.mult).then_inc(pm_ready.sem, 1)

            @block.tensor
            def _(pe):
                for sg in (xn1_turned, pro_made, ring_made, kq_turned, pre_made, gates_turned, gates_spread, h1T_made, h1_turned,
                           dh_turned, back_made, g1_made, g0_made, gtotal_made, nw_turned, h2T_made, h2_turned, ffn_made,
                           gf_turned):
                    pe.sem_inc(sg.sem, sg.per)
                with pe.Fori(0, B) as i:
                    pe.wait_ge(xn1_ready.sem, xn1_ready.now(i))
                    pe.wait_ge(h2_ready.sem, h2_ready.before(i))
                    for t in range(TT):
                        last = nc.tensor.transpose(pt[:, t * P:t * P + P], xn[:, t, :], ident)
                    last.then_inc(xn1_turned.sem, 1)
                    pe.wait_ge(xn1T_ready.sem, xn1T_ready.now(i))
                    pe.wait_ge(dh1_ready.sem, dh1_ready.before(i))
                    for t in range(TT):
                        last = nc.tensor.matmul(px[:, t, 0:NPRO], xnT[:, t * P:t * P + P], w_pro[:, :], start=True, stop=True)
                    last.then_inc(pro_made.sem, 1)
                    for n in range(NUP):
                        if n < 2:
                            pe.wait_ge(ring_read.sem, ring_read.before(i))
                        else:
                            pe.wait_ge(ring_read.sem, ring_read.now(i, n - 1))
                        for c in range(2 * n, min(2 * n + 2, NC1)):
                            last = nc.tensor.matmul(psum[:, 2 + n % 2, c % 2 * S:c % 2 * S + S], wT[:, T_UP + c, :], xnT[:, :],
                                                    start=True, stop=True)
                        last.then_inc(ring_made.sem, 1)
                    pe.wait_ge(kq_ready.sem, kq_ready.now(i))
                    for m in range(2):
                        for t in range(TT):
                            last = nc.tensor.transpose(pt[:, m * S + t * P:m * S + t * P + P], kq[:, t, m * D:m * D + D], ident)
                    last.then_inc(kq_turned.sem, 1)

                    def hidden(m, w, n0):
                        for n in range(n0, n0 + 2):
                            if n0 == NUP:
                                pe.wait_ge(ring_read.sem, ring_read.now(i, n - 1))
                            for c in range(2 * (n - n0), 2 * (n - n0) + 2):
                                last = nc.tensor.matmul(psum[:, 2 + n % 2, c % 2 * S:c % 2 * S + S], w[:, c * P:c * P + P],
                                                        kqT[:, m, :], start=True, stop=True)
                            last.then_inc(ring_made.sem, 1)

                    pe.wait_ge(kqT_ready.sem, kqT_ready.now(i))
                    hidden(0, w_bd, NUP)
                    pe.wait_ge(pro_read.sem, pro_read.now(i))
                    for t in range(TT):
                        nc.tensor.matmul(px[:, t, :], kqT[:, 0, t * P:t * P + P], w_bd[:, 0:H * HID], start=True, stop=True
                                         ).then_inc(pre_made.sem, 1)
                    pe.wait_ge(ring_read.sem, ring_read.now(i, NUP + 2))
                    pe.wait_ge(h2T_copied.sem, h2T_copied.before(i))
                    for c in range(NJ):
                        last = nc.tensor.matmul(pg[BD * c:BD * c + BD, GH:GH + S], w1_bd[:, :], aT[:, c, :],
                                                start=True, stop=True)
                    last.then_inc(h1T_made.sem, 1)
                    pe.wait_ge(h1T_copied.sem, h1T_copied.now(i))
                    for t in range(TT):
                        last = nc.tensor.transpose(pt[:, t * P:t * P + P], hT[:, t * P:t * P + P], ident)
                    last.then_inc(h1_turned.sem, 1)
                    pe.wait_ge(dh_ready.sem, dh_ready.now(i))
                    pe.wait_ge(h1_ready.sem, h1_ready.now(i))
                    for t in range(TT):
                        last = nc.tensor.transpose(pt[:, t * P:t * P + P], dh[:, t, :], ident)
                    last.then_inc(dh_turned.sem, 1)
                    pe.wait_ge(dhT_ready.sem, dhT_ready.now(i))
                    pe.wait_ge(pre_read.sem, pre_read.now(i))
                    for t in range(TT):
                        nc.tensor.matmul(px[:, t, :], dhT[:, t * P:t * P + P], w1t_bd[:, :], start=True, stop=True
                                         ).then_inc(back_made.sem, 1)
                    for c in range(NJ):
                        for t in range(TT):
                            nc.tensor.matmul(pg[BD * c:BD * c + BD, G1:G1 + P], dh[:, t, BD * c:BD * c + BD],
                                             a1[:, t, P * c:P * c + P], start=(t == 0), stop=(t == TT - 1))
                    pe.wait_ge(thx_ready.sem, thx_ready.now(i))
                    for m in range(2):
                        for t in range(TT):
                            last = nc.tensor.matmul(pg[:, GS + m:GS + m + 1],
                                                    thx[:, t, m * H:m * H + H, :].rearrange("p h d -> p (h d)"),
                                                    cst[:, C_ONE:C_ONE + 1], start=(t == 0), stop=(t == TT - 1))
                    last.then_inc(g1_made.sem, 1)
                    pe.wait_ge(gates_ready.sem, gates_ready.now(i))
                    for t in range(TT):
                        last = nc.tensor.transpose(pt[0:2 * E1, t * P:t * P + P], mask[:, t, :], ident)
                    last.then_inc(gates_turned.sem, 1)

                    def spread_gates(c):
                        if c >= 2:
                            pe.wait_ge(gated.sem, gated.now(i, c - 1))
                        for e2 in range(2):
                            last = nc.tensor.matmul(psum[:, 2 + c % 2, e2 * S:e2 * S + S], sel1[:, 2 * c + e2, :], maskT[:, :],
                                                    start=True, stop=True)
                        last.then_inc(gates_spread.sem, 1)

                    pe.wait_ge(gatesT_ready.sem, gatesT_ready.now(i))
                    spread_gates(0)
                    spread_gates(1)
                    pe.wait_ge(dh1_ready.sem, dh1_ready.now(i))
                    pe.wait_ge(gm_ready.sem, gm_ready.before(i))
                    for t in range(TT):
                        last = nc.tensor.matmul(pg[:, G0:G0 + H * HID], kq[:, t, 0:D], dh1[:, t, :],
                                                start=(t == 0), stop=(t == TT - 1))
                    last.then_inc(g0_made.sem, 1)
                    spread_gates(2)
                    spread_gates(3)
                    pe.wait_ge(gsum_ready.sem, gsum_ready.now(i))
                    nc.tensor.matmul(pg[:, GQ:GQ + 1], cst[:, C_HEAD:C_HEAD + P], gsum[:, :], start=True, stop=True
                                     ).then_inc(gtotal_made.sem, 1)
                    pe.wait_ge(y_ready.sem, y_ready.before(i))
                    for c in range(NC1):
                        if c >= 1:
                            pe.wait_ge(gated.sem, gated.now(i, (c + 1) // 2))
                        last = nc.tensor.matmul(pf[:, 0:S], wT[:, T_DOWN + c, :], actT[:, c, :], start=(c == 0), stop=(c == NC1 - 1))
                    last.then_inc(ffn_made.sem, 1)
                    pe.wait_ge(nw_ready.sem, nw_ready.now(i))
                    nc.tensor.transpose(pt[:, 0:P], nwf[:, H * HID:NW], ident).then_inc(nw_turned.sem, 1)
                    hidden(1, nwf, NUP + 2)
                    pe.wait_ge(nw1_ready.sem, nw1_ready.now(i))
                    pe.wait_ge(ring_read.sem, ring_read.now(i, RING))
                    for c in range(NJ):
                        last = nc.tensor.matmul(pg[BD * c:BD * c + BD, GH:GH + S], nw1[:, BD * c:BD * c + BD], aT[:, c, :],
                                                start=True, stop=True)
                    last.then_inc(h2T_made.sem, 1)
                    pe.wait_ge(gT1_ready.sem, gT1_ready.now(i))
                    for t in range(TT):
                        last = nc.tensor.transpose(pf[:, S + t * P:S + t * P + P], gT1[:, t * P:t * P + P], ident)
                    last.then_inc(gf_turned.sem, 1)
                    pe.wait_ge(h2T_copied.sem, h2T_copied.now(i))
                    for t in range(TT):
                        last = nc.tensor.transpose(pt[:, t * P:t * P + P], hT[:, t * P:t * P + P], ident)
                    last.then_inc(h2_turned.sem, 1)

            @block.scalar
            def _(act):
                for sg in (xn1T_ready, th1_ready, sq_ready, ring_read, kqT_ready, a1_ready, pre_copied, pre_read, rex_ready,
                           pdf_ready, gatesT_ready, h1T_copied, h1_copied, h1_ready, dhT_ready, gsum_ready, nw1_ready,
                           h2T_copied, h2_ready, thf_ready):
                    act.sem_inc(sg.sem, sg.per)
                with act.Fori(0, B) as i:
                    act.wait_ge(xn1_turned.sem, xn1_turned.now(i))
                    act.wait_ge(ring_made.sem, ring_made.before(i))
                    nc.scalar.activation(xnT[:, :], pt[:, 0:S], ACT.Copy).then_inc(xn1T_ready.sem, 1)

                    def up(n):
                        act.wait_ge(ring_made.sem, ring_made.now(i, n + 1))
                        if n == 0:
                            act.wait_ge(ffn_made.sem, ffn_made.before(i))
                        m = min(2, NC1 - 2 * n)
                        nc.scalar.activation(actT[:, 2 * n:2 * n + m, :].rearrange("p c n -> p (c n)"),
                                             psum[:, 2 + n % 2, 0:m * S], ACT.Gelu).then_inc(ring_read.sem, 1)

                    def hidden(n):
                        act.wait_ge(ring_made.sem, ring_made.now(i, n + 1))
                        if n == NUP:
                            act.wait_ge(h2T_made.sem, h2T_made.before(i))
                        if n == NUP + 2:
                            act.wait_ge(h1T_made.sem, h1T_made.now(i))
                        a = (n - NUP) % 2
                        nc.scalar.activation(aT[:, 2 * a:2 * a + 2, :].rearrange("p c n -> p (c n)"), psum[:, 2 + n % 2, :],
                                             ACT.Gelu).then_inc(ring_read.sem, 1)

                    up(0)
                    up(1)
                    act.wait_ge(gl_ready.sem, gl_ready.now(i))
                    act.wait_ge(thx_ready.sem, thx_ready.before(i))
                    act.wait_ge(dh_ready.sem, dh_ready.before(i))
                    nc.scalar.activation(th1[:, :, :], gl[:, :, :], ACT.Tanh, scale=0.5).then_inc(th1_ready.sem, 1)
                    act.wait_ge(pro_ready.sem, pro_ready.now(i))
                    nc.scalar.activation(sq[:, :, :], pro[:, :, 0:2 * D], ACT.Square).then_inc(sq_ready.sem, 1)
                    for n in range(2, NUP):
                        up(n)
                    act.wait_ge(kq_turned.sem, kq_turned.now(i))
                    nc.scalar.activation(kqT[:, :, :].rearrange("p m n -> p (m n)"), pt, ACT.Copy).then_inc(kqT_ready.sem, 1)
                    hidden(NUP)
                    hidden(NUP + 1)
                    act.wait_ge(dh1_ready.sem, dh1_ready.before(i))
                    for t in range(TT):
                        act.wait_ge(pre_made.sem, pre_made.now(i, t + 1))
                        act.wait_ge(g1_made.sem, g1_made.before(i))
                        nc.scalar.activation(a1[:, t, :], px[:, t, :], ACT.Gelu).then_inc(a1_ready.sem, 1)
                        nc.scalar.activation(pre[:, t, :], px[:, t, :], ACT.Copy).then_inc(pre_copied.sem, 1)
                        nc.scalar.activation(pdf[:, t, :], px[:, t, :], ACT.Square).then_inc(pre_read.sem, 1)
                    act.wait_ge(h1T_made.sem, h1T_made.now(i))
                    act.wait_ge(h2_turned.sem, h2_turned.before(i))
                    nc.scalar.activation(hT[:, :], pg[:, GH:GH + S], ACT.Copy).then_inc(h1T_copied.sem, 1)
                    act.wait_ge(h1_turned.sem, h1_turned.now(i))
                    nc.scalar.activation(h1[:, :, :].rearrange("p t d -> p (t d)"), pt[:, 0:S], ACT.Copy).then_inc(h1_copied.sem, 1)
                    nc.scalar.activation(h1sq[:, :, :].rearrange("p t d -> p (t d)"), pt[:, 0:S], ACT.Square).then_inc(h1_ready.sem, 1)
                    act.wait_ge(pro_read.sem, pro_read.now(i))
                    act.wait_ge(gates_ready.sem, gates_ready.before(i))
                    nc.scalar.activation(rex[:, :, :], rld[:, :, :], ACT.Exp).then_inc(rex_ready.sem, 1)
                    act.wait_ge(pre_read.sem, pre_read.now(i))
                    for t in range(TT):
                        nc.scalar.activation(pdf[:, t, :], pdf[:, t, :], ACT.Exp, scale=-0.5).then_inc(pdf_ready.sem, 1)
                    act.wait_ge(dh_turned.sem, dh_turned.now(i))
                    act.wait_ge(back_made.sem, back_made.before(i))
                    nc.scalar.activation(dhT[:, :], pt[:, 0:S], ACT.Copy).then_inc(dhT_ready.sem, 1)
                    act.wait_ge(gates_turned.sem, gates_turned.now(i))
                    act.wait_ge(gates_spread.sem, gates_spread.before(i))
                    nc.scalar.activation(maskT[:, :], pt[0:2 * E1, 0:S], ACT.Copy).then_inc(gatesT_ready.sem, 1)
                    act.wait_ge(gm_ready.sem, gm_ready.now(i))
                    act.wait_ge(gtotal_made.sem, gtotal_made.before(i))
                    nc.scalar.activation(gsq[:, :], gm[:, :], ACT.Square, accum_out=gsum[:, :]).then_inc(gsum_ready.sem, 1)
                    act.wait_ge(ffn_made.sem, ffn_made.now(i))
                    act.wait_ge(gT1_ready.sem, gT1_ready.before(i))
                    nc.scalar.activation(thf[:, :], pf[:, 0:S], ACT.Tanh, scale=0.5).then_inc(thf_ready.sem, 1)
                    act.wait_ge(nw_turned.sem, nw_turned.now(i))
                    act.wait_ge(h2T_made.sem, h2T_made.before(i))
                    nc.scalar.activation(nw1[:, :], pt[:, 0:P], ACT.Copy).then_inc(nw1_ready.sem, 1)
                    hidden(NUP + 2)
                    hidden(NUP + 3)
                    act.wait_ge(h2T_made.sem, h2T_made.now(i))
                    nc.scalar.activation(hT[:, :], pg[:, GH:GH + S], ACT.Copy).then_inc(h2T_copied.sem, 1)
                    act.wait_ge(h2_turned.sem, h2_turned.now(i))
                    act.wait_ge(y_ready.sem, y_ready.before(i))
                    nc.scalar.activation(h2[:, :, :].rearrange("p t d -> p (t d)"), pt[:, 0:S], ACT.Copy).then_inc(h2_ready.sem, 1)

            @block.vector
            def _(dve):
                for sg in (xn1_ready, pro_ready, gl_ready, pro_read, kq_ready, gates_ready, gated, dh_ready, dh1_ready, gm_ready,
                           nw_ready, gT1_ready, y_ready):
                    dve.sem_inc(sg.sem, sg.per)

                def heads(ap):
                    return ap.rearrange("p t (h d) -> p (t h) d", d=HD)

                def per_head(ap):
                    return ap.unsqueeze(2).to_broadcast([P, ap.shape[1], HD])

                with dve.Fori(0, B) as i:
                    ch = Steps(dve_turn1, DVE_TURN1, i)
                    dve.wait_ge(xn1_turned.sem, xn1_turned.before(i))
                    for t in range(TT):
                        ins = dve.tensor_scalar(xn[:, t, :], x_all[:, bass.ds(i, 1), t, :].rearrange("p a d -> p (a d)"),
                                                mean[:, bass.ds(i * TT + t, 1)], nrm[:, 0, bass.ds(i * TT + t, 1)],
                                                ALU.subtract, ALU.mult)
                        if t == TT - 1:
                            ins.then_inc(xn1_ready.sem, 1)
                        else:
                            ins.then_inc(ch.sem, ch.one())
                    dve.wait_ge(pro_made.sem, pro_made.now(i))
                    dve.wait_ge(kmv_ready.sem, kmv_ready.before(i))
                    for t in range(TT):
                        rms = nrm[:, 1, bass.ds(i * TT + t, 1)]
                        dve.tensor_scalar(pro[:, t, :], px[:, t, 0:3 * D], rms, None, ALU.mult).then_inc(pro_ready.sem, 1)
                        dve.scalar_tensor_tensor(out=gl[:, t, :], in0=px[:, t, 3 * D:3 * D + 3 * H], scalar=rms, in1=gate_b[:, :],
                                                 op0=ALU.mult, op1=ALU.add).then_inc(gl_ready.sem, 1)
                    rl = px[:, :, 3 * D + 3 * H:NPRO]
                    dve.tensor_reduce(top[:, :], rl, AX_X, ALU.max).then_inc(ch.sem, ch.one())
                    dve.wait_ge(ch.sem, ch.value())
                    dve.wait_ge(rex_ready.sem, rex_ready.before(i))
                    dve.tensor_tensor(rld[:, :, :], rl, top[:, :].unsqueeze(2).to_broadcast([P, TT, E1]), ALU.subtract
                                      ).then_inc(pro_read.sem, 1)
                    dve.wait_ge(sq_ready.sem, sq_ready.now(i))
                    dve.tensor_reduce(ms[:, :], sq[:, :, :].rearrange("p t (h d) -> p (t h) d", d=HD), AX_X, ALU.add).then_inc(ch.sem, ch.one())
                    dve.wait_ge(ch.sem, ch.value())
                    dve.tensor_scalar(ms[:, :], ms[:, :], 1.0 / HD, RMS_EPS, ALU.mult, ALU.add).then_inc(ch.sem, ch.one())
                    dve.wait_ge(ch.sem, ch.value())
                    newton(dve, ch, rinv[:, :], ms[:, :], scratch[:, :], 2 * TT * H)
                    dve.wait_ge(g0_made.sem, g0_made.before(i))
                    dve.wait_ge(y_ready.sem, y_ready.before(i))
                    dve.tensor_tensor(kq[:, :, :].rearrange("p t (a h d) -> p t (a h) d", h=H, d=HD),
                                      pro[:, :, 0:2 * D].rearrange("p t (a h d) -> p t (a h) d", h=H, d=HD),
                                      rinv[:, :].rearrange("p (t h) -> p t h", t=TT).unsqueeze(3).to_broadcast([P, TT, 2 * H, HD]),
                                      ALU.mult).then_inc(ch.sem, ch.one())
                    dve.wait_ge(ch.sem, ch.value())
                    dve.tensor_tensor(kq[:, :, :], kq[:, :, :],
                                      knq_bc[:, :, :, :].rearrange("p a h d -> p (a h d)").unsqueeze(1).to_broadcast([P, TT, 2 * D]),
                                      ALU.mult).then_inc(kq_ready.sem, 1)
                    dve.wait_ge(th1_ready.sem, th1_ready.now(i))
                    dve.tensor_scalar(th2[:, :, :], th1[:, :, 2 * H:3 * H], MAX_LR, MAX_LR, ALU.mult, ALU.add).then_inc(ch.sem, ch.one())
                    dve.wait_ge(ch.sem, ch.value())

                    def unit(x_sq):
                        dve.tensor_reduce(ms[:, 0:TT * H], heads(x_sq), AX_X, ALU.add).then_inc(ch.sem, ch.one())
                        dve.wait_ge(ch.sem, ch.value())
                        dve.tensor_scalar(ms[:, 0:TT * H], ms[:, 0:TT * H], 1.0 / HD, PF_EPS, ALU.mult, ALU.add).then_inc(ch.sem, ch.one())
                        dve.wait_ge(ch.sem, ch.value())
                        newton(dve, ch, rinv[:, 0:TT * H], ms[:, 0:TT * H], scratch[:, 0:TT * H], TT * H)
                        return per_head(rinv[:, 0:TT * H])

                    dve.wait_ge(h1_ready.sem, h1_ready.now(i))
                    dve.wait_ge(kmv_ready.sem, kmv_ready.now(i))
                    r = unit(h1sq[:, :, :])
                    dve.tensor_tensor(heads(hn[:, :, :]), heads(h1[:, :, :]), r, ALU.mult).then_inc(ch.sem, ch.one())
                    dve.wait_ge(ch.sem, ch.value())
                    dve.tensor_tensor(dp[:, :, :], hn[:, :, :], kmv[:, :, :], ALU.add).then_inc(ch.sem, ch.one())
                    dve.wait_ge(ch.sem, ch.value())
                    dve.tensor_tensor(heads(dp[:, :, :]), heads(dp[:, :, :]),
                                      per_head(th2[:, :, :].rearrange("p t h -> p (t h)")), ALU.mult).then_inc(ch.sem, ch.one())
                    dve.wait_ge(ch.sem, ch.value())
                    dve.tensor_tensor(tmp[:, :, :], dp[:, :, :], hn[:, :, :], ALU.mult).then_inc(ch.sem, ch.one())
                    dve.wait_ge(ch.sem, ch.value())
                    dve.tensor_reduce(dy[:, :], heads(tmp[:, :, :]), AX_X, ALU.add).then_inc(ch.sem, ch.one())
                    dve.wait_ge(ch.sem, ch.value())
                    dve.tensor_tensor(heads(tmp[:, :, :]), heads(hn[:, :, :]), per_head(dy[:, :]), ALU.mult).then_inc(ch.sem, ch.one())
                    dve.wait_ge(ch.sem, ch.value())
                    dve.scalar_tensor_tensor(out=dp[:, :, :], in0=tmp[:, :, :], scalar=-1.0 / HD, in1=dp[:, :, :],
                                             op0=ALU.mult, op1=ALU.add).then_inc(ch.sem, ch.one())
                    dve.wait_ge(ch.sem, ch.value())
                    dve.wait_ge(g1_made.sem, g1_made.before(i))
                    dve.tensor_tensor(heads(dh[:, :, :]), heads(dp[:, :, :]), r, ALU.mult).then_inc(dh_ready.sem, 1)
                    dve.wait_ge(rex_ready.sem, rex_ready.now(i))
                    dve.tensor_reduce(rsm[:, :], rex[:, :, :], AX_X, ALU.add).then_inc(ch.sem, ch.one())
                    dve.wait_ge(ch.sem, ch.value())
                    dve.reciprocal(rsm[:, :], rsm[:, :]).then_inc(ch.sem, ch.one())
                    dve.wait_ge(ch.sem, ch.value())
                    dve.tensor_tensor(prob[:, :, :], rex[:, :, :], rsm[:, :].unsqueeze(2).to_broadcast([P, TT, E1]), ALU.mult).then_inc(ch.sem, ch.one())
                    dve.wait_ge(ch.sem, ch.value())
                    dve.tensor_copy(work[:, :, :], prob[:, :, :]).then_inc(ch.sem, ch.one())
                    dve.wait_ge(ch.sem, ch.value())
                    others, fourth = choose(dve, ch, E1, TOP1, 4.0)
                    dve.tensor_tensor(others, others, fourth, ALU.add).then_inc(ch.sem, ch.one())
                    dve.wait_ge(ch.sem, ch.value())
                    dve.tensor_tensor(prob[:, :, :], prob[:, :, :], others, ALU.mult).then_inc(ch.sem, ch.one())
                    dve.wait_ge(ch.sem, ch.value())
                    dve.wait_ge(gates_turned.sem, gates_turned.before(i))
                    dve.tensor_copy(mask[:, :, 0:E1].bitcast(F32R), prob[:, :, :]).then_inc(ch.sem, ch.one())
                    dve.wait_ge(ch.sem, ch.value())
                    dve.tensor_tensor(mask[:, :, E1:2 * E1], prob[:, :, :], mask[:, :, 0:E1], ALU.subtract).then_inc(gates_ready.sem, 1)
                    dve.wait_ge(g0_made.sem, g0_made.before(i))
                    for t in range(TT):
                        dve.wait_ge(pre_copied.sem, pre_copied.now(i, t + 1))
                        dve.scalar_tensor_tensor(out=inv[:, t, :], in0=pre[:, t, :], scalar=0.0, in1=pre[:, t, :],
                                                 op0=ALU.is_equal, op1=ALU.add).then_inc(ch.sem, ch.one())
                        dve.wait_ge(ch.sem, ch.value())
                        dve.reciprocal(inv[:, t, :], inv[:, t, :]).then_inc(ch.sem, ch.one())
                        dve.wait_ge(a1_ready.sem, a1_ready.now(i, t + 1))
                        dve.scalar_tensor_tensor(out=gg[:, t, :], in0=pre[:, t, :], scalar=-0.5, in1=a1[:, t, :],
                                                 op0=ALU.mult, op1=ALU.add).then_inc(ch.sem, ch.one())
                        dve.wait_ge(ch.sem, ch.value())
                        dve.tensor_tensor(gg[:, t, :], gg[:, t, :], inv[:, t, :], ALU.mult).then_inc(ch.sem, ch.one())
                        dve.wait_ge(ch.sem, ch.value())
                        dve.wait_ge(pm_ready.sem, pm_ready.now(i, t + 1))
                        dve.scalar_tensor_tensor(out=gg[:, t, :], in0=pdf[:, t, :], scalar=0.3989422804014327,
                                                 in1=gg[:, t, :], op0=ALU.mult, op1=ALU.add).then_inc(ch.sem, ch.one())
                        dve.wait_ge(ch.sem, ch.value())
                        dve.wait_ge(back_made.sem, back_made.now(i, t + 1))
                        dve.scalar_tensor_tensor(out=dh1[:, t, :], in0=gg[:, t, :], scalar=0.5, in1=px[:, t, :],
                                                 op0=ALU.add, op1=ALU.mult).then_inc(dh1_ready.sem, 1)

                    def gate(c):
                        dve.wait_ge(gates_spread.sem, gates_spread.now(i, c + 1))
                        a = actT[:, 1 + 2 * c:3 + 2 * c, :].rearrange("p c n -> p (c n)")
                        dve.tensor_tensor(a, psum[:, 2 + c % 2, :], a, ALU.mult).then_inc(gated.sem, 1)

                    dve.wait_ge(ring_read.sem, ring_read.now(i, NUP))
                    gate(0)
                    gate(1)
                    dve.wait_ge(g0_made.sem, g0_made.now(i))
                    dve.wait_ge(g1_made.sem, g1_made.now(i))
                    dve.wait_ge(gsum_ready.sem, gsum_ready.before(i))
                    dve.tensor_copy(sums[:, :], pg[:, GS:GS + 2]).then_inc(ch.sem, ch.one())
                    dve.tensor_tensor(gm[:, :], pg[:, 0:NW], cst[:, C_BD0:C_BD0 + NW], ALU.mult).then_inc(gm_ready.sem, 1)
                    gate(2)
                    gate(3)
                    dve.wait_ge(gtotal_made.sem, gtotal_made.now(i))
                    total, root, factor, keep_w, momentum, t1 = (cf[:, k:k + 1] for k in range(6))
                    dve.tensor_copy(total, pg[:, GQ:GQ + 1]).then_inc(ch.sem, ch.one())
                    dve.wait_ge(ch.sem, ch.value())
                    newton(dve, ch, root, total, t1, 1)
                    dve.tensor_tensor(root, root, total, ALU.mult).then_inc(ch.sem, ch.one())
                    dve.wait_ge(ch.sem, ch.value())
                    dve.tensor_scalar(root, root, 1e-6, None, ALU.add).then_inc(ch.sem, ch.one())
                    dve.wait_ge(ch.sem, ch.value())
                    dve.reciprocal(root, root).then_inc(ch.sem, ch.one())
                    dve.wait_ge(ch.sem, ch.value())
                    dve.tensor_scalar(factor, root, CLIP, 1.0, ALU.mult, ALU.min).then_inc(ch.sem, ch.one())
                    dve.wait_ge(ch.sem, ch.value())
                    dve.tensor_scalar(factor, factor, -1.0, None, ALU.mult).then_inc(ch.sem, ch.one())
                    dve.tensor_scalar(keep_w, sums[:, 0:1], -0.5 / S, 0.5, ALU.mult, ALU.add).then_inc(ch.sem, ch.one())
                    dve.tensor_scalar(momentum, sums[:, 1:2], 0.5 / S, 0.5, ALU.mult, ALU.add).then_inc(ch.sem, ch.one())
                    dve.wait_ge(ch.sem, ch.value())
                    dve.tensor_scalar(momentum, momentum, 0.0, None, ALU.mult).then_inc(ch.sem, ch.one())
                    dve.wait_ge(ch.sem, ch.value())
                    dve.tensor_scalar(gm[:, :], gm[:, :], factor, momentum, ALU.mult, ALU.add).then_inc(ch.sem, ch.one())
                    dve.wait_ge(ch.sem, ch.value())
                    dve.scalar_tensor_tensor(out=nw[:, :], in0=w_bd[:, :], scalar=keep_w, in1=gm[:, :],
                                             op0=ALU.mult, op1=ALU.add).then_inc(ch.sem, ch.one())
                    dve.wait_ge(ch.sem, ch.value())
                    dve.tensor_scalar(nwok[:, :], nw[:, :], 0.0, 0.0, ALU.mult, ALU.is_equal).then_inc(ch.sem, ch.one())
                    dve.wait_ge(ch.sem, ch.value())
                    dve.wait_ge(nwf_set.sem, nwf_set.now(i))
                    dve.sem_inc(dve_waits_met, 1)
                    dve.copy_predicated(nwf[:, :], nwok[:, :], nw[:, :]).then_inc(nw_ready.sem, 1)
                    dve.wait_ge(thf_ready.sem, thf_ready.now(i))
                    dve.wait_ge(gf_turned.sem, gf_turned.before(i))
                    dve.scalar_tensor_tensor(out=gT1[:, :], in0=thf[:, :], scalar=1.0, in1=pf[:, 0:S],
                                             op0=ALU.add, op1=ALU.mult).then_inc(gT1_ready.sem, 1)
                    dve.wait_ge(h2_ready.sem, h2_ready.now(i))
                    dve.tensor_scalar(h2ok[:, :, :], h2[:, :, :], 0.0, 0.0, ALU.mult, ALU.is_equal).then_inc(ch.sem, ch.one())
                    dve.wait_ge(ch.sem, ch.value())
                    dve.wait_ge(hz_set.sem, hz_set.now(i))
                    dve.sem_inc(dve_waits_met, 1)
                    dve.copy_predicated(hz[:, :, :], h2ok[:, :, :], h2[:, :, :]).then_inc(ch.sem, ch.one())
                    dve.wait_ge(ch.sem, ch.value())
                    dve.tensor_tensor(y2[:, :, :], hz[:, :, :], hz[:, :, :], ALU.mult).then_inc(ch.sem, ch.one())
                    dve.wait_ge(ch.sem, ch.value())
                    r = unit(y2[:, :, :])
                    dve.tensor_tensor(heads(y2[:, :, :]), heads(hz[:, :, :]), r, ALU.mult).then_inc(ch.sem, ch.one())
                    dve.wait_ge(ch.sem, ch.value())
                    dve.tensor_tensor(y2[:, :, :], y2[:, :, :], kq[:, :, D:2 * D], ALU.add).then_inc(ch.sem, ch.one())
                    dve.wait_ge(ch.sem, ch.value())
                    dve.wait_ge(gf_turned.sem, gf_turned.now(i))
                    dve.scalar_tensor_tensor(out=y2[:, :, :], in0=y2[:, :, :], scalar=0.5,
                                             in1=pf[:, S:2 * S].rearrange("p (t d) -> p t d", t=TT), op0=ALU.mult, op1=ALU.mult).then_inc(ch.sem, ch.one())
                    dve.wait_ge(ch.sem, ch.value())
                    xs = x_all[:, bass.ds(i, 1), :, :].rearrange("p a t d -> p (a t) d")
                    dve.tensor_tensor(xs, xs, y2[:, :, :], ALU.add).then_inc(y_ready.sem, 1)
                    ch.end()


_INS = ['L0_attn_x', 'L0_attn_Wq', 'L0_attn_Wk', 'L0_attn_Wv', 'L0_attn_Wu', 'L0_attn_bu', 'L0_ffn_router_w',
        'L0_ffn_router_b', 'L0_ffn_expert_w', 'L0_ffn_expert_b', 'L1_attn_W_K', 'L1_attn_W_V', 'L1_attn_W_Q',
        'L1_attn_mem_W0', 'L1_attn_mem_W1', 'L1_attn_k_norm_w', 'L1_attn_q_norm_w', 'L1_attn_store_norm_w',
        'L1_attn_retrieve_norm_w', 'L1_attn_alpha_w', 'L1_attn_alpha_b', 'L1_attn_theta_w', 'L1_attn_theta_b',
        'L1_attn_eta_w', 'L1_attn_eta_b', 'L1_ffn_shared_up', 'L1_ffn_shared_down', 'L1_ffn_routed_up',
        'L1_ffn_routed_down', 'L1_ffn_router_w']


def shape_constants():
    import numpy as np

    c = np.zeros((P, N_C), np.float32)
    p = np.arange(P)
    c[:, C_ID:C_ID + P] = np.eye(P)
    c[:, C_SELQ] = -1.0 * ((p % 32) // HD == 2)
    c[:, C_SELK] = -1.0 * ((p % 32) // HD == 1)
    c[:, C_ONEK] = p % 32 == 3 * HD
    c[:, C_HEAD:C_HEAD + P] = p[:, None] // HD == p[None] // HD
    c[:, C_BD0:C_BD0 + H * HID] = p[:, None] // HD == np.arange(H * HID)[None] // HID
    c[:, C_BD1T:C_BD1T + P] = p[:, None] // HD % NG == p[None] // HID
    c[:, C_BD1:C_BD1 + NG * HD] = p[:, None] // HID == np.arange(NG * HD)[None] // HD
    c[:, C_CODE:C_CODE + E1] = E1 - np.arange(E1)
    c[:HD, C_REP8:C_REP8 + P] = np.arange(HD)[:, None] == p[None] % HD
    c[:HID, C_REP32:C_REP32 + P] = np.arange(HID)[:, None] == p[None] % HID
    c[:E0, C_SEL0:C_SEL0 + E0 * P] = np.arange(E0)[:, None] == np.arange(E0 * P)[None] // P
    r = np.arange(2 * E1)[:, None] % E1
    c[:2 * E1, C_SEL1:C_SEL1 + 8 * P] = r == np.arange(8 * P)[None] // FE
    c[:, C_ONE] = 1.0
    return c


def kernel(**inputs):
    import numpy as _np
    import concourse.bacc as _bacc
    from concourse import mybir as _mybir
    from concourse.bass_utils import run_bass_kernel_spmd as _run

    nc = _bacc.Bacc("TRN2", target_bir_lowering=False, num_devices=1)
    arrays = {"consts": shape_constants()}
    args = [nc.dram_tensor("consts", (P, N_C), F32, kind="ExternalInput").ap()]
    for name in _INS:
        a = _np.ascontiguousarray(inputs[name])
        arrays[f"in_{name}"] = a
        args.append(nc.dram_tensor(f"in_{name}", a.shape, _mybir.dt.from_np(a.dtype), kind="ExternalInput").ap())
    args.append(nc.dram_tensor("out", (B, S, D), F32, kind="ExternalOutput").ap())
    build(nc, *args)
    r = _run(nc, [arrays], core_ids=[0])
    return r.results[0]["out"]
```

```python
from contextlib import ExitStack

import concourse.bass as bass
from concourse import mybir

ALU = mybir.AluOpType
ACT = mybir.ActivationFunctionType
AX_X = mybir.AxisListType.X
F32 = mybir.dt.float32
F32R = mybir.dt.float32r
I32 = mybir.dt.int32

P = 128
B, S, D = 16, 256, 128
TT = S // P
NT = B * TT
H, HD = 16, 8
NJ, NG = 4, 4
HID = 4 * HD
E0, TOP0 = 8, 2
E1, TOP1 = 16, 4
FE = 64
NC1 = 1 + E1 * FE // P
LN_EPS, RMS_EPS, PF_EPS = 1e-5, 1e-6, 1e-8
ATT_SCALE = float(D) ** 0.25
CLIP = 10.0
MAX_LR = 0.01
RSQRT_MAGIC = float(0x5F3759DF)
FILL0 = -3.0e38
TAKEN0, TAKEN1 = -3.4e38, -100.0

T_Q, T_K, T_V, T_U, T_EXP, T_UP, T_DOWN, T_ROUTE, N_T = 0, 1, 2, 3, 4, 20, 29, 38, 39

N_R = 2 * E0 + E1

C_ID = 0
C_SELQ = C_ID + P
C_SELK = C_SELQ + 1
C_ONEK = C_SELK + 1
C_HEAD = C_ONEK + 1
C_BD0 = C_HEAD + P
C_BD1T = C_BD0 + H * HID
C_BD1 = C_BD1T + P
C_FILL0 = C_BD1 + NG * HD
C_FILL1 = C_FILL0 + 8 - TOP0
C_REP8 = C_FILL1 + 8 - TOP1
C_REP32 = C_REP8 + P
C_SEL0 = C_REP32 + P
C_SEL1 = C_SEL0 + E0 * P
C_ONE = C_SEL1 + 8 * P
C_LNPHI = C_ONE + 1
N_C = C_LNPHI + 1


class Signal:

    def __init__(self, sem, per):
        self.sem, self.per = sem, per

    def now(self, i, k=None):
        return i * self.per + self.per + (self.per if k is None else k)

    def before(self, i, k=None):
        return i * self.per + (self.per if k is None else k)


class Steps:

    def __init__(self, sem, per=0, turn=0):
        self.sem, self.per, self.turn, self.n = sem, per, turn, 0

    def one(self):
        self.n += 1
        return 1

    def value(self):
        return self.turn * self.per + self.n

    def end(self):
        assert self.n == self.per, (self.n, self.per)


DVE_TURN0, DVE_TURN1 = 15, 92


def build(nc, consts, L0_attn_x, L0_attn_Wq, L0_attn_Wk, L0_attn_Wv, L0_attn_Wu, L0_attn_bu,
          L0_ffn_router_w, L0_ffn_router_b, L0_ffn_expert_w, L0_ffn_expert_b,
          L1_attn_W_K, L1_attn_W_V, L1_attn_W_Q, L1_attn_mem_W0, L1_attn_mem_W1,
          L1_attn_k_norm_w, L1_attn_q_norm_w, L1_attn_store_norm_w, L1_attn_retrieve_norm_w,
          L1_attn_alpha_w, L1_attn_alpha_b, L1_attn_theta_w, L1_attn_theta_b, L1_attn_eta_w,
          L1_attn_eta_b, L1_ffn_shared_up, L1_ffn_shared_down, L1_ffn_routed_up,
          L1_ffn_routed_down, L1_ffn_router_w, out):
    ctx = ExitStack()
    with ctx:
        def sb(name, shape, dt=F32):
            return ctx.enter_context(nc.sbuf_tensor(name, shape, dt))

        def sem(name):
            return ctx.enter_context(nc.semaphore(name))

        cst = sb("cst", [P, N_C])
        ident = cst[:, C_ID:C_ID + P]
        wraw = sb("wraw", [P, N_T, P])
        wT = sb("wT", [P, N_T, P])
        wq_rep = sb("wq_rep", [P, NJ, P])
        wk_rep = sb("wk_rep", [P, NJ, P])
        wv_route = sb("wv_route", [P, D + E0])
        sel0 = sb("sel0", [P, E0, P], F32R)
        sel1 = sb("sel1", [P, NC1 - 1, P], F32R)
        exp_b = sb("exp_b", [E0, 2, D])
        bu_bc = sb("bu_bc", [P, D])
        rb_bc = sb("rb_bc", [P, 2, E0])
        gate_b = sb("gate_b", [P, 3 * H])
        norm_col = sb("norm_col", [P, 2])
        knq = sb("knq", [P, 2, HD])
        knq_bc = sb("knq_bc", [P, 2, H, HD])
        wraw1 = sb("wraw1", [P, 3, P])
        graw1 = sb("graw1", [P, 3 * H])
        NPRO = 3 * D + 3 * H + E1
        w_pro = sb("w_pro", [P, NPRO])
        mem0 = sb("mem0", [HD, HID])
        mem1 = sb("mem1", [HID, HD])
        mem1r = sb("mem1r", [HID, H, HD])
        rep = sb("rep", [P, 2 * HID + HD])
        NW = H * HID + P
        w_bd = sb("w_bd", [P, NW])
        w1_bd = sb("w1_bd", [P, NG * HD])
        w1t_bd = sb("w1t_bd", [P, H * HID])
        x_all = sb("x_all", [P, B, TT, D])
        stats = sb("stats", [P, NT, 6])
        mean = sb("mean", [P, NT])
        nrm = sb("nrm", [P, 2, NT])
        nrm_in = sb("nrm_in", [P, 2, NT])
        nt0 = sb("nt0", [P, NT])
        nt1 = sb("nt1", [P, NT])
        newt = sb("newt", [P, 2 * NT])

        xn = sb("xn", [P, TT, D])
        xnT = sb("xnT", [P, S])
        v1 = sb("v1", [P, TT, H, 32])
        top = sb("top", [P, TT])
        eight = sb("eight", [P, TT, 8])
        work0 = sb("work0", [P, TT, E0 + 8 - TOP0])
        find0 = sb("find0", [P, TT, 8])
        rest0 = sb("rest0", [P, TT, E0 + 8 - TOP0])
        work1 = sb("work1", [P, TT, E1 + 8 - TOP1])
        find1 = sb("find1", [P, TT, 8])
        rest1 = sb("rest1", [P, TT, E1 + 8 - TOP1])
        mask = sb("mask", [P, TT, 2 * E1])
        maskT = sb("maskT", [P, S], F32R)
        big = ctx.enter_context(ExitStack())

        def sb0(name, shape, dt=F32):
            return big.enter_context(nc.sbuf_tensor(name, shape, dt))

        psum = ctx.enter_context(nc.psum_tensor("psum", [P, 8, 512], F32))

        consts_in, raw_in, small_in, x_in = sem("consts_in"), sem("raw_in"), sem("small_in"), [sem(f"x_in{q}") for q in range(4)]
        x_out = sem("x_out")
        raw_turned, raw_copied, mem_rep, setup_done = (
            sem("raw_turned"), sem("raw_copied"), sem("mem_rep"), sem("setup_done"))
        zeroed = sem("zeroed")
        rep_src = sem("rep_src")
        dve_setup = sem("dve_setup")
        stats_ready = sem("stats_ready")
        dve_mid = sem("dve_mid")
        layer0_done = sem("layer0_done")

        loads = [
            (wraw[:, T_Q, :], L0_attn_Wq), (wraw[:, T_K, :], L0_attn_Wk),
            (wraw[:, T_V, :], L0_attn_Wv), (wraw[:, T_U, :], L0_attn_Wu),
            (wraw[:, T_EXP:T_UP, :], L0_ffn_expert_w.rearrange("l e d h -> d (l e) h")),
            (wraw[:, T_UP, :], L1_ffn_shared_up.rearrange("s e h -> (s e) h")),
            (wraw[:, T_UP + 1:T_DOWN, :], L1_ffn_routed_up.rearrange("(c s) e h -> (s e) c h", s=2)),
            (wraw[:, T_DOWN, :].rearrange("p (s e) -> p s e", s=2), L1_ffn_shared_down.rearrange("s h e -> h s e")),
            (wraw[:, T_DOWN + 1:T_ROUTE, :].rearrange("p c (s e) -> p (c s) e", s=2),
             L1_ffn_routed_down.rearrange("r h e -> h r e")),
            (wraw[0:2 * E0, T_ROUTE, :], L0_ffn_router_w.rearrange("l e h -> (l e) h")),
            (wraw[2 * E0:2 * E0 + E1, T_ROUTE, :], L1_ffn_router_w),
        ]
        small = [
            (wraw1[:, 0, :], L1_attn_W_K), (wraw1[:, 1, :], L1_attn_W_Q), (wraw1[:, 2, :], L1_attn_W_V),
            (graw1[:, 0:H], L1_attn_alpha_w), (graw1[:, H:2 * H], L1_attn_eta_w), (graw1[:, 2 * H:3 * H], L1_attn_theta_w),
            (gate_b[:, 0:H], L1_attn_alpha_b.partition_broadcast(P)),
            (gate_b[:, H:2 * H], L1_attn_eta_b.partition_broadcast(P)),
            (gate_b[:, 2 * H:3 * H], L1_attn_theta_b.partition_broadcast(P)),
            (bu_bc[:, :], L0_attn_bu.partition_broadcast(P)),
            (rb_bc[:, :, :], L0_ffn_router_b.partition_broadcast(P)),
            (norm_col[:, 0:1], L1_attn_store_norm_w.rearrange("(p a) -> p a", a=1)),
            (norm_col[:, 1:2], L1_attn_retrieve_norm_w.rearrange("(p a) -> p a", a=1)),
            (knq[:, 0, :], L1_attn_k_norm_w.partition_broadcast(P)),
            (knq[:, 1, :], L1_attn_q_norm_w.partition_broadcast(P)),
            (exp_b[:, :, :], L0_ffn_expert_b.rearrange("l e d -> e l d")),
            (mem0[:, :], L1_attn_mem_W0), (mem1[:, :], L1_attn_mem_W1),
        ]
        n_groups = (N_T + 3) // 4
        XQ = len(x_in)

        def newton(dve, chain, y, x, t, n):
            yi, xi = y.bitcast(I32), x.bitcast(I32)
            dve.tensor_scalar(yi, xi, 1, None, ALU.logical_shift_right).then_inc(chain.sem, chain.one())
            dve.wait_ge(chain.sem, chain.value())
            dve.tensor_scalar(yi, yi, -1.0, RSQRT_MAGIC, ALU.mult, ALU.add).then_inc(chain.sem, chain.one())
            dve.wait_ge(chain.sem, chain.value())
            for _ in range(3):
                dve.tensor_tensor(t, y, y, ALU.mult).then_inc(chain.sem, chain.one())
                dve.wait_ge(chain.sem, chain.value())
                dve.scalar_tensor_tensor(out=t, in0=t, scalar=-0.5, in1=x, op0=ALU.mult, op1=ALU.mult).then_inc(chain.sem, chain.one())
                dve.wait_ge(chain.sem, chain.value())
                dve.scalar_tensor_tensor(out=y, in0=t, scalar=1.5, in1=y, op0=ALU.add, op1=ALU.mult).then_inc(chain.sem, chain.one())
                dve.wait_ge(chain.sem, chain.value())

        def layer_stats(dve, chain, second):
            me, mo = stats[:, :, 1], stats[:, :, 4]
            dve.tensor_tensor(nt0[:, :], me, mo, ALU.add).then_inc(chain.sem, chain.one())
            dve.wait_ge(chain.sem, chain.value())
            dve.tensor_scalar(mean[:, :], nt0[:, :], 0.5, None, ALU.mult).then_inc(chain.sem, chain.one())
            dve.tensor_tensor(nt1[:, :], me, mo, ALU.subtract).then_inc(chain.sem, chain.one())
            dve.wait_ge(chain.sem, chain.value())
            dve.scalar_tensor_tensor(out=nt1[:, :], in0=nt1[:, :], scalar=0.25, in1=nt1[:, :],
                                     op0=ALU.mult, op1=ALU.mult).then_inc(chain.sem, chain.one())
            dve.wait_ge(chain.sem, chain.value())
            dve.tensor_tensor(nt0[:, :], stats[:, :, 2], stats[:, :, 5], ALU.add).then_inc(chain.sem, chain.one())
            dve.wait_ge(chain.sem, chain.value())
            dve.scalar_tensor_tensor(out=nt0[:, :], in0=nt0[:, :], scalar=1.0 / D, in1=nt1[:, :],
                                     op0=ALU.mult, op1=ALU.add).then_inc(chain.sem, chain.one())
            dve.wait_ge(chain.sem, chain.value())
            dve.tensor_scalar(nrm_in[:, 0, :], nt0[:, :], LN_EPS, None, ALU.add).then_inc(chain.sem, chain.one())
            dve.wait_ge(chain.sem, chain.value())
            if not second:
                newton(dve, chain, nrm[:, 0, :], nrm_in[:, 0, :], newt[:, 0:NT], NT)
                return
            dve.reciprocal(nt1[:, :], nrm_in[:, 0, :]).then_inc(chain.sem, chain.one())
            dve.wait_ge(chain.sem, chain.value())
            dve.tensor_tensor(nt1[:, :], nt0[:, :], nt1[:, :], ALU.mult).then_inc(chain.sem, chain.one())
            dve.wait_ge(chain.sem, chain.value())
            dve.tensor_scalar(nrm_in[:, 1, :], nt1[:, :], RMS_EPS, None, ALU.add).then_inc(chain.sem, chain.one())
            dve.wait_ge(chain.sem, chain.value())
            newton(dve, chain, nrm[:, :, :].rearrange("p a n -> p (a n)"), nrm_in[:, :, :].rearrange("p a n -> p (a n)"),
                   newt[:, :], 2 * NT)

        with nc.Block() as block:
            @block.sync
            def _(sp):
                xs = L0_attn_x.rearrange("b (t p) d -> p b t d", p=P)
                for q in range(XQ):
                    b0, b1 = q * (B // XQ), (q + 1) * (B // XQ)
                    sp.dma_start(x_all[:, b0:b1, :, :], xs[:, b0:b1, :, :]).then_inc(x_in[q], 16)
                    if q == 0:
                        sp.dma_start(cst[:, :], consts).then_inc(consts_in, 16)
                for dst, src in loads:
                    sp.dma_start(dst, src).then_inc(raw_in, 16)

            @block.gpsimd
            def _(pool):
                pool.memset(v1[:, :, :, :], 0.0).then_inc(zeroed, 1)
                pool.memset(wq_rep[:, :, :], 0.0).then_inc(zeroed, 1)
                pool.memset(wk_rep[:, :, :], 0.0).then_inc(zeroed, 1)
                pool.memset(mask[:, :, :], 0.0).then_inc(zeroed, 1)
                pool.wait_ge(zeroed, 4)
                pool.memset(v1[:, :, :, HD:HD + 1], 1.0).then_inc(zeroed, 1)

            @block.scalar
            def _(act):
                for dst, src in small:
                    act.dma_start(dst, src).then_inc(small_in, 16)
                for n in range(n_groups):
                    m = min(4, N_T - 4 * n)
                    act.wait_ge(raw_turned, n + 1)
                    w = m * P if n < n_groups - 1 else (m - 1) * P + N_R
                    nc.scalar.activation(wT[:, 4 * n:4 * n + m, :].rearrange("p m n -> p (m n)")[:, 0:w],
                                         psum[:, n % 4, 0:w], ACT.Copy).then_inc(raw_copied, 1)

            @block.tensor
            def _(pe):
                pe.wait_ge(consts_in, 16)
                pe.wait_ge(raw_in, 16 * len(loads))
                for n in range(n_groups):
                    m = min(4, N_T - 4 * n)
                    if n >= 4:
                        pe.wait_ge(raw_copied, n - 3)
                    for t in range(m):
                        r = N_R if 4 * n + t == T_ROUTE else P
                        last = nc.tensor.transpose(psum[:, n % 4, t * P:t * P + r], wraw[0:r, 4 * n + t, :], ident[0:r, 0:r])
                    last.then_inc(raw_turned, 1)
                pe.wait_ge(small_in, 16 * len(small))
                pe.wait_ge(rep_src, 1)
                nc.tensor.matmul(psum[:, 4, 0:HID], cst[0:HD, C_REP8:C_REP8 + P], mem0[:, :], start=True, stop=True)
                nc.tensor.matmul(psum[:, 4, HID:HID + HD], cst[0:HID, C_REP32:C_REP32 + P], mem1[:, :], start=True, stop=True)
                nc.tensor.matmul(psum[:, 4, HID + HD:2 * HID + HD], mem1r[:, :, :].rearrange("j h d -> j (h d)"),
                                 cst[0:HID, C_ID:C_ID + HID], start=True, stop=True).then_inc(mem_rep, 1)

            @block.vector
            def _(dve):
                ch = Steps(dve_setup)
                for q in range(XQ):
                    dve.wait_ge(x_in[q], 16)
                    with dve.Fori(q * NT // XQ // 4, (q + 1) * NT // XQ // 4) as g:
                        for t in range(4):
                            dve.bn_stats(stats[:, bass.ds(g * 4 + t, 1), :].rearrange("p a s -> p (a s)"),
                                         x_all[:, :, :, :].rearrange("p b t d -> p (b t) d")[:, bass.ds(g * 4 + t, 1), :].rearrange("p a d -> p (a d)")
                                         ).then_inc(stats_ready, 1)
                dve.wait_ge(small_in, 16 * len(small))
                dve.wait_ge(consts_in, 16)
                dve.tensor_copy(mem1r[:, :, :], mem1[:, :].unsqueeze(1).to_broadcast([HID, H, HD])).then_inc(rep_src, 1)
                dve.tensor_copy(sel0[:, :, :], cst[:, C_SEL0:C_SEL0 + E0 * P].rearrange("e (a p) -> e a p", p=P)).then_inc(ch.sem, ch.one())
                dve.tensor_copy(sel1[:, :, :], cst[:, C_SEL1:C_SEL1 + 8 * P].rearrange("e (a p) -> e a p", p=P)).then_inc(ch.sem, ch.one())
                for work, find, n, top_n, fill in ((work0, find0, E0, TOP0, C_FILL0), (work1, find1, E1, TOP1, C_FILL1)):
                    fillers = cst[:, fill:fill + 8 - top_n].unsqueeze(1).to_broadcast([P, TT, 8 - top_n])
                    dve.tensor_copy(work[:, :, n:n + 8 - top_n], fillers).then_inc(ch.sem, ch.one())
                    dve.tensor_copy(find[:, :, top_n:8], fillers).then_inc(ch.sem, ch.one())
                dve.tensor_scalar(maskT[:, :], cst[:, 0:S], 0.0, None, ALU.mult).then_inc(ch.sem, ch.one())
                dve.tensor_copy(knq_bc[:, :, :, :].rearrange("p a h d -> p a h d"),
                                knq[:, :, :].unsqueeze(2).to_broadcast([P, 2, H, HD])).then_inc(ch.sem, ch.one())
                for m, (col, c) in enumerate(((0, 0), (1, 1), (0, 2))):
                    dve.tensor_scalar(w_pro[:, m * D:m * D + D], wraw1[:, c, :], norm_col[:, col:col + 1], None, ALU.mult).then_inc(ch.sem, ch.one())
                dve.tensor_scalar(w_pro[:, 3 * D:3 * D + 3 * H], graw1[:, :], norm_col[:, 0:1], None, ALU.mult).then_inc(ch.sem, ch.one())
                dve.wait_ge(mem_rep, 1)
                dve.tensor_tensor(w_bd[:, 0:H * HID].rearrange("p (h j) -> p h j", h=H),
                                  cst[:, C_BD0:C_BD0 + H * HID].rearrange("p (h j) -> p h j", h=H),
                                  psum[:, 4, 0:HID].unsqueeze(1).to_broadcast([P, H, HID]), ALU.mult).then_inc(ch.sem, ch.one())
                dve.tensor_tensor(w1_bd[:, :].rearrange("p (g d) -> p g d", g=NG),
                                  cst[:, C_BD1:C_BD1 + NG * HD].rearrange("p (g d) -> p g d", g=NG),
                                  psum[:, 4, HID:HID + HD].unsqueeze(1).to_broadcast([P, NG, HD]), ALU.mult).then_inc(ch.sem, ch.one())
                turned = psum[:, 4, HID + HD:2 * HID + HD]
                dve.tensor_tensor(w1t_bd[:, :].rearrange("p (h j) -> p h j", h=H),
                                  cst[:, C_BD0:C_BD0 + H * HID].rearrange("p (h j) -> p h j", h=H),
                                  turned.unsqueeze(1).to_broadcast([P, H, HID]), ALU.mult).then_inc(ch.sem, ch.one())
                dve.tensor_tensor(w_bd[:, H * HID:NW].rearrange("p (g j) -> p g j", g=NG),
                                  cst[:, C_BD1T:C_BD1T + P].rearrange("p (g j) -> p g j", g=NG),
                                  turned.unsqueeze(1).to_broadcast([P, NG, HID]), ALU.mult).then_inc(ch.sem, ch.one())
                dve.wait_ge(raw_copied, n_groups)
                dve.wait_ge(zeroed, 5)
                for rep_w, t, signs in ((wq_rep, T_Q, (1, -1, 1)), (wk_rep, T_K, (1, 1, -1))):
                    for r, sign in enumerate(signs):
                        dve.tensor_scalar(
                     rep_w[:, :, :].rearrange("p j (g c) -> p (j g) c", g=NG)[:, :, HD * r:HD * r + HD],
                     wT[:, t, :].rearrange("p (h d) -> p h d", h=H), sign / ATT_SCALE, None, ALU.mult).then_inc(ch.sem, ch.one())
                dve.tensor_copy(wv_route[:, 0:D], wT[:, T_V, :]).then_inc(ch.sem, ch.one())
                dve.tensor_copy(wv_route[:, D:D + E0], wT[:, T_ROUTE, 0:E0]).then_inc(ch.sem, ch.one())
                dve.tensor_copy(w_pro[:, 3 * D + 3 * H:NPRO], wT[:, T_ROUTE, 2 * E0:2 * E0 + E1]).then_inc(ch.sem, ch.one())
                dve.wait_ge(stats_ready, NT)
                layer_stats(dve, ch, False)

        qhi, khi = sb0("qhi", [P, NJ, S], F32R), sb0("khi", [P, NJ, S], F32R)
        qst, kst = sb0("qst", [P, NJ, S], F32R), sb0("kst", [P, NJ, S], F32R)
        mneg = sb0("mneg", [P, TT, NJ, P])
        NPT = 3
        pT = sb0("pT", [P, NPT, 2, 2, S])
        oTs = sb0("oTs", [P, NJ, S])
        rsum = sb0("rsum", [P, TT * H])
        att = sb0("att", [P, TT, D])
        attT = sb0("attT", [P, S])
        xm = sb0("xm", [P, 2, 2, S])
        yT = sb0("yT", [P, S])
        th0 = sb0("th0", [P, S])
        gT0 = sb0("gT0", [P, S])
        sat = sb0("sat", [P, TT, D])
        zat = sb0("zat", [P, TT, D])

        scr = psum[:, 0:4, :].rearrange("p (s g) n -> p s g n", s=2)
        oT = psum[:, 4:6, :].rearrange("p a (j n) -> p (a j) n", j=2)
        pa, pb = psum[:, 6, :], psum[:, 7, :]
        NU = NJ * 2
        MASK_AT = 0

        xn_ready = Signal(sem("xn_ready"), 1)
        xn_turned = Signal(sem("xn_turned"), 1)
        xnT_ready = Signal(sem("xnT_ready"), 1)
        v_made = Signal(sem("v_made"), 1)
        v_ready = Signal(sem("v_ready"), 1)
        qk_made = Signal(sem("qk_made"), 2)
        qk_high = Signal(sem("qk_high"), 2)
        qk_ready = Signal(sem("qk_ready"), 2)
        scores_made = Signal(sem("scores_made"), NU)
        max_taken = Signal(sem("max_taken"), NU)
        max_turned = Signal(sem("max_turned"), 1)
        max_placed = Signal(sem("max_placed"), 1)
        st_made = Signal(sem("st_made"), NU)
        probs_ready = Signal(sem("probs_ready"), NU)
        pv_made = Signal(sem("pv_made"), NU)
        o_copied = Signal(sem("o_copied"), 1)
        o_turned = Signal(sem("o_turned"), 1)
        att_ready = Signal(sem("att_ready"), 1)
        att_turned = Signal(sem("att_turned"), 1)
        attT_ready = Signal(sem("attT_ready"), 1)
        s_made = Signal(sem("s_made"), 1)
        logits_made = Signal(sem("logits_made"), 1)
        router_read = Signal(sem("router_read"), 1)
        logits_read = Signal(sem("logits_read"), 1)
        mask_ready = Signal(sem("mask_ready"), 2)
        mask_turned = Signal(sem("mask_turned"), 2)
        maskT_ready = Signal(sem("maskT_ready"), 2)
        NCH = E0 // 2
        spread = Signal(sem("spread"), 2 * NCH)
        chosen_x = Signal(sem("chosen_x"), 2 * NCH)
        chunk_used = Signal(sem("chunk_used"), 2 * (NCH - 1))
        moe_made = Signal(sem("moe_made"), 2)
        yT_ready = Signal(sem("yT_ready"), 1)
        tanh_ready = Signal(sem("tanh_ready"), 1)
        gT_ready = Signal(sem("gT_ready"), 1)
        g_turned = Signal(sem("g_turned"), 1)
        x_updated = Signal(sem("x_updated"), 1)
        dve_turn0 = sem("dve_turn0")
        dve_front = sem("dve_front")
        x_waits_met = sem("x_waits_met")
        choice_waits_met = sem("choice_waits_met")

        def choose(dve, chain, n, rounds, values, find, rest, taken):
            dve.wait_ge(chain.sem, chain.value())
            dve.sem_inc(choice_waits_met, 1)
            for t in range(TT):
                dve.max(eight[:, t, :], values[:, t, :]).then_inc(chain.sem, chain.one())
            dve.wait_ge(chain.sem, chain.value())
            dve.tensor_copy(find[:, :, 0:rounds], eight[:, :, 0:rounds]).then_inc(chain.sem, chain.one())
            dve.wait_ge(chain.sem, chain.value())
            dve.sem_inc(choice_waits_met, 1)
            for t in range(TT):
                dve.match_replace(rest[:, t, :], find[:, t, :], values[:, t, :], taken).then_inc(chain.sem, chain.one())
            dve.wait_ge(chain.sem, chain.value())

        with nc.Block() as block:
            @block.tensor
            def _(pe):
                for sg in (xn_turned, v_made, qk_made, scores_made, max_turned, st_made, pv_made, o_turned, att_turned,
                           s_made, logits_made, mask_turned, spread, chunk_used, moe_made, g_turned):
                    pe.sem_inc(sg.sem, sg.per)

                def turn_tokens(n):
                    pe.wait_ge(xn_ready.sem, xn_ready.now(n))
                    pe.wait_ge(chosen_x.sem, chosen_x.before(n))
                    for t in range(TT):
                        last = nc.tensor.transpose(pa[:, t * P:t * P + P], xn[:, t, :], ident)
                    last.then_inc(xn_turned.sem, 1)

                def project(n):
                    pe.wait_ge(xnT_ready.sem, xnT_ready.now(n))
                    pe.wait_ge(gT_ready.sem, gT_ready.before(n))
                    for t in range(TT):
                        last = nc.tensor.matmul(pb[:, t * 136:t * 136 + 136], xnT[:, t * P:t * P + P], wv_route[:, :],
                                                start=True, stop=True)
                    last.then_inc(v_made.sem, 1)
                    pe.wait_ge(probs_ready.sem, probs_ready.before(n))
                    for m, w in enumerate((wq_rep, wk_rep)):
                        o = scr[:, m, :, :].rearrange("p g (j n) -> p (g j) n", j=2)
                        for j in range(NJ):
                            last = nc.tensor.matmul(o[:, j, :], w[:, j, :], xnT[:, :], start=True, stop=True)
                        last.then_inc(qk_made.sem, 1)

                def turn(i, follows):
                    def scores(u):
                        j, gp = u // 2, u % 2
                        if u == 0:
                            pe.wait_ge(qk_ready.sem, qk_ready.now(i))
                        if u >= 2:
                            pe.wait_ge(max_taken.sem, max_taken.now(i, u - 1))
                        for t in range(TT):
                            for g2 in range(2):
                                r = 32 * (2 * gp + g2)
                                last = nc.tensor.matmul(scr[:, u % 2, g2, t * S:t * S + S], qst[r:r + 32, j, t * P:t * P + P],
                                                        kst[r:r + 32, j, :], start=True, stop=True)
                        last.then_inc(scores_made.sem, 1)

                    def mask_turn(l):
                        pe.wait_ge(mask_ready.sem, mask_ready.now(i, l + 1))
                        if l == 1:
                            pe.wait_ge(logits_read.sem, logits_read.now(i))
                        for t in range(TT):
                            last = nc.tensor.transpose(pa[0:E0, t * P:t * P + P], mask[:, t, 0:E0], ident)
                        last.then_inc(mask_turned.sem, 1)

                    def spread_chunk(l, c):
                        if c == 0:
                            pe.wait_ge(maskT_ready.sem, maskT_ready.now(i, l + 1))
                        else:
                            pe.wait_ge(chosen_x.sem, chosen_x.now(i, NCH * l + c))
                        for e2 in range(2):
                            last = nc.tensor.matmul(pa[:, e2 * S:e2 * S + S], sel0[:, 2 * c + e2, :], maskT[:, :],
                                                    start=True, stop=True)
                        last.then_inc(spread.sem, 1)

                    def experts(l, c):
                        if c == 0:
                            if l == 0:
                                pe.wait_ge(v_ready.sem, v_ready.now(i))
                                pe.wait_ge(router_read.sem, router_read.now(i))
                            else:
                                pe.wait_ge(yT_ready.sem, yT_ready.now(i))
                            nc.tensor.matmul(pb[:, 0:S], exp_b[:, l, :], maskT[0:E0, :].bitcast(F32), start=True, stop=False)
                        pe.wait_ge(chosen_x.sem, chosen_x.now(i, NCH * l + c + 1))
                        for e2 in range(2):
                            last = nc.tensor.matmul(pb[:, 0:S], wT[:, T_EXP + E0 * l + 2 * c + e2, :], xm[:, c % 2, e2, :],
                                                    start=False, stop=(c == NCH - 1 and e2 == 1))
                        last.then_inc((chunk_used if c < NCH - 1 else moe_made).sem, 1)

                    def route_again():
                        pe.wait_ge(yT_ready.sem, yT_ready.now(i))
                        for t in range(TT):
                            last = nc.tensor.matmul(pa[:, t * E0:t * E0 + E0], yT[:, t * P:t * P + P], wT[:, T_ROUTE, E0:2 * E0],
                                                    start=True, stop=True)
                        last.then_inc(logits_made.sem, 1)

                    def scores_t(u):
                        j, gp = u // 2, u % 2
                        if u == 0:
                            pe.wait_ge(max_placed.sem, max_placed.now(i))
                        if u >= 2:
                            pe.wait_ge(probs_ready.sem, probs_ready.now(i, u - 1))
                        for c in range(2):
                            for g2 in range(2):
                                r = 32 * (2 * gp + g2)
                                last = nc.tensor.matmul(scr[:, u % 2, g2, c * S:c * S + S], kst[r:r + 32, j, c * P:c * P + P],
                                                        qst[r:r + 32, j, :], start=True, stop=True)
                        last.then_inc(st_made.sem, 1)

                    def weigh(u):
                        j, gp = u // 2, u % 2
                        pe.wait_ge(probs_ready.sem, probs_ready.now(i, u + 1))
                        for c in range(2):
                            for g2 in range(2):
                                g = 2 * gp + g2
                                last = nc.tensor.matmul(oT[32 * g:32 * g + 32, j, :], v1[:, c, NG * j + g, :],
                                                        pT[:, u % NPT, g2, c, :], start=(c == 0), stop=(c == 1),
                                                        skip_group_check=True)
                        last.then_inc(pv_made.sem, 1)

                    scores(0)
                    scores(1)
                    mask_turn(0)
                    scores(2)
                    spread_chunk(0, 0)
                    scores(3)
                    for c in range(NCH):
                        if c + 1 < NCH:
                            spread_chunk(0, c + 1)
                        experts(0, c)
                        scores(NCH + c)
                    pe.wait_ge(max_taken.sem, max_taken.now(i))
                    pe.wait_ge(x_updated.sem, x_updated.before(i))
                    for j in range(NJ):
                        for t in range(TT):
                            last = nc.tensor.transpose(oT[:, j, t * P:t * P + P], mneg[:, t, j, :], ident)
                    last.then_inc(max_turned.sem, 1)
                    route_again()
                    for u in range(NU + 1):
                        if u < NU:
                            scores_t(u)
                        if u >= 1:
                            weigh(u - 1)
                        if u == MASK_AT:
                            mask_turn(1)
                        if u == MASK_AT + 1:
                            spread_chunk(1, 0)
                        if u > MASK_AT + 1 and u - MASK_AT - 2 < NCH - 1:
                            spread_chunk(1, u - MASK_AT - 1)
                            experts(1, u - MASK_AT - 2)
                    for c in range(NU - MASK_AT - 1, NCH):
                        if c < NCH - 1:
                            spread_chunk(1, c + 1)
                            experts(1, c)
                    oX = psum[:, 4:6, :].rearrange("p t (j c) -> p t j c", j=NJ)
                    if follows:
                        turn_tokens(i + 1)
                    experts(1, NCH - 1)
                    pe.wait_ge(o_copied.sem, o_copied.now(i))
                    for t in range(TT):
                        for j in range(NJ):
                            last = nc.tensor.transpose(oX[:, t, j, :], oTs[:, j, t * P:t * P + P], ident)
                    last.then_inc(o_turned.sem, 1)
                    if follows:
                        project(i + 1)
                    pe.wait_ge(att_ready.sem, att_ready.now(i))
                    for t in range(TT):
                        last = nc.tensor.transpose(psum[:, 4, t * P:t * P + P], att[:, t, :], ident)
                    last.then_inc(att_turned.sem, 1)
                    pe.wait_ge(gT_ready.sem, gT_ready.now(i))
                    for t in range(TT):
                        last = nc.tensor.transpose(psum[:, 5, t * P:t * P + P], gT0[:, t * P:t * P + P], ident)
                    last.then_inc(g_turned.sem, 1)
                    pe.wait_ge(attT_ready.sem, attT_ready.now(i))
                    for t in range(TT):
                        last = nc.tensor.matmul(psum[:, 5, S + t * P:S + t * P + P], attT[:, t * P:t * P + P], wT[:, T_U, :],
                                                start=True, stop=True)
                    last.then_inc(s_made.sem, 1)

                turn_tokens(0)
                project(0)
                with pe.Fori(0, B - 1) as i:
                    turn(i, True)
                turn(B - 1, False)

            @block.scalar
            def _(act):
                for sg in (xnT_ready, v_ready, qk_high, probs_ready, o_copied, maskT_ready, yT_ready, tanh_ready, attT_ready):
                    act.sem_inc(sg.sem, sg.per)

                def tokens_copy(n):
                    act.wait_ge(xn_turned.sem, xn_turned.now(n))
                    act.wait_ge(qk_made.sem, qk_made.before(n))
                    act.wait_ge(chosen_x.sem, chosen_x.before(n, NCH))
                    nc.scalar.activation(xnT[:, :], pa[:, 0:S], ACT.Copy).then_inc(xnT_ready.sem, 1)

                def values_copy(n):
                    act.wait_ge(v_made.sem, v_made.now(n))
                    act.wait_ge(router_read.sem, router_read.now(n))
                    act.wait_ge(pv_made.sem, pv_made.before(n))
                    nc.scalar.activation(v1[:, :, :, 0:HD],
                                         pb[:, 0:TT * 136].rearrange("p (t c) -> p t c", t=TT)[:, :, 0:D]
                                         .rearrange("p t (h d) -> p t h d", h=H), ACT.Copy).then_inc(v_ready.sem, 1)

                def high_parts(n):
                    for m, hi in enumerate((qhi, khi)):
                        act.wait_ge(qk_made.sem, qk_made.now(n, m + 1))
                        act.wait_ge(qk_ready.sem, qk_ready.before(n))
                        src = scr[:, m, :, :].rearrange("p g (j n) -> p (g j) n", j=2)
                        if m == 0:
                            nc.scalar.activation(hi[:, :, :], src, ACT.Copy).then_inc(qk_high.sem, 1)
                        else:
                            nc.scalar.activation(hi[:, :, :], src, ACT.Identity, bias=cst[:, C_ONEK:C_ONEK + 1]
                                                 ).then_inc(qk_high.sem, 1)

                def turn(i, follows):
                    def probs(u):
                        act.wait_ge(st_made.sem, st_made.now(i, u + 1))
                        if u >= NPT:
                            act.wait_ge(pv_made.sem, pv_made.now(i, u + 1 - NPT))
                        else:
                            act.wait_ge(pv_made.sem, pv_made.before(i))
                        nc.scalar.activation(pT[:, u % NPT, :, :, :].rearrange("p g c n -> p g (c n)"), scr[:, u % 2, :, :],
                                             ACT.Exp).then_inc(probs_ready.sem, 1)

                    def mask_copy(l):
                        act.wait_ge(mask_turned.sem, mask_turned.now(i, l + 1))
                        if l == 0:
                            act.wait_ge(moe_made.sem, moe_made.before(i))
                        else:
                            act.wait_ge(moe_made.sem, moe_made.now(i, 1))
                        nc.scalar.activation(maskT[0:E0, :], pa[0:E0, 0:S], ACT.Copy).then_inc(maskT_ready.sem, 1)

                    mask_copy(0)
                    act.wait_ge(moe_made.sem, moe_made.now(i, 1))
                    nc.scalar.activation(yT[:, :], pb[:, 0:S], ACT.Copy).then_inc(yT_ready.sem, 1)
                    for u in range(NU):
                        probs(u)
                        if u == MASK_AT:
                            mask_copy(1)
                    act.wait_ge(pv_made.sem, pv_made.now(i))
                    act.wait_ge(o_turned.sem, o_turned.before(i))
                    nc.scalar.activation(oTs[:, :, :], oT, ACT.Copy).then_inc(o_copied.sem, 1)
                    if follows:
                        tokens_copy(i + 1)
                    act.wait_ge(moe_made.sem, moe_made.now(i))
                    act.wait_ge(gT_ready.sem, gT_ready.before(i))
                    nc.scalar.activation(th0[:, :], pb[:, 0:S], ACT.Tanh, scale=0.5).then_inc(tanh_ready.sem, 1)
                    if follows:
                        high_parts(i + 1)
                        values_copy(i + 1)
                    act.wait_ge(att_turned.sem, att_turned.now(i))
                    act.wait_ge(s_made.sem, s_made.before(i))
                    nc.scalar.activation(attT[:, :], psum[:, 4, 0:S], ACT.Copy).then_inc(attT_ready.sem, 1)

                tokens_copy(0)
                high_parts(0)
                values_copy(0)
                with act.Fori(0, B - 1) as i:
                    turn(i, True)
                turn(B - 1, False)

            @block.vector
            def _(dve):
                for sg in (xn_ready, qk_ready, max_taken, max_placed, att_ready, router_read, logits_read, mask_ready,
                           chosen_x, gT_ready, x_updated):
                    dve.sem_inc(sg.sem, sg.per)
                dve.memset(mneg[:, :, :, :], 0.0).then_inc(stats_ready, 1)
                dve.wait_ge(stats_ready, NT + 1)

                def normalise(n, ch):
                    dve.wait_ge(xn_turned.sem, xn_turned.before(n))
                    for t in range(TT):
                        ins = dve.tensor_scalar(xn[:, t, :], x_all[:, bass.ds(n, 1), t, :].rearrange("p a d -> p (a d)"),
                                                mean[:, bass.ds(n * TT + t, 1)], nrm[:, 0, bass.ds(n * TT + t, 1)],
                                                ALU.subtract, ALU.mult)
                        if t == TT - 1:
                            ins.then_inc(xn_ready.sem, 1)
                        else:
                            ins.then_inc(ch.sem, ch.one())

                def pick(n, l, src, read, ch):
                    dve.tensor_tensor(work0[:, :, 0:E0], src, rb_bc[:, l, :].unsqueeze(1).to_broadcast([P, TT, E0]),
                                      ALU.add).then_inc(read.sem, 1)
                    dve.wait_ge(read.sem, read.now(n))
                    choose(dve, ch, E0, TOP0, work0, find0, rest0, TAKEN0)
                    if l == 0:
                        dve.wait_ge(mask_turned.sem, mask_turned.before(n))
                    else:
                        dve.wait_ge(mask_turned.sem, mask_turned.now(n, 1))
                    dve.tensor_scalar(mask[:, :, 0:E0], rest0[:, :, 0:E0], TAKEN0, None, ALU.is_equal).then_inc(mask_ready.sem, 1)

                def route(n, ch):
                    dve.wait_ge(v_made.sem, v_made.now(n))
                    pick(n, 0, pb[:, 0:TT * 136].rearrange("p (t c) -> p t c", t=TT)[:, :, D:D + E0], router_read, ch)

                def strips(n):
                    for m, (st, hi, sel) in enumerate(((qst, qhi, C_SELQ), (kst, khi, C_SELK))):
                        dve.wait_ge(qk_high.sem, qk_high.now(n, m + 1))
                        dve.wait_ge(st_made.sem, st_made.before(n))
                        src = scr[:, m, :, :].rearrange("p g (j n) -> p (g j) n", j=2)
                        dve.scalar_tensor_tensor(out=st[:, :, :], in0=src, scalar=cst[:, sel:sel + 1], in1=hi[:, :, :].bitcast(F32),
                                                 op0=ALU.mult, op1=ALU.add).then_inc(qk_ready.sem, 1)

                def turn(i, follows):
                    ch = Steps(dve_turn0, DVE_TURN0, i)

                    def maximum(u):
                        j, gp = u // 2, u % 2
                        dve.wait_ge(scores_made.sem, scores_made.now(i, u + 1))
                        o = mneg[:, :, j, 64 * gp:64 * gp + 64].rearrange("p t (g c) -> p g t c", g=2)[:, :, :, 24]
                        dve.tensor_reduce(o, scr[:, u % 2, :, :].rearrange("p g (t n) -> p g t n", t=TT), AX_X, ALU.max,
                                          negate=True).then_inc(max_taken.sem, 1)

                    def mult_chunk(l, c, src):
                        k = NCH * l + c
                        dve.wait_ge(spread.sem, spread.now(i, k + 1))
                        if c >= 2:
                            dve.wait_ge(chunk_used.sem, chunk_used.now(i, (NCH - 1) * l + c - 1))
                        elif l == 1:
                            dve.wait_ge(moe_made.sem, moe_made.now(i, 1))
                        else:
                            dve.wait_ge(moe_made.sem, moe_made.before(i))
                        dve.tensor_tensor(xm[:, c % 2, :, :], pa[:, 0:2 * S].rearrange("p (e n) -> p e n", e=2),
                                          src[:, :].unsqueeze(1).to_broadcast([P, 2, S]), ALU.mult).then_inc(chosen_x.sem, 1)

                    dve.wait_ge(max_turned.sem, max_turned.before(i))
                    maximum(0)
                    maximum(1)
                    for c in range(NCH):
                        mult_chunk(0, c, xnT)
                        maximum(c + 2)
                    maximum(NCH + 2)
                    maximum(NCH + 3)
                    dve.wait_ge(max_turned.sem, max_turned.now(i))
                    dve.wait_ge(qk_ready.sem, qk_ready.now(i))
                    for a in range(2):
                        ins = dve.tensor_tensor(qst[:, 2 * a:2 * a + 2, :], oT[:, 2 * a:2 * a + 2, :],
                                                qst[:, 2 * a:2 * a + 2, :].bitcast(F32), ALU.add)
                        if a == 0:
                            ins.then_inc(ch.sem, ch.one())
                        else:
                            ins.then_inc(max_placed.sem, 1)

                    dve.wait_ge(logits_made.sem, logits_made.now(i))
                    pick(i, 1, pa[:, 0:TT * E0].rearrange("p (t c) -> p t c", t=TT), logits_read, ch)
                    if follows:
                        normalise(i + 1, ch)
                    for c in range(NCH):
                        mult_chunk(1, c, yT)
                    dve.wait_ge(tanh_ready.sem, tanh_ready.now(i))
                    dve.wait_ge(g_turned.sem, g_turned.before(i))
                    dve.scalar_tensor_tensor(out=gT0[:, :], in0=th0[:, :], scalar=1.0, in1=pb[:, 0:S],
                                             op0=ALU.add, op1=ALU.mult).then_inc(gT_ready.sem, 1)
                    dve.wait_ge(o_turned.sem, o_turned.now(i))
                    oh = psum[:, 4:6, :].rearrange("p t (h c) -> p (t h) c", c=32)
                    dve.reciprocal(rsum[:, :], oh[:, :, HD]).then_inc(ch.sem, ch.one())
                    dve.wait_ge(ch.sem, ch.value())
                    dve.wait_ge(att_turned.sem, att_turned.before(i))
                    dve.tensor_tensor(att[:, :, :].rearrange("p t (h d) -> p (t h) d", d=HD), oh[:, :, 0:HD],
                                      rsum[:, :].unsqueeze(2).to_broadcast([P, TT * H, HD]), ALU.mult).then_inc(att_ready.sem, 1)
                    if follows:
                        route(i + 1, ch)
                        strips(i + 1)
                    dve.wait_ge(s_made.sem, s_made.now(i))
                    dve.wait_ge(g_turned.sem, g_turned.now(i))
                    dve.tensor_tensor(sat[:, :, :], psum[:, 5, S:2 * S].rearrange("p (t d) -> p t d", t=TT),
                                      bu_bc[:, :].unsqueeze(1).to_broadcast([P, TT, D]), ALU.add).then_inc(ch.sem, ch.one())
                    dve.wait_ge(ch.sem, ch.value())
                    dve.scalar_tensor_tensor(out=zat[:, :, :], in0=sat[:, :, :], scalar=0.5,
                                             in1=psum[:, 5, 0:S].rearrange("p (t d) -> p t d", t=TT), op0=ALU.mult, op1=ALU.mult).then_inc(ch.sem, ch.one())
                    dve.wait_ge(ch.sem, ch.value())
                    xs = x_all[:, bass.ds(i, 1), :, :].rearrange("p a t d -> p (a t) d")
                    dve.tensor_tensor(xs, xs, zat[:, :, :], ALU.add).then_inc(x_updated.sem, 1)
                    dve.wait_ge(x_updated.sem, x_updated.now(i))
                    dve.sem_inc(x_waits_met, 1)
                    for t in range(TT):
                        dve.bn_stats(stats[:, bass.ds(i * TT + t, 1), :].rearrange("p a s -> p (a s)"),
                                     x_all[:, bass.ds(i, 1), t, :].rearrange("p a d -> p (a d)")).then_inc(stats_ready, 1)
                    if follows:
                        ch.end()

                first = Steps(dve_front)
                normalise(0, first)
                route(0, first)
                strips(0)
                with dve.Fori(0, B - 1) as i:
                    turn(i, True)
                turn(B - 1, False)
        big.close()

        with nc.Block() as block:
            @block.vector
            def _(dve):
                ch = Steps(dve_mid)
                dve.wait_ge(stats_ready, 2 * NT + 1)
                layer_stats(dve, ch, True)

        pro = sb("pro", [P, TT, 3 * D])
        gl = sb("gl", [P, TT, 3 * H])
        th1 = sb("th1", [P, TT, 3 * H])
        thx = sb("thx", [P, TT, 2 * H, HD])
        th2 = sb("th2", [P, TT, H])
        sq = sb("sq", [P, TT, 2 * D])
        ms = sb("ms", [P, 2 * TT * H])
        rinv = sb("rinv", [P, 2 * TT * H])
        scratch = sb("scratch", [P, 2 * TT * H])
        kq = sb("kq", [P, TT, 2 * D])
        qkeep = sb("qkeep", [P, TT, D])
        kmv = sb("kmv", [P, TT, D])
        kqT = sb("kqT", [P, 2, S])
        aT = sb("aT", [P, NJ, S])
        a1 = sb("a1", [P, TT, H * HID])
        pre = sb("pre", [P, TT, H * HID])
        pdf = sb("pdf", [P, TT, H * HID])
        inv = sb("inv", [P, TT, H * HID])
        gg = sb("gg", [P, TT, H * HID])
        dh1 = sb("dh1", [P, TT, H * HID])
        hT = sb("hT", [P, S])
        h1 = sb("h1", [P, TT, D])
        h1sq = sb("h1sq", [P, TT, D])
        hn = sb("hn", [P, TT, D])
        dp = sb("dp", [P, TT, D])
        tmp = sb("tmp", [P, TT, D])
        dy = sb("dy", [P, TT * H])
        dh = sb("dh", [P, TT, D])
        dhT = sb("dhT", [P, S])
        gm = sb("gm", [P, NW])
        gsq = sb("gsq", [P, NW])
        gsum = sb("gsum", [P, 1])
        sums = sb("sums", [P, 2])
        cf = sb("cf", [P, 8])
        nw = sb("nw", [P, NW])
        nwok = sb("nwok", [P, NW], I32)
        nwf = sb("nwf", [P, NW])
        nw1 = sb("nw1", [P, P])
        h2 = sb("h2", [P, TT, D])
        h2ok = sb("h2ok", [P, TT, D], I32)
        hz = sb("hz", [P, TT, D])
        y2 = sb("y2", [P, TT, D])
        actT = sb("actT", [P, NC1, S])
        rld = sb("rld", [P, TT, E1])
        rex = sb("rex", [P, TT, E1])
        rsm = sb("rsm", [P, TT])
        prob = sb("prob", [P, TT, E1])
        thf = sb("thf", [P, S])
        gT1 = sb("gT1", [P, S])

        px = psum[:, 0:2, :]
        pt, pf = psum[:, 4, :], psum[:, 5, :]
        pg = psum[:, 6:8, :].rearrange("p b n -> p (b n)")
        G0, G1, GS, GQ, GH = 0, 512, 640, 642, 768
        NUP = (NC1 + 1) // 2
        BD = P // NJ

        def sig(name, per=1):
            return Signal(sem(name), per)

        xn1_ready, xn1_turned, xn1T_ready = sig("xn1_ready"), sig("xn1_turned"), sig("xn1T_ready")
        pro_made, pro_read, pro_ready = sig("pro_made"), sig("pro_read"), sig("pro_ready", TT)
        gl_ready = sig("gl_ready", TT)
        th1_ready, sq_ready = sig("th1_ready"), sig("sq_ready")
        up_made, up_read = sig("up_made", NUP), sig("up_read", NUP)
        khid_made, khid_read = sig("khid_made", 2), sig("khid_read", 2)
        qhid_made, qhid_read = sig("qhid_made", 2), sig("qhid_read", 2)
        q_kept = sig("q_kept")
        inv_ready, half_less, quotient, slope_ready = (sig("inv_ready", TT), sig("half_less", TT), sig("quotient", TT),
                                                       sig("slope_ready", TT))
        kq_ready, kq_turned, kqT_ready = sig("kq_ready"), sig("kq_turned"), sig("kqT_ready")
        thx_ready, kmv_ready = sig("thx_ready"), sig("kmv_ready")
        pre_made, pre_read, a1_ready = sig("pre_made", TT), sig("pre_read", TT), sig("a1_ready", TT)
        pre_copied, pre_squared = sig("pre_copied", TT), sig("pre_squared", TT)
        rex_ready, pdf_ready, pm_ready = sig("rex_ready"), sig("pdf_ready", TT), sig("pm_ready", TT)
        gates_ready, gates_turned, gatesT_ready = sig("gates_ready"), sig("gates_turned"), sig("gatesT_ready")
        NGC = (NC1 - 1) // 2
        gates_spread, gated = sig("gates_spread", NGC), sig("gated", NGC)
        h1T_made, h1T_copied, h1_turned = sig("h1T_made"), sig("h1T_copied"), sig("h1_turned")
        h1_copied, h1_ready = sig("h1_copied"), sig("h1_ready")
        dh_ready, dh_turned, dhT_ready = sig("dh_ready"), sig("dh_turned"), sig("dhT_ready")
        back_made, dh1_ready = sig("back_made", TT), sig("dh1_ready", TT)
        g1_made, g0_made, gm_ready = sig("g1_made"), sig("g0_made"), sig("gm_ready")
        gsum_ready, gtotal_made = sig("gsum_ready"), sig("gtotal_made")
        nwf_set, nw_ready, nw_turned, nw1_ready = sig("nwf_set"), sig("nw_ready"), sig("nw_turned"), sig("nw1_ready")
        h2T_made, h2T_copied, h2_turned, h2_ready = sig("h2T_made"), sig("h2T_copied"), sig("h2_turned"), sig("h2_ready")
        hz_set = sig("hz_set")
        ffn_made, thf_ready, gT1_ready, gf_turned = sig("ffn_made"), sig("thf_ready"), sig("gT1_ready"), sig("gf_turned")
        y_ready = sig("y_ready")
        y_stored = sem("y_stored")
        dve_turn1, dve_front1 = sem("dve_turn1"), sem("dve_front1")
        dve_waits_met, pool_waits_met = sem("dve_waits_met"), sem("pool_waits_met")

        with nc.Block() as block:
            @block.sync
            def _(sp):
                with sp.Fori(0, B) as i:
                    sp.wait_ge(y_ready.sem, y_ready.now(i))
                    sp.dma_start(out.rearrange("b (t p) d -> b p t d", p=P)[bass.ds(i, 1)].rearrange("a p t d -> (a p) t d"),
                                 x_all[:, bass.ds(i, 1), :, :].rearrange("p a t d -> p (a t) d")).then_inc(y_stored, 16)
                sp.wait_ge(y_stored, 16 * B)

            @block.gpsimd
            def _(pool):
                for sg in (thx_ready, kmv_ready, half_less, quotient, pm_ready, slope_ready, nwf_set, hz_set, q_kept):
                    pool.sem_inc(sg.sem, sg.per)

                def front(n):
                    pool.wait_ge(th1_ready.sem, th1_ready.now(n))
                    pool.wait_ge(g1_made.sem, g1_made.before(n))
                    pool.sem_inc(pool_waits_met, 1)
                    pool.tensor_copy(thx[:, :, :, :], th1[:, :, 0:2 * H].unsqueeze(3).to_broadcast([P, TT, 2 * H, HD])
                                     ).then_inc(thx_ready.sem, 1)
                    pool.wait_ge(kq_ready.sem, kq_ready.now(n))
                    pool.wait_ge(dh_ready.sem, dh_ready.before(n))
                    pool.tensor_tensor(kmv[:, :, :], kq[:, :, 0:D], pro[:, :, 2 * D:3 * D], ALU.subtract).then_inc(kmv_ready.sem, 1)

                def turn(i, follows):
                    pool.wait_ge(h2T_made.sem, h2T_made.before(i))
                    pool.sem_inc(pool_waits_met, 1)
                    pool.tensor_copy(nwf[:, :], w_bd[:, :]).then_inc(nwf_set.sem, 1)
                    pool.wait_ge(y_ready.sem, y_ready.before(i))
                    pool.sem_inc(pool_waits_met, 1)
                    pool.memset(hz[:, :, :], 0.0).then_inc(hz_set.sem, 1)
                    pool.tensor_copy(qkeep[:, :, :], kq[:, :, D:2 * D]).then_inc(q_kept.sem, 1)
                    for t in range(TT):
                        pool.wait_ge(pre_read.sem, pre_read.now(i, t + 1))
                        pool.tensor_tensor(gg[:, t, :], gg[:, t, :], a1[:, t, :], ALU.add).then_inc(half_less.sem, 1)
                    for t in range(TT):
                        pool.wait_ge(half_less.sem, half_less.now(i, t + 1))
                        pool.wait_ge(inv_ready.sem, inv_ready.now(i, t + 1))
                        pool.tensor_tensor(gg[:, t, :], gg[:, t, :], inv[:, t, :], ALU.mult).then_inc(quotient.sem, 1)
                        pool.wait_ge(pdf_ready.sem, pdf_ready.now(i, t + 1))
                        pool.tensor_tensor(pdf[:, t, :], pdf[:, t, :], pre[:, t, :], ALU.mult).then_inc(pm_ready.sem, 1)
                        pool.wait_ge(quotient.sem, quotient.now(i, t + 1))
                        pool.wait_ge(pm_ready.sem, pm_ready.now(i, t + 1))
                        pool.tensor_tensor(gg[:, t, :], gg[:, t, :], pdf[:, t, :], ALU.add).then_inc(slope_ready.sem, 1)
                    if follows:
                        front(i + 1)

                front(0)
                with pool.Fori(0, B - 1) as i:
                    turn(i, True)
                turn(B - 1, False)

            @block.tensor
            def _(pe):
                for sg in (xn1_turned, pro_made, up_made, khid_made, qhid_made, kq_turned, pre_made, gates_turned, gates_spread,
                           h1T_made, h1_turned, dh_turned, back_made, g1_made, g0_made, gtotal_made, nw_turned, h2T_made,
                           h2_turned, ffn_made, gf_turned):
                    pe.sem_inc(sg.sem, sg.per)

                def turn_tokens(n):
                    pe.wait_ge(xn1_ready.sem, xn1_ready.now(n))
                    pe.wait_ge(gatesT_ready.sem, gatesT_ready.before(n))
                    for t in range(TT):
                        last = nc.tensor.transpose(pt[:, t * P:t * P + P], xn[:, t, :], ident)
                    last.then_inc(xn1_turned.sem, 1)

                def project(n):
                    pe.wait_ge(xn1T_ready.sem, xn1T_ready.now(n))
                    pe.wait_ge(dh1_ready.sem, dh1_ready.before(n))
                    for t in range(TT):
                        last = nc.tensor.matmul(px[:, t, 0:NPRO], xnT[:, t * P:t * P + P], w_pro[:, :], start=True, stop=True)
                    last.then_inc(pro_made.sem, 1)

                def up_products(n):
                    for m in range(NUP):
                        if m == 0:
                            pe.wait_ge(gated.sem, gated.before(n))
                        elif m >= 2:
                            pe.wait_ge(up_read.sem, up_read.now(n, m - 1))
                        for c in range(2 * m, min(2 * m + 2, NC1)):
                            last = nc.tensor.matmul(psum[:, 2 + m % 2, c % 2 * S:c % 2 * S + S], wT[:, T_UP + c, :], xnT[:, :],
                                                    start=True, stop=True)
                        last.then_inc(up_made.sem, 1)

                def turn_kq(n):
                    pe.wait_ge(kq_ready.sem, kq_ready.now(n))
                    pe.wait_ge(h2_ready.sem, h2_ready.before(n))
                    for m in range(2):
                        for t in range(TT):
                            last = nc.tensor.transpose(pt[:, m * S + t * P:m * S + t * P + P], kq[:, t, m * D:m * D + D], ident)
                    last.then_inc(kq_turned.sem, 1)

                def hidden(m, w, made):
                    for a in range(2):
                        for c in range(2 * a, 2 * a + 2):
                            last = nc.tensor.matmul(psum[:, 2 + a, c % 2 * S:c % 2 * S + S], w[:, c * P:c * P + P],
                                                    kqT[:, m, :], start=True, stop=True)
                        last.then_inc(made.sem, 1)

                def turn(i, follows):
                    pe.wait_ge(kqT_ready.sem, kqT_ready.now(i))
                    pe.wait_ge(pro_read.sem, pro_read.now(i))
                    for t in range(TT):
                        nc.tensor.matmul(px[:, t, :], kqT[:, 0, t * P:t * P + P], w_bd[:, 0:H * HID], start=True, stop=True
                                         ).then_inc(pre_made.sem, 1)
                    pe.wait_ge(up_read.sem, up_read.now(i))
                    pe.wait_ge(qhid_read.sem, qhid_read.before(i))
                    hidden(0, w_bd, khid_made)
                    pe.wait_ge(khid_read.sem, khid_read.now(i))
                    pe.wait_ge(h2T_copied.sem, h2T_copied.before(i))
                    for c in range(NJ):
                        last = nc.tensor.matmul(pg[BD * c:BD * c + BD, GH:GH + S], w1_bd[:, :], aT[:, c, :],
                                                start=True, stop=True)
                    last.then_inc(h1T_made.sem, 1)
                    pe.wait_ge(h1T_copied.sem, h1T_copied.now(i))
                    for t in range(TT):
                        last = nc.tensor.transpose(pt[:, t * P:t * P + P], hT[:, t * P:t * P + P], ident)
                    last.then_inc(h1_turned.sem, 1)
                    pe.wait_ge(dh_ready.sem, dh_ready.now(i))
                    pe.wait_ge(h1_ready.sem, h1_ready.now(i))
                    for t in range(TT):
                        last = nc.tensor.transpose(pt[:, t * P:t * P + P], dh[:, t, :], ident)
                    last.then_inc(dh_turned.sem, 1)
                    pe.wait_ge(dhT_ready.sem, dhT_ready.now(i))
                    pe.wait_ge(pre_read.sem, pre_read.now(i))
                    for t in range(TT):
                        nc.tensor.matmul(px[:, t, :], dhT[:, t * P:t * P + P], w1t_bd[:, :], start=True, stop=True
                                         ).then_inc(back_made.sem, 1)
                    for c in range(NJ):
                        for t in range(TT):
                            nc.tensor.matmul(pg[BD * c:BD * c + BD, G1:G1 + P], dh[:, t, BD * c:BD * c + BD],
                                             a1[:, t, P * c:P * c + P], start=(t == 0), stop=(t == TT - 1))
                    pe.wait_ge(thx_ready.sem, thx_ready.now(i))
                    for m in range(2):
                        for t in range(TT):
                            last = nc.tensor.matmul(pg[:, GS + m:GS + m + 1],
                                                    thx[:, t, m * H:m * H + H, :].rearrange("p h d -> p (h d)"),
                                                    cst[:, C_ONE:C_ONE + 1], start=(t == 0), stop=(t == TT - 1))
                    last.then_inc(g1_made.sem, 1)
                    pe.wait_ge(gates_ready.sem, gates_ready.now(i))
                    for t in range(TT):
                        last = nc.tensor.transpose(pt[0:2 * E1, t * P:t * P + P], mask[:, t, :], ident)
                    last.then_inc(gates_turned.sem, 1)

                    def spread_gates(c):
                        if c >= 2:
                            pe.wait_ge(gated.sem, gated.now(i, c - 1))
                        for e2 in range(2):
                            last = nc.tensor.matmul(psum[:, 2 + c % 2, e2 * S:e2 * S + S], sel1[:, 2 * c + e2, :], maskT[:, :],
                                                    start=True, stop=True)
                        last.then_inc(gates_spread.sem, 1)

                    pe.wait_ge(gatesT_ready.sem, gatesT_ready.now(i))
                    spread_gates(0)
                    spread_gates(1)
                    if follows:
                        turn_tokens(i + 1)
                    pe.wait_ge(dh1_ready.sem, dh1_ready.now(i))
                    pe.wait_ge(gm_ready.sem, gm_ready.before(i))
                    for t in range(TT):
                        last = nc.tensor.matmul(pg[:, G0:G0 + H * HID], kq[:, t, 0:D], dh1[:, t, :],
                                                start=(t == 0), stop=(t == TT - 1))
                    last.then_inc(g0_made.sem, 1)
                    spread_gates(2)
                    spread_gates(3)
                    if follows:
                        project(i + 1)
                    pe.wait_ge(gsum_ready.sem, gsum_ready.now(i))
                    nc.tensor.matmul(pg[:, GQ:GQ + 1], cst[:, C_HEAD:C_HEAD + P], gsum[:, :], start=True, stop=True
                                     ).then_inc(gtotal_made.sem, 1)
                    pe.wait_ge(y_ready.sem, y_ready.before(i))
                    for c in range(NC1):
                        if c >= 1:
                            pe.wait_ge(gated.sem, gated.now(i, (c + 1) // 2))
                        last = nc.tensor.matmul(pf[:, 0:S], wT[:, T_DOWN + c, :], actT[:, c, :], start=(c == 0), stop=(c == NC1 - 1))
                    last.then_inc(ffn_made.sem, 1)
                    if follows:
                        up_products(i + 1)
                    pe.wait_ge(nw_ready.sem, nw_ready.now(i))
                    nc.tensor.transpose(pt[:, 0:P], nwf[:, H * HID:NW], ident).then_inc(nw_turned.sem, 1)
                    if follows:
                        pe.wait_ge(up_read.sem, up_read.now(i + 1))
                    hidden(1, nwf, qhid_made)
                    pe.wait_ge(gT1_ready.sem, gT1_ready.now(i))
                    for t in range(TT):
                        last = nc.tensor.transpose(pf[:, S + t * P:S + t * P + P], gT1[:, t * P:t * P + P], ident)
                    last.then_inc(gf_turned.sem, 1)
                    pe.wait_ge(nw1_ready.sem, nw1_ready.now(i))
                    pe.wait_ge(qhid_read.sem, qhid_read.now(i))
                    for c in range(NJ):
                        last = nc.tensor.matmul(pg[BD * c:BD * c + BD, GH:GH + S], nw1[:, BD * c:BD * c + BD], aT[:, c, :],
                                                start=True, stop=True)
                    last.then_inc(h2T_made.sem, 1)
                    pe.wait_ge(h2T_copied.sem, h2T_copied.now(i))
                    for t in range(TT):
                        last = nc.tensor.transpose(pt[:, t * P:t * P + P], hT[:, t * P:t * P + P], ident)
                    last.then_inc(h2_turned.sem, 1)
                    if follows:
                        turn_kq(i + 1)

                turn_tokens(0)
                project(0)
                up_products(0)
                turn_kq(0)
                with pe.Fori(0, B - 1) as i:
                    turn(i, True)
                turn(B - 1, False)

            @block.scalar
            def _(act):
                for sg in (xn1T_ready, pro_ready, th1_ready, sq_ready, up_read, khid_read, qhid_read, kqT_ready, a1_ready, pre_copied, pre_squared,
                           pre_read, rex_ready, pdf_ready, gatesT_ready, h1T_copied, h1_copied, h1_ready, dhT_ready, gsum_ready,
                           nw1_ready, h2T_copied, h2_ready, thf_ready):
                    act.sem_inc(sg.sem, sg.per)

                def tokens_copy(n):
                    act.wait_ge(xn1_turned.sem, xn1_turned.now(n))
                    act.wait_ge(up_made.sem, up_made.before(n))
                    nc.scalar.activation(xnT[:, :], pt[:, 0:S], ACT.Copy).then_inc(xn1T_ready.sem, 1)

                def gate_inputs(n):
                    act.wait_ge(pro_made.sem, pro_made.now(n))
                    act.wait_ge(kmv_ready.sem, kmv_ready.before(n))
                    for t in range(TT):
                        nc.scalar.activation(pro[:, t, :], px[:, t, 0:3 * D], ACT.Copy, scale=nrm[:, 1, bass.ds(n * TT + t, 1)]
                                             ).then_inc(pro_ready.sem, 1)
                    act.wait_ge(kq_ready.sem, kq_ready.before(n))
                    act.wait_ge(pro_ready.sem, pro_ready.now(n))
                    nc.scalar.activation(sq[:, :, :], pro[:, :, 0:2 * D], ACT.Square).then_inc(sq_ready.sem, 1)
                    act.wait_ge(pro_read.sem, pro_read.now(n))
                    act.wait_ge(gates_ready.sem, gates_ready.before(n))
                    nc.scalar.activation(rex[:, :, :], rld[:, :, :], ACT.Exp).then_inc(rex_ready.sem, 1)
                    act.wait_ge(gl_ready.sem, gl_ready.now(n))
                    act.wait_ge(thx_ready.sem, thx_ready.before(n))
                    act.wait_ge(dh_ready.sem, dh_ready.before(n))
                    nc.scalar.activation(th1[:, :, :], gl[:, :, :], ACT.Tanh, scale=0.5).then_inc(th1_ready.sem, 1)

                def up(n):
                    act.wait_ge(ffn_made.sem, ffn_made.before(n))
                    for k in range(NUP):
                        act.wait_ge(up_made.sem, up_made.now(n, k + 1))
                        m = min(2, NC1 - 2 * k)
                        nc.scalar.activation(actT[:, 2 * k:2 * k + m, :].rearrange("p c n -> p (c n)"),
                                             psum[:, 2 + k % 2, 0:m * S], ACT.Gelu).then_inc(up_read.sem, 1)

                def kqT_copy(n):
                    act.wait_ge(kq_turned.sem, kq_turned.now(n))
                    nc.scalar.activation(kqT[:, :, :].rearrange("p m n -> p (m n)"), pt, ACT.Copy).then_inc(kqT_ready.sem, 1)

                def hidden(i, a, made, read):
                    act.wait_ge(made.sem, made.now(i, a + 1))
                    nc.scalar.activation(aT[:, 2 * a:2 * a + 2, :].rearrange("p c n -> p (c n)"), psum[:, 2 + a, :],
                                         ACT.Gelu).then_inc(read.sem, 1)

                def turn(i, follows):
                    act.wait_ge(dh1_ready.sem, dh1_ready.before(i))
                    for t in range(TT):
                        act.wait_ge(pre_made.sem, pre_made.now(i, t + 1))
                        act.wait_ge(g1_made.sem, g1_made.before(i))
                        nc.scalar.activation(a1[:, t, :], px[:, t, :], ACT.Gelu).then_inc(a1_ready.sem, 1)
                        nc.scalar.activation(pre[:, t, :], px[:, t, :], ACT.Copy).then_inc(pre_copied.sem, 1)
                        nc.scalar.activation(pdf[:, t, :], px[:, t, :], ACT.Square).then_inc(pre_squared.sem, 1)
                        nc.scalar.activation(gg[:, t, :], px[:, t, :], ACT.Copy, scale=-0.5).then_inc(pre_read.sem, 1)
                        act.wait_ge(h2T_made.sem, h2T_made.before(i))
                        hidden(i, t, khid_made, khid_read)
                    act.wait_ge(h1T_made.sem, h1T_made.now(i))
                    act.wait_ge(h2_turned.sem, h2_turned.before(i))
                    nc.scalar.activation(hT[:, :], pg[:, GH:GH + S], ACT.Copy).then_inc(h1T_copied.sem, 1)
                    act.wait_ge(h1_turned.sem, h1_turned.now(i))
                    nc.scalar.activation(h1[:, :, :].rearrange("p t d -> p (t d)"), pt[:, 0:S], ACT.Copy).then_inc(h1_copied.sem, 1)
                    nc.scalar.activation(h1sq[:, :, :].rearrange("p t d -> p (t d)"), pt[:, 0:S], ACT.Square).then_inc(h1_ready.sem, 1)
                    act.wait_ge(pre_squared.sem, pre_squared.now(i))
                    for t in range(TT):
                        nc.scalar.activation(pdf[:, t, :], pdf[:, t, :], ACT.Exp, scale=-0.5, bias=cst[:, C_LNPHI:C_LNPHI + 1]
                                             ).then_inc(pdf_ready.sem, 1)
                    act.wait_ge(dh_turned.sem, dh_turned.now(i))
                    act.wait_ge(back_made.sem, back_made.before(i))
                    nc.scalar.activation(dhT[:, :], pt[:, 0:S], ACT.Copy).then_inc(dhT_ready.sem, 1)
                    act.wait_ge(gates_turned.sem, gates_turned.now(i))
                    act.wait_ge(gates_spread.sem, gates_spread.before(i))
                    nc.scalar.activation(maskT[0:2 * E1, :], pt[0:2 * E1, 0:S], ACT.Copy).then_inc(gatesT_ready.sem, 1)
                    if follows:
                        tokens_copy(i + 1)
                    act.wait_ge(gm_ready.sem, gm_ready.now(i))
                    act.wait_ge(gtotal_made.sem, gtotal_made.before(i))
                    nc.scalar.activation(gsq[:, :], gm[:, :], ACT.Square, accum_out=gsum[:, :]).then_inc(gsum_ready.sem, 1)
                    if follows:
                        gate_inputs(i + 1)
                    act.wait_ge(ffn_made.sem, ffn_made.now(i))
                    act.wait_ge(gT1_ready.sem, gT1_ready.before(i))
                    nc.scalar.activation(thf[:, :], pf[:, 0:S], ACT.Tanh, scale=0.5).then_inc(thf_ready.sem, 1)
                    if follows:
                        up(i + 1)
                    act.wait_ge(nw_turned.sem, nw_turned.now(i))
                    act.wait_ge(h2T_made.sem, h2T_made.before(i))
                    nc.scalar.activation(nw1[:, :], pt[:, 0:P], ACT.Copy).then_inc(nw1_ready.sem, 1)
                    act.wait_ge(h1T_made.sem, h1T_made.now(i))
                    hidden(i, 0, qhid_made, qhid_read)
                    hidden(i, 1, qhid_made, qhid_read)
                    act.wait_ge(h2T_made.sem, h2T_made.now(i))
                    nc.scalar.activation(hT[:, :], pg[:, GH:GH + S], ACT.Copy).then_inc(h2T_copied.sem, 1)
                    act.wait_ge(h2_turned.sem, h2_turned.now(i))
                    act.wait_ge(y_ready.sem, y_ready.before(i))
                    nc.scalar.activation(h2[:, :, :].rearrange("p t d -> p (t d)"), pt[:, 0:S], ACT.Copy).then_inc(h2_ready.sem, 1)
                    if follows:
                        kqT_copy(i + 1)

                tokens_copy(0)
                gate_inputs(0)
                up(0)
                kqT_copy(0)
                with act.Fori(0, B - 1) as i:
                    turn(i, True)
                turn(B - 1, False)

            @block.vector
            def _(dve):
                for sg in (xn1_ready, gl_ready, pro_read, kq_ready, gates_ready, gated, dh_ready, dh1_ready, gm_ready,
                           nw_ready, gT1_ready, y_ready, inv_ready):
                    dve.sem_inc(sg.sem, sg.per)

                def heads(ap):
                    return ap.rearrange("p t (h d) -> p (t h) d", d=HD)

                def per_head(ap):
                    return ap.unsqueeze(2).to_broadcast([P, ap.shape[1], HD])

                def normalise(n, ch):
                    dve.wait_ge(xn1_turned.sem, xn1_turned.before(n))
                    for t in range(TT):
                        ins = dve.tensor_scalar(xn[:, t, :], x_all[:, bass.ds(n, 1), t, :].rearrange("p a d -> p (a d)"),
                                                mean[:, bass.ds(n * TT + t, 1)], nrm[:, 0, bass.ds(n * TT + t, 1)],
                                                ALU.subtract, ALU.mult)
                        if t == TT - 1:
                            ins.then_inc(xn1_ready.sem, 1)
                        else:
                            ins.then_inc(ch.sem, ch.one())

                def projections(n, ch):
                    dve.wait_ge(pro_ready.sem, pro_ready.now(n))
                    for t in range(TT):
                        dve.scalar_tensor_tensor(out=gl[:, t, :], in0=px[:, t, 3 * D:3 * D + 3 * H],
                                                 scalar=nrm[:, 1, bass.ds(n * TT + t, 1)], in1=gate_b[:, :],
                                                 op0=ALU.mult, op1=ALU.add).then_inc(gl_ready.sem, 1)
                    rl = px[:, :, 3 * D + 3 * H:NPRO]
                    dve.tensor_reduce(top[:, :], rl, AX_X, ALU.max).then_inc(ch.sem, ch.one())
                    dve.wait_ge(ch.sem, ch.value())
                    dve.wait_ge(rex_ready.sem, rex_ready.before(n))
                    dve.tensor_tensor(rld[:, :, :], rl, top[:, :].unsqueeze(2).to_broadcast([P, TT, E1]), ALU.subtract
                                      ).then_inc(pro_read.sem, 1)

                def keys_queries(n, ch):
                    dve.wait_ge(sq_ready.sem, sq_ready.now(n))
                    dve.tensor_reduce(ms[:, :], sq[:, :, :].rearrange("p t (h d) -> p (t h) d", d=HD), AX_X, ALU.add).then_inc(ch.sem, ch.one())
                    dve.wait_ge(ch.sem, ch.value())
                    dve.tensor_scalar(ms[:, :], ms[:, :], 1.0 / HD, RMS_EPS, ALU.mult, ALU.add).then_inc(ch.sem, ch.one())
                    dve.wait_ge(ch.sem, ch.value())
                    newton(dve, ch, rinv[:, :], ms[:, :], scratch[:, :], 2 * TT * H)
                    dve.wait_ge(g0_made.sem, g0_made.before(n))
                    dve.wait_ge(q_kept.sem, q_kept.before(n))
                    dve.tensor_tensor(kq[:, :, :].rearrange("p t (a h d) -> p t (a h) d", h=H, d=HD),
                                      pro[:, :, 0:2 * D].rearrange("p t (a h d) -> p t (a h) d", h=H, d=HD),
                                      rinv[:, :].rearrange("p (t h) -> p t h", t=TT).unsqueeze(3).to_broadcast([P, TT, 2 * H, HD]),
                                      ALU.mult).then_inc(ch.sem, ch.one())
                    dve.wait_ge(ch.sem, ch.value())
                    dve.tensor_tensor(kq[:, :, :], kq[:, :, :],
                                      knq_bc[:, :, :, :].rearrange("p a h d -> p (a h d)").unsqueeze(1).to_broadcast([P, TT, 2 * D]),
                                      ALU.mult).then_inc(kq_ready.sem, 1)
                    dve.wait_ge(th1_ready.sem, th1_ready.now(n))
                    dve.tensor_scalar(th2[:, :, :], th1[:, :, 2 * H:3 * H], MAX_LR, MAX_LR, ALU.mult, ALU.add).then_inc(ch.sem, ch.one())
                    dve.wait_ge(ch.sem, ch.value())


                def turn(i, follows):
                    ch = Steps(dve_turn1, DVE_TURN1, i)

                    def unit(x_sq):
                        dve.tensor_reduce(ms[:, 0:TT * H], heads(x_sq), AX_X, ALU.add).then_inc(ch.sem, ch.one())
                        dve.wait_ge(ch.sem, ch.value())
                        dve.tensor_scalar(ms[:, 0:TT * H], ms[:, 0:TT * H], 1.0 / HD, PF_EPS, ALU.mult, ALU.add).then_inc(ch.sem, ch.one())
                        dve.wait_ge(ch.sem, ch.value())
                        newton(dve, ch, rinv[:, 0:TT * H], ms[:, 0:TT * H], scratch[:, 0:TT * H], TT * H)
                        return per_head(rinv[:, 0:TT * H])

                    for t in range(TT):
                        dve.wait_ge(pre_copied.sem, pre_copied.now(i, t + 1))
                        dve.scalar_tensor_tensor(out=inv[:, t, :], in0=pre[:, t, :], scalar=0.0, in1=pre[:, t, :],
                                                 op0=ALU.is_equal, op1=ALU.add).then_inc(ch.sem, ch.one())
                        dve.wait_ge(ch.sem, ch.value())
                        dve.reciprocal(inv[:, t, :], inv[:, t, :]).then_inc(inv_ready.sem, 1)
                    dve.wait_ge(h1_ready.sem, h1_ready.now(i))
                    dve.wait_ge(kmv_ready.sem, kmv_ready.now(i))
                    r = unit(h1sq[:, :, :])
                    dve.tensor_tensor(heads(hn[:, :, :]), heads(h1[:, :, :]), r, ALU.mult).then_inc(ch.sem, ch.one())
                    dve.wait_ge(ch.sem, ch.value())
                    dve.tensor_tensor(dp[:, :, :], hn[:, :, :], kmv[:, :, :], ALU.add).then_inc(ch.sem, ch.one())
                    dve.wait_ge(ch.sem, ch.value())
                    dve.tensor_tensor(heads(dp[:, :, :]), heads(dp[:, :, :]),
                                      per_head(th2[:, :, :].rearrange("p t h -> p (t h)")), ALU.mult).then_inc(ch.sem, ch.one())
                    dve.wait_ge(ch.sem, ch.value())
                    dve.tensor_tensor(tmp[:, :, :], dp[:, :, :], hn[:, :, :], ALU.mult).then_inc(ch.sem, ch.one())
                    dve.wait_ge(ch.sem, ch.value())
                    dve.tensor_reduce(dy[:, :], heads(tmp[:, :, :]), AX_X, ALU.add).then_inc(ch.sem, ch.one())
                    dve.wait_ge(ch.sem, ch.value())
                    dve.tensor_tensor(heads(tmp[:, :, :]), heads(hn[:, :, :]), per_head(dy[:, :]), ALU.mult).then_inc(ch.sem, ch.one())
                    dve.wait_ge(ch.sem, ch.value())
                    dve.scalar_tensor_tensor(out=dp[:, :, :], in0=tmp[:, :, :], scalar=-1.0 / HD, in1=dp[:, :, :],
                                             op0=ALU.mult, op1=ALU.add).then_inc(ch.sem, ch.one())
                    dve.wait_ge(ch.sem, ch.value())
                    dve.wait_ge(g1_made.sem, g1_made.before(i))
                    dve.tensor_tensor(heads(dh[:, :, :]), heads(dp[:, :, :]), r, ALU.mult).then_inc(dh_ready.sem, 1)
                    if follows:
                        normalise(i + 1, ch)
                    dve.wait_ge(rex_ready.sem, rex_ready.now(i))
                    dve.tensor_reduce(rsm[:, :], rex[:, :, :], AX_X, ALU.add).then_inc(ch.sem, ch.one())
                    dve.wait_ge(ch.sem, ch.value())
                    dve.reciprocal(rsm[:, :], rsm[:, :]).then_inc(ch.sem, ch.one())
                    dve.wait_ge(ch.sem, ch.value())
                    probs1 = work1[:, :, 0:E1]
                    dve.tensor_tensor(probs1, rex[:, :, :], rsm[:, :].unsqueeze(2).to_broadcast([P, TT, E1]), ALU.mult).then_inc(ch.sem, ch.one())
                    choose(dve, ch, E1, TOP1, work1, find1, rest1, TAKEN1)
                    dve.scalar_tensor_tensor(out=prob[:, :, :], in0=rest1[:, :, 0:E1], scalar=TAKEN1, in1=probs1,
                                             op0=ALU.is_equal, op1=ALU.mult).then_inc(ch.sem, ch.one())
                    dve.wait_ge(ch.sem, ch.value())
                    dve.wait_ge(gates_turned.sem, gates_turned.before(i))
                    dve.tensor_copy(mask[:, :, 0:E1].bitcast(F32R), prob[:, :, :]).then_inc(ch.sem, ch.one())
                    dve.wait_ge(ch.sem, ch.value())
                    dve.tensor_tensor(mask[:, :, E1:2 * E1], prob[:, :, :], mask[:, :, 0:E1], ALU.subtract).then_inc(gates_ready.sem, 1)
                    dve.wait_ge(g0_made.sem, g0_made.before(i))
                    dve.wait_ge(slope_ready.sem, slope_ready.now(i))
                    for t in range(TT):
                        dve.wait_ge(back_made.sem, back_made.now(i, t + 1))
                        dve.scalar_tensor_tensor(out=dh1[:, t, :], in0=gg[:, t, :], scalar=0.5, in1=px[:, t, :],
                                                 op0=ALU.add, op1=ALU.mult).then_inc(dh1_ready.sem, 1)

                    def gate(c):
                        dve.wait_ge(gates_spread.sem, gates_spread.now(i, c + 1))
                        a = actT[:, 1 + 2 * c:3 + 2 * c, :].rearrange("p c n -> p (c n)")
                        dve.tensor_tensor(a, psum[:, 2 + c % 2, :], a, ALU.mult).then_inc(gated.sem, 1)

                    dve.wait_ge(up_read.sem, up_read.now(i))
                    gate(0)
                    gate(1)
                    dve.wait_ge(g0_made.sem, g0_made.now(i))
                    dve.wait_ge(g1_made.sem, g1_made.now(i))
                    dve.wait_ge(gsum_ready.sem, gsum_ready.before(i))
                    dve.tensor_copy(sums[:, :], pg[:, GS:GS + 2]).then_inc(ch.sem, ch.one())
                    dve.tensor_tensor(gm[:, :], pg[:, 0:NW], cst[:, C_BD0:C_BD0 + NW], ALU.mult).then_inc(gm_ready.sem, 1)
                    gate(2)
                    gate(3)
                    if follows:
                        projections(i + 1, ch)
                    dve.wait_ge(gtotal_made.sem, gtotal_made.now(i))
                    total, root, factor, keep_w, momentum, t1 = (cf[:, k:k + 1] for k in range(6))
                    dve.tensor_copy(total, pg[:, GQ:GQ + 1]).then_inc(ch.sem, ch.one())
                    dve.wait_ge(ch.sem, ch.value())
                    newton(dve, ch, root, total, t1, 1)
                    dve.tensor_tensor(root, root, total, ALU.mult).then_inc(ch.sem, ch.one())
                    dve.wait_ge(ch.sem, ch.value())
                    dve.tensor_scalar(root, root, 1e-6, None, ALU.add).then_inc(ch.sem, ch.one())
                    dve.wait_ge(ch.sem, ch.value())
                    dve.reciprocal(root, root).then_inc(ch.sem, ch.one())
                    dve.wait_ge(ch.sem, ch.value())
                    dve.tensor_scalar(factor, root, CLIP, 1.0, ALU.mult, ALU.min).then_inc(ch.sem, ch.one())
                    dve.wait_ge(ch.sem, ch.value())
                    dve.tensor_scalar(factor, factor, -1.0, None, ALU.mult).then_inc(ch.sem, ch.one())
                    dve.tensor_scalar(keep_w, sums[:, 0:1], -0.5 / S, 0.5, ALU.mult, ALU.add).then_inc(ch.sem, ch.one())
                    dve.tensor_scalar(momentum, sums[:, 1:2], 0.5 / S, 0.5, ALU.mult, ALU.add).then_inc(ch.sem, ch.one())
                    dve.wait_ge(ch.sem, ch.value())
                    dve.tensor_scalar(momentum, momentum, 0.0, None, ALU.mult).then_inc(ch.sem, ch.one())
                    dve.wait_ge(ch.sem, ch.value())
                    dve.tensor_scalar(gm[:, :], gm[:, :], factor, momentum, ALU.mult, ALU.add).then_inc(ch.sem, ch.one())
                    dve.wait_ge(ch.sem, ch.value())
                    dve.scalar_tensor_tensor(out=nw[:, :], in0=w_bd[:, :], scalar=keep_w, in1=gm[:, :],
                                             op0=ALU.mult, op1=ALU.add).then_inc(ch.sem, ch.one())
                    dve.wait_ge(ch.sem, ch.value())
                    dve.tensor_scalar(nwok[:, :], nw[:, :], 0.0, 0.0, ALU.mult, ALU.is_equal).then_inc(ch.sem, ch.one())
                    dve.wait_ge(ch.sem, ch.value())
                    dve.wait_ge(nwf_set.sem, nwf_set.now(i))
                    dve.sem_inc(dve_waits_met, 1)
                    dve.copy_predicated(nwf[:, :], nwok[:, :], nw[:, :]).then_inc(nw_ready.sem, 1)
                    dve.wait_ge(thf_ready.sem, thf_ready.now(i))
                    dve.wait_ge(gf_turned.sem, gf_turned.before(i))
                    dve.scalar_tensor_tensor(out=gT1[:, :], in0=thf[:, :], scalar=1.0, in1=pf[:, 0:S],
                                             op0=ALU.add, op1=ALU.mult).then_inc(gT1_ready.sem, 1)
                    if follows:
                        keys_queries(i + 1, ch)
                    dve.wait_ge(q_kept.sem, q_kept.now(i))
                    dve.wait_ge(h2_ready.sem, h2_ready.now(i))
                    dve.tensor_scalar(h2ok[:, :, :], h2[:, :, :], 0.0, 0.0, ALU.mult, ALU.is_equal).then_inc(ch.sem, ch.one())
                    dve.wait_ge(ch.sem, ch.value())
                    dve.wait_ge(hz_set.sem, hz_set.now(i))
                    dve.sem_inc(dve_waits_met, 1)
                    dve.copy_predicated(hz[:, :, :], h2ok[:, :, :], h2[:, :, :]).then_inc(ch.sem, ch.one())
                    dve.wait_ge(ch.sem, ch.value())
                    dve.tensor_tensor(y2[:, :, :], hz[:, :, :], hz[:, :, :], ALU.mult).then_inc(ch.sem, ch.one())
                    dve.wait_ge(ch.sem, ch.value())
                    r = unit(y2[:, :, :])
                    dve.tensor_tensor(heads(y2[:, :, :]), heads(hz[:, :, :]), r, ALU.mult).then_inc(ch.sem, ch.one())
                    dve.wait_ge(ch.sem, ch.value())
                    dve.tensor_tensor(y2[:, :, :], y2[:, :, :], qkeep[:, :, :], ALU.add).then_inc(ch.sem, ch.one())
                    dve.wait_ge(ch.sem, ch.value())
                    dve.wait_ge(gf_turned.sem, gf_turned.now(i))
                    dve.scalar_tensor_tensor(out=y2[:, :, :], in0=y2[:, :, :], scalar=0.5,
                                             in1=pf[:, S:2 * S].rearrange("p (t d) -> p t d", t=TT), op0=ALU.mult, op1=ALU.mult).then_inc(ch.sem, ch.one())
                    dve.wait_ge(ch.sem, ch.value())
                    xs = x_all[:, bass.ds(i, 1), :, :].rearrange("p a t d -> p (a t) d")
                    dve.tensor_tensor(xs, xs, y2[:, :, :], ALU.add).then_inc(y_ready.sem, 1)
                    if follows:
                        ch.end()

                first = Steps(dve_front1)
                normalise(0, first)
                projections(0, first)
                keys_queries(0, first)
                with dve.Fori(0, B - 1) as i:
                    turn(i, True)
                turn(B - 1, False)


_INS = ['L0_attn_x', 'L0_attn_Wq', 'L0_attn_Wk', 'L0_attn_Wv', 'L0_attn_Wu', 'L0_attn_bu', 'L0_ffn_router_w',
        'L0_ffn_router_b', 'L0_ffn_expert_w', 'L0_ffn_expert_b', 'L1_attn_W_K', 'L1_attn_W_V', 'L1_attn_W_Q',
        'L1_attn_mem_W0', 'L1_attn_mem_W1', 'L1_attn_k_norm_w', 'L1_attn_q_norm_w', 'L1_attn_store_norm_w',
        'L1_attn_retrieve_norm_w', 'L1_attn_alpha_w', 'L1_attn_alpha_b', 'L1_attn_theta_w', 'L1_attn_theta_b',
        'L1_attn_eta_w', 'L1_attn_eta_b', 'L1_ffn_shared_up', 'L1_ffn_shared_down', 'L1_ffn_routed_up',
        'L1_ffn_routed_down', 'L1_ffn_router_w']


def shape_constants():
    import numpy as np

    c = np.zeros((P, N_C), np.float32)
    p = np.arange(P)
    c[:, C_ID:C_ID + P] = np.eye(P)
    c[:, C_SELQ] = -1.0 * ((p % 32) // HD == 2)
    c[:, C_SELK] = -1.0 * ((p % 32) // HD == 1)
    c[:, C_ONEK] = p % 32 == 3 * HD
    c[:, C_HEAD:C_HEAD + P] = p[:, None] // HD == p[None] // HD
    c[:, C_BD0:C_BD0 + H * HID] = p[:, None] // HD == np.arange(H * HID)[None] // HID
    c[:, C_BD1T:C_BD1T + P] = p[:, None] // HD % NG == p[None] // HID
    c[:, C_BD1:C_BD1 + NG * HD] = p[:, None] // HID == np.arange(NG * HD)[None] // HD
    c[:, C_FILL0:C_FILL1] = FILL0 * (1.0 + 0.01 * np.arange(8 - TOP0))
    c[:, C_FILL1:C_REP8] = -1.0 - np.arange(8 - TOP1)
    c[:HD, C_REP8:C_REP8 + P] = np.arange(HD)[:, None] == p[None] % HD
    c[:HID, C_REP32:C_REP32 + P] = np.arange(HID)[:, None] == p[None] % HID
    c[:E0, C_SEL0:C_SEL0 + E0 * P] = np.arange(E0)[:, None] == np.arange(E0 * P)[None] // P
    r = np.arange(2 * E1)[:, None] % E1
    c[:2 * E1, C_SEL1:C_SEL1 + 8 * P] = r == np.arange(8 * P)[None] // FE
    c[:, C_ONE] = 1.0
    c[:, C_LNPHI] = np.log(0.3989422804014327)
    return c


def kernel(**inputs):
    import numpy as _np
    import concourse.bacc as _bacc
    from concourse import mybir as _mybir
    from concourse.bass_utils import run_bass_kernel_spmd as _run

    nc = _bacc.Bacc("TRN2", target_bir_lowering=False, num_devices=1)
    arrays = {"consts": shape_constants()}
    args = [nc.dram_tensor("consts", (P, N_C), F32, kind="ExternalInput").ap()]
    for name in _INS:
        a = _np.ascontiguousarray(inputs[name])
        arrays[f"in_{name}"] = a
        args.append(nc.dram_tensor(f"in_{name}", a.shape, _mybir.dt.from_np(a.dtype), kind="ExternalInput").ap())
    args.append(nc.dram_tensor("out", (B, S, D), F32, kind="ExternalOutput").ap())
    build(nc, *args)
    r = _run(nc, [arrays], core_ids=[0])
    return r.results[0]["out"]
```
